# Optimizing a Trainium2 kernel written in Bass

```python
import numpy as np
import jax
import jax.numpy as jnp

def _softmax(x, axis=-1):
    return jax.nn.softmax(x, axis=axis)

def _gelu(x):
    return jax.nn.gelu(x, approximate=True)

def _silu(x):
    return jax.nn.silu(x)

def _sigmoid(x):
    return jax.nn.sigmoid(x)

def _layernorm(x, axis=-1, eps=1e-05):
    m = jnp.mean(x, axis=axis, keepdims=True)
    v = jnp.var(x, axis=axis, keepdims=True)
    return (x - m) / jnp.sqrt(v + eps)

def _scatter_add(tgt, idx, src, axis=0):
    return tgt.at[idx].add(src)

def _segment_sum(src, seg, n):
    return jax.ops.segment_sum(src, seg, n)
kernel_name = 'mk_hybrid_d1_jaxref_r4_cc963f'

def setup_inputs(seed: int=0):
    np.random.seed(seed)
    _w = jnp.asarray

    def _L0_attn_a_setup():
        import jax, jax.numpy as jnp
        import numpy as np
        import math
        _OFFSETS = list(range(41)) + [128, 96, 384]
        key = jax.random.key(seed)
        B, T, C, H = (1, 512, 256, 16)
        HD = C // H
        J = len(_OFFSETS)
        k0, k1, k2, k3 = jax.random.split(key, 4)
        x = jax.random.normal(k0, (B, T, C), jnp.float32)
        w_qkv = jax.random.normal(k1, (C, 3 * C), jnp.float32) / math.sqrt(C)
        w_out = jax.random.normal(k2, (C, C), jnp.float32) / math.sqrt(C)
        delta_vals = jnp.log1p(jnp.asarray(_OFFSETS, jnp.float32))
        alphas = jnp.concatenate([jnp.linspace(0.2, 2.0, H - 1) * 1.5, jnp.array([1.0], jnp.float32)])
        pos_bias = -delta_vals[:, None] * alphas[None, :]
        scale_embed = 0.05 * jax.random.normal(k3, (J, HD), jnp.float32)
        if_gain = jnp.ones((H,), jnp.float32)
        return {'x': x, 'w_qkv': w_qkv, 'w_out': w_out, 'pos_bias': pos_bias, 'scale_embed': scale_embed, 'if_gain': if_gain}
    _L0_attn_a_in = _L0_attn_a_setup()

    def _L0_attn_b_setup():
        import jax, jax.numpy as jnp
        import numpy as np
        D_MODEL = 256
        N_HEADS = 16
        D_HEAD = D_MODEL // N_HEADS
        key = jax.random.key(seed)
        ks = jax.random.split(key, 9)
        s = 1.0 / np.sqrt(D_MODEL)
        x = jax.random.normal(ks[0], (2, 512, D_MODEL), dtype=jnp.float32)
        Wq = jax.random.uniform(ks[1], (D_MODEL, D_MODEL), jnp.float32, -s, s)
        bq = jax.random.uniform(ks[2], (D_MODEL,), jnp.float32, -s, s)
        Wk = jax.random.uniform(ks[3], (D_MODEL, D_MODEL), jnp.float32, -s, s)
        bk = jax.random.uniform(ks[4], (D_MODEL,), jnp.float32, -s, s)
        Wv = jax.random.uniform(ks[5], (D_MODEL, D_MODEL), jnp.float32, -s, s)
        bv = jax.random.uniform(ks[6], (D_MODEL,), jnp.float32, -s, s)
        Wo = jax.random.uniform(ks[7], (D_MODEL, D_MODEL), jnp.float32, -s, s)
        bo = jax.random.uniform(ks[8], (D_MODEL,), jnp.float32, -s, s)
        return {'x': x, 'Wq': Wq, 'bq': bq, 'Wk': Wk, 'bk': bk, 'Wv': Wv, 'bv': bv, 'Wo': Wo, 'bo': bo}
    _L0_attn_b_in = _L0_attn_b_setup()

    def _L0_ffn_setup():
        import jax, jax.numpy as jnp
        import numpy as np
        B, S, D, H, M, E, K = (4, 512, 256, 512, 64, 8, 2)

        def _layernorm(x, g, b, eps=1e-05):
            mu = x.mean(-1, keepdims=True)
            var = ((x - mu) ** 2).mean(-1, keepdims=True)
            return (x - mu) * jax.lax.rsqrt(var + eps) * g + b

        def _forward(inputs_embeds, enc_W, enc_b, s2c_W, s2c_b, rW1, rb1, rW2, rb2, We1, be1, We2, be2, c2s_W, c2s_b, dec_W, dec_b, ln_g, ln_b):
            b, s, _ = inputs_embeds.shape
            spikes_enc = jax.nn.sigmoid(inputs_embeds @ enc_W + enc_b)
            flat = spikes_enc.reshape(b * s, H)
            cont = flat @ s2c_W + s2c_b
            logits = jnp.tanh(cont @ rW1 + rb1) @ rW2 + rb2
            probs = jax.nn.softmax(logits, axis=-1)
            topw, topi = jax.lax.top_k(probs, K)
            w = topw / topw.sum(-1, keepdims=True)
            gates = (jax.nn.one_hot(topi, E, dtype=cont.dtype) * w[..., None]).sum(1)
            h = jax.nn.relu(jnp.einsum('nm,emh->enh', cont, We1) + be1[:, None, :])
            expert_out = jnp.einsum('enh,ehm->enm', h, We2) + be2[:, None, :]
            output_flat = jnp.einsum('enm,ne->nm', expert_out, gates)
            spikes_moe = jax.nn.sigmoid(output_flat @ c2s_W + c2s_b).reshape(b, s, H)
            decoded = jax.nn.sigmoid(spikes_moe @ dec_W + dec_b)
            return _layernorm(decoded, ln_g, ln_b)
        key = jax.random.key(seed)
        ks = jax.random.split(key, 10)
        r = lambda k, shape: jax.random.normal(k, shape, dtype=jnp.float32) * 0.02
        return {'inputs_embeds': jax.random.normal(ks[0], (B, S, D), dtype=jnp.float32), 'enc_W': r(ks[1], (D, H)), 'enc_b': jnp.zeros((H,), jnp.float32), 's2c_W': r(ks[2], (H, M)), 's2c_b': jnp.zeros((M,), jnp.float32), 'rW1': r(ks[3], (M, 64)), 'rb1': jnp.zeros((64,), jnp.float32), 'rW2': r(ks[4], (64, E)), 'rb2': jnp.zeros((E,), jnp.float32), 'We1': r(ks[5], (E, M, H // 2)), 'be1': jnp.zeros((E, H // 2), jnp.float32), 'We2': r(ks[6], (E, H // 2, M)), 'be2': jnp.zeros((E, M), jnp.float32), 'c2s_W': r(ks[7], (M, H)), 'c2s_b': jnp.zeros((H,), jnp.float32), 'dec_W': r(ks[8], (H, D)), 'dec_b': jnp.zeros((D,), jnp.float32), 'ln_g': jnp.ones((D,), jnp.float32), 'ln_b': jnp.zeros((D,), jnp.float32)}
    _L0_ffn_in = _L0_ffn_setup()
    _d = {'L0_attn_a_x': _L0_attn_a_in['x'], 'L0_attn_a_w_qkv': _L0_attn_a_in['w_qkv'], 'L0_attn_a_w_out': _L0_attn_a_in['w_out'], 'L0_attn_a_pos_bias': _L0_attn_a_in['pos_bias'], 'L0_attn_a_scale_embed': _L0_attn_a_in['scale_embed'], 'L0_attn_a_if_gain': _L0_attn_a_in['if_gain'], 'L0_attn_b_Wq': _L0_attn_b_in['Wq'], 'L0_attn_b_bq': _L0_attn_b_in['bq'], 'L0_attn_b_Wk': _L0_attn_b_in['Wk'], 'L0_attn_b_bk': _L0_attn_b_in['bk'], 'L0_attn_b_Wv': _L0_attn_b_in['Wv'], 'L0_attn_b_bv': _L0_attn_b_in['bv'], 'L0_attn_b_Wo': _L0_attn_b_in['Wo'], 'L0_attn_b_bo': _L0_attn_b_in['bo'], 'L0_ffn_enc_W': _L0_ffn_in['enc_W'], 'L0_ffn_enc_b': _L0_ffn_in['enc_b'], 'L0_ffn_s2c_W': _L0_ffn_in['s2c_W'], 'L0_ffn_s2c_b': _L0_ffn_in['s2c_b'], 'L0_ffn_rW1': _L0_ffn_in['rW1'], 'L0_ffn_rb1': _L0_ffn_in['rb1'], 'L0_ffn_rW2': _L0_ffn_in['rW2'], 'L0_ffn_rb2': _L0_ffn_in['rb2'], 'L0_ffn_We1': _L0_ffn_in['We1'], 'L0_ffn_be1': _L0_ffn_in['be1'], 'L0_ffn_We2': _L0_ffn_in['We2'], 'L0_ffn_be2': _L0_ffn_in['be2'], 'L0_ffn_c2s_W': _L0_ffn_in['c2s_W'], 'L0_ffn_c2s_b': _L0_ffn_in['c2s_b'], 'L0_ffn_dec_W': _L0_ffn_in['dec_W'], 'L0_ffn_dec_b': _L0_ffn_in['dec_b'], 'L0_ffn_ln_g': _L0_ffn_in['ln_g'], 'L0_ffn_ln_b': _L0_ffn_in['ln_b']}
    _x0 = _d['L0_attn_a_x']
    _d['L0_attn_a_x'] = jax.random.normal(jax.random.fold_in(jax.random.key(seed), 1), (8, 512, 256), dtype=_x0.dtype)
    del _x0
    return _d

def reference(L0_attn_a_x, L0_attn_a_w_qkv, L0_attn_a_w_out, L0_attn_a_pos_bias, L0_attn_a_scale_embed, L0_attn_a_if_gain, L0_attn_b_Wq, L0_attn_b_bq, L0_attn_b_Wk, L0_attn_b_bk, L0_attn_b_Wv, L0_attn_b_bv, L0_attn_b_Wo, L0_attn_b_bo, L0_ffn_enc_W, L0_ffn_enc_b, L0_ffn_s2c_W, L0_ffn_s2c_b, L0_ffn_rW1, L0_ffn_rb1, L0_ffn_rW2, L0_ffn_rb2, L0_ffn_We1, L0_ffn_be1, L0_ffn_We2, L0_ffn_be2, L0_ffn_c2s_W, L0_ffn_c2s_b, L0_ffn_dec_W, L0_ffn_dec_b, L0_ffn_ln_g, L0_ffn_ln_b):

    def _L0_attn_a_ref(x, w_qkv, w_out, pos_bias, scale_embed, if_gain):
        import jax, jax.numpy as jnp
        import numpy as np
        import math
        _OFFSETS = list(range(41)) + [128, 96, 384]
        B, T, C = x.shape
        H = if_gain.shape[0]
        HD = C // H
        deltas = jnp.asarray(_OFFSETS)
        qkv = x @ w_qkv
        q, k, v = jnp.split(qkv, 3, axis=-1)
        q = q.reshape(B, T, H, HD).transpose(0, 2, 1, 3)
        k = k.reshape(B, T, H, HD).transpose(0, 2, 1, 3)
        v = v.reshape(B, T, H, HD).transpose(0, 2, 1, 3)
        idx = jnp.arange(T)[:, None] - deltas[None, :]
        valid = idx >= 0
        idxc = jnp.maximum(idx, 0)
        k_g = k[:, :, idxc]
        v_g = v[:, :, idxc]
        k_mod = k_g * (1.0 + scale_embed)
        scale = 1.0 / math.sqrt(HD)
        scores = jnp.einsum('bhtd,bhtjd->bhtj', q, k_mod) * scale
        scores = scores + pos_bias.T[None, :, None, :]
        scores = jnp.where(valid[None, None], scores, jnp.finfo(scores.dtype).min)
        attn = jax.nn.softmax(scores, axis=-1)
        out = jnp.einsum('bhtj,bhtjd->bhtd', attn, v_g)
        out = out * if_gain[None, :, None, None]
        out = out.transpose(0, 2, 1, 3).reshape(B, T, C)
        return out @ w_out

    def _L0_attn_b_ref(x, Wq, bq, Wk, bk, Wv, bv, Wo, bo):
        import jax, jax.numpy as jnp
        import numpy as np
        D_MODEL = 256
        N_HEADS = 16
        D_HEAD = D_MODEL // N_HEADS
        B, T, _ = x.shape

        def split_heads(y):
            return y.reshape(B, T, N_HEADS, D_HEAD).transpose(0, 2, 1, 3)
        Q = split_heads(x @ Wq + bq)
        K = split_heads(x @ Wk + bk)
        V = split_heads(x @ Wv + bv)
        scores = jnp.einsum('bhqd,bhkd->bhqk', Q, K) / jnp.sqrt(jnp.float32(D_HEAD))
        causal = jnp.tril(jnp.ones((T, T), dtype=bool))
        scores = jnp.where(causal, scores, -jnp.inf)
        attn = jax.nn.softmax(scores, axis=-1)
        out = jnp.einsum('bhqk,bhkd->bhqd', attn, V)
        out = out.transpose(0, 2, 1, 3).reshape(B, T, D_MODEL)
        return out @ Wo + bo

    def _L0_ffn_ref(inputs_embeds, enc_W, enc_b, s2c_W, s2c_b, rW1, rb1, rW2, rb2, We1, be1, We2, be2, c2s_W, c2s_b, dec_W, dec_b, ln_g, ln_b):
        import jax, jax.numpy as jnp
        import numpy as np
        B, S, D, H, M, E, K = (4, 512, 256, 512, 64, 8, 2)

        def _layernorm(x, g, b, eps=1e-05):
            mu = x.mean(-1, keepdims=True)
            var = ((x - mu) ** 2).mean(-1, keepdims=True)
            return (x - mu) * jax.lax.rsqrt(var + eps) * g + b

        def _forward(inputs_embeds, enc_W, enc_b, s2c_W, s2c_b, rW1, rb1, rW2, rb2, We1, be1, We2, be2, c2s_W, c2s_b, dec_W, dec_b, ln_g, ln_b):
            b, s, _ = inputs_embeds.shape
            spikes_enc = jax.nn.sigmoid(inputs_embeds @ enc_W + enc_b)
            flat = spikes_enc.reshape(b * s, H)
            cont = flat @ s2c_W + s2c_b
            logits = jnp.tanh(cont @ rW1 + rb1) @ rW2 + rb2
            probs = jax.nn.softmax(logits, axis=-1)
            topw, topi = jax.lax.top_k(probs, K)
            w = topw / topw.sum(-1, keepdims=True)
            gates = (jax.nn.one_hot(topi, E, dtype=cont.dtype) * w[..., None]).sum(1)
            h = jax.nn.relu(jnp.einsum('nm,emh->enh', cont, We1) + be1[:, None, :])
            expert_out = jnp.einsum('enh,ehm->enm', h, We2) + be2[:, None, :]
            output_flat = jnp.einsum('enm,ne->nm', expert_out, gates)
            spikes_moe = jax.nn.sigmoid(output_flat @ c2s_W + c2s_b).reshape(b, s, H)
            decoded = jax.nn.sigmoid(spikes_moe @ dec_W + dec_b)
            return _layernorm(decoded, ln_g, ln_b)
        return _forward(inputs_embeds, enc_W, enc_b, s2c_W, s2c_b, rW1, rb1, rW2, rb2, We1, be1, We2, be2, c2s_W, c2s_b, dec_W, dec_b, ln_g, ln_b)
    x = L0_attn_a_x
    x = x + _L0_attn_a_ref(_layernorm(x, axis=-1), L0_attn_a_w_qkv, L0_attn_a_w_out, L0_attn_a_pos_bias, L0_attn_a_scale_embed, L0_attn_a_if_gain)
    x = x + _L0_ffn_ref(_layernorm(x, axis=-1), L0_ffn_enc_W, L0_ffn_enc_b, L0_ffn_s2c_W, L0_ffn_s2c_b, L0_ffn_rW1, L0_ffn_rb1, L0_ffn_rW2, L0_ffn_rb2, L0_ffn_We1, L0_ffn_be1, L0_ffn_We2, L0_ffn_be2, L0_ffn_c2s_W, L0_ffn_c2s_b, L0_ffn_dec_W, L0_ffn_dec_b, L0_ffn_ln_g, L0_ffn_ln_b)
    x = x + _L0_attn_b_ref(_layernorm(x, axis=-1), L0_attn_b_Wq, L0_attn_b_bq, L0_attn_b_Wk, L0_attn_b_bk, L0_attn_b_Wv, L0_attn_b_bv, L0_attn_b_Wo, L0_attn_b_bo)
    x = x + _L0_ffn_ref(_layernorm(x, axis=-1), L0_ffn_enc_W, L0_ffn_enc_b, L0_ffn_s2c_W, L0_ffn_s2c_b, L0_ffn_rW1, L0_ffn_rb1, L0_ffn_rW2, L0_ffn_rb2, L0_ffn_We1, L0_ffn_be1, L0_ffn_We2, L0_ffn_be2, L0_ffn_c2s_W, L0_ffn_c2s_b, L0_ffn_dec_W, L0_ffn_dec_b, L0_ffn_ln_g, L0_ffn_ln_b)
    return x

_drawn_inputs = setup_inputs


def setup_inputs(seed=0):
    import zlib

    import numpy as np

    out = dict(_drawn_inputs(seed))
    spreads = {'L0_attn_a_if_gain': (1.0, 0.2),
     'L0_ffn_enc_b': (0.0, 0.8),
     'L0_ffn_s2c_b': (0.0, 0.8),
     'L0_ffn_rb1': (0.0, 0.8),
     'L0_ffn_rb2': (0.0, 0.8),
     'L0_ffn_be1': (0.0, 0.8),
     'L0_ffn_be2': (0.0, 0.8),
     'L0_ffn_c2s_b': (0.0, 0.1),
     'L0_ffn_dec_b': (0.0, 0.1),
     'L0_ffn_ln_g': (1.0, 0.2),
     'L0_ffn_ln_b': (0.0, 0.1)}
    factors = {'L0_attn_a_scale_embed': 7.15,
     'L0_attn_b_Wq': 8.0,
     'L0_attn_b_bq': 8.0,
     'L0_attn_b_Wk': 8.0,
     'L0_attn_b_bk': 8.0,
     'L0_attn_b_bv': 6.324,
     'L0_attn_b_bo': 3.853,
     'L0_ffn_enc_W': 8.0,
     'L0_ffn_s2c_W': 8.0,
     'L0_ffn_rW1': 8.0,
     'L0_ffn_rW2': 8.0,
     'L0_ffn_We1': 8.0,
     'L0_ffn_We2': 8.0,
     'L0_ffn_c2s_W': 8.0}
    for name, (base, spread) in spreads.items():
        noise = np.random.default_rng([zlib.crc32(name.encode()), seed]).standard_normal(out[name].shape)
        drawn = base * np.exp(spread * noise) if base else spread * noise
        out[name] = jnp.asarray(drawn.astype(out[name].dtype))
    for name, factor in factors.items():
        out[name] = (out[name] * factor).astype(out[name].dtype)
    return out
```

```python
import concourse.bass as bass
from concourse import mybir
from concourse.alu_op_type import AluOpType as ALU
from contextlib import ExitStack
import numpy as np

P = 128
NB, T, D = 8, 512, 256
TT = T // P
KD = D // P
H, HD = 16, 16
HS = 32
HPT = P // HD
NEAR = 41
SLOTS = [NEAR - 1 - s for s in range(NEAR)] + [96, 128, 384]
REF_OF = [NEAR - 1 - s for s in range(NEAR)] + [42, 41, 43]
J = len(SLOTS)
GROUP_J = [16, 16, 12]
NG = len(GROUP_J)
PAD = 384
BW = P + NEAR - 1
FF, M, E, EH = 512, 64, 8, 256
KF = FF // P
NEG = -1.0e30
EPS = 1e-5

PACK = [
    ("ident", P), ("slot_mask", 4 * HS), ("offset_mask", 2 * NG * T), ("pos_bias", 2 * NG), ("se", J),
    ("w_qkv", KD * 3 * D), ("w_out_a", KD * D), ("gain", KD),
    ("wq", KD * D), ("wk", KD * D), ("wv", KD * D), ("wo", KD * D), ("bq", KD), ("bk", KD), ("bv", D), ("bo", D),
    ("enc_w", KD * FF), ("enc_b", KF), ("s2c_w", KF * M), ("s2c_b", 1), ("rw1", M), ("rw2", E),
    ("we1", E * EH), ("we2", E * 2 * M), ("be2", E // 2), ("c2s_w", FF), ("c2s_b", KF),
    ("dec_w", KF * D), ("dec_b", D), ("ln_g", D), ("ln_b", D),
    ("pair_sel", (E // 2) * P), ("before", E * E), ("causal", P),
]
AT, _n = {}, 0
for _name, _w in PACK:
    AT[_name] = (_n, _n + _w)
    _n += _w
PACK_W = _n

UNITS = [(q, h) for q in range(TT) for h in range(H)]
ROT = 6


def causal_steps():
    steps = []
    for u in range(len(UNITS) + 3):
        if u < len(UNITS):
            steps.append(("S", u))
        if 2 <= u < len(UNITS) + 2:
            steps.append(("T", u - 2))
        v = u - 3
        if v >= 0 and v % 4 == 3:
            steps.append(("V", v // 4))
            if v % H == H - 1:
                steps.append(("O", v // H))
    return steps


def plan():
    order = []

    def xnT():
        order.extend([("xnT", 0), ("xnT", 1)])

    def output(i):
        order.extend([("on", i), ("oNT", i), ("pr", i)])

    def ffn():
        xnT()
        order.extend([("enc", m) for m in range(KF)] + ["cont", "rh", "lg"])
        for p in range(E // 2):
            order.extend([("hid", 4 * p + n) for n in range(4)])
            if p == 0:
                order.append("gT")
            order.extend([("gb", p), ("eo", p)])
        order.extend([("c2s", m) for m in range(KF)] + [("dec", n) for n in range(TT // 2)])

    xnT()
    order.extend([("qk", m) for m in range(4)] + [("v", n) for n in range(2)])
    order.extend([("sT", g) for g in range(2 * NG)])
    order.extend([("tS", 0, 0), ("tS", 0, 1), ("tS", 1, 0), ("tS", 1, 1)])
    for i in range(TT):
        if i + 2 < TT:
            order.extend([("tS", i + 2, 0), ("tS", i + 2, 1)])
        order.extend([("pA", i, q) for q in range(4)] + [("pB", i, q) for q in range(2) if i > 0])
        order.append(("oT", i))
        output(i)
    ffn()
    xnT()
    order.extend([("qk", m) for m in range(4)] + [("v", n) for n in range(2)])
    for kind, u in causal_steps():
        if kind in "ST":
            order.append((kind, u))
        elif kind == "V" and u % 4 == 0:
            order.append(("oT", u // 4))
        elif kind == "O":
            output(u)
    ffn()
    turn, uses, fills, held = 0, [0] * 8, {}, 0
    for name in order:
        if name[0] == "oT":
            bank = 6 + held % 2
            held += 1
        else:
            bank = turn % ROT
            turn += 1
        fills.setdefault(name, []).append((bank, uses[bank]))
        uses[bank] += 1
    return fills, uses


FILLS, USES = plan()

PRODUCTS = [(hf, g, col, r) for hf in range(2) for g in range(NG) for r in range(4) for col in range(GROUP_J[g] // 4)]
FIRST = [hf * J + 16 * g for hf in range(2) for g in range(NG)]
LAST = [n - 1 for n in FIRST[1:]] + [2 * J - 1]
BY_POOL = [n for n in range(2 * J) if n % 3 == 1]
BY_DVE = [n for n in range(2 * J) if n % 3 != 1]
READ_AT = [min(n + 6, 2 * J - 1) for n in LAST]


def slot(n):
    _, g, col, r = PRODUCTS[n]
    return 16 * g + 4 * col + r


DVE_SETUP = 26
DVE_STEPS = 69

PARITY = ("_even", "_odd")

SIGNALS = {
    "x_loaded": (16, 1), "x_free": (1, 1), "ln_var": (1, 6), "ln_rstd": (1, 6), "xn_ready": (TT, 4),
    "vs_shifted": (64, 1), "prod_dve": (len(BY_DVE), 1), "prod_pool": (len(BY_POOL), 1),
    "prod_used": (2 * J - len(LAST), 1), "pa_ready": (TT, 1),
    "band_written_even": (16 * TT // 2, 1), "band_written_odd": (16 * TT // 2, 1),
    "band_read_even": (16 * TT // 2, 1), "band_read_odd": (16 * TT // 2, 1), "far_ready": (TT, 1),
    "oN_ready": (TT, 1), "hi_ready": (4, 1), "r1_ready": (4, 1), "mid_ready": (4, 1), "lo_ready": (4, 1),
    "split_written": (16 * 12, 1), "stack_read": (16 * 24, 1), "max_ready": (TT * H, 1), "pv_done": (12, 1),
    "lgd_ready": (1, 2), "gexp_ready": (1, 2), "gates_ready": (1, 2), "dect_ready": (TT, 2),
    "moe_ready": (1, 2), "y_ready": (1, 1), "y_stored": (16, 1), "dve_step": (DVE_STEPS, 1), "pool_step": (8, 1),
}


def build(nc, x_dram, pack_dram, out_dram):
    fp32, bf16 = mybir.dt.float32, mybir.dt.bfloat16
    ACT = mybir.ActivationFunctionType
    AX = mybir.AxisListType.X

    band_dram = nc.dram_tensor("band", (TT, P * (BW + 1) * H), fp32, kind="Internal").ap()
    split_dram = nc.dram_tensor("splits", (4, 3, P, T), bf16, kind="Internal").ap()

    ctx = ExitStack()
    with ctx:
        def sb(name, shape, dt=fp32):
            return ctx.enter_context(nc.sbuf_tensor(name, shape, dt))

        pack = sb("consts", [P, PACK_W])
        x_in = sb("x_in", [P, TT, D])
        x_res = sb("x_res", [P, TT, D])
        xn = sb("xn", [P, TT, D])
        xnT = sb("xnT", [P, KD, T])
        v_96 = sb("v_96", [P, TT, H, HS])
        kT = sb("kT", [P, KD, PAD + T])
        cont = sb("cont", [P, T])
        rh = sb("rh", [P, T])
        gT = sb("gT", [P, T])
        V = sb("V", [P, TT, H, HS])
        slot_w = sb("slot_w", [P, J, HS])
        stats = sb("stats", [P, TT, 6])
        mv = sb("mv", [P, TT, 2])
        var_eps = sb("var_eps", [P, TT])
        rstd = sb("rstd", [P, TT])
        minus_half = sb("minus_half", [P, TT])
        ones = sb("ones", [P, P])
        scrap = sb("scrap", [P, 16])
        half_c2s_b = sb("half_c2s_b", [P, KF])
        half_enc_b = sb("half_enc_b", [P, KF])
        q_bias = sb("q_bias", [P, KD])
        s2c_bias = sb("s2c_bias", [P, 1])
        causal = sb("causal_b", [P, P], bf16)
        ident_b = sb("ident_b", [P, P], bf16)
        oTs = xn[:].rearrange("p (r a) c -> p r (a c)", r=2)
        oN = sb("oN", [P, 2, D])
        oNT = sb("oNT", [P, 2, KD, P])
        den = sb("den", [P, 2, H])
        ARENA = 21600
        arena = sb("arena", [P, ARENA])
        taken = [0]

        def part(n, restart=False):
            if restart:
                taken[0] = 0
            a = taken[0]
            taken[0] += n
            assert taken[0] <= ARENA, taken[0]
            return arena[:, a:a + n]

        qT = part(KD * T, True).rearrange("p (m t) -> p m t", m=KD)
        RD, RP = 6, 3
        prod_d = part(RD * T).rearrange("p (r t) -> p r t", r=RD)
        prod_p = part(RP * T).rearrange("p (r t) -> p r t", r=RP)
        sT = part(2 * NG * T).rearrange("p (g t) -> p g t", g=2 * NG)
        p_nat = part(2 * J * H).rearrange("p (r j h) -> p r j h", r=2, j=J)
        band = part(2 * BW * H).rearrange("p (r s h) -> p r s h", r=2, s=BW)
        ptA = part(H * P).rearrange("p (h t) -> p h t", h=H)
        ptB = part(H * (NEAR - 1)).rearrange("p (h t) -> p h t", h=H)
        v_near = part(TT * H * HS).rearrange("p (i h d) -> p i h d", i=TT, h=H)
        far = part(2 * D).rearrange("p (r h d) -> p r h d", r=2, h=H)
        far_t = part(D).rearrange("p (h d) -> p h d", h=H)
        mx = part(TT * H).rearrange("p (i h) -> p i h", i=TT)
        far_den = part(2 * H).rearrange("p (r h) -> p r h", r=2)
        q32 = part(4 * T, True).rearrange("p (m t) -> p m t", m=4)
        r1 = part(4 * T).rearrange("p (m t) -> p m t", m=4)
        split = part(4 * 3 * T // 2).bitcast(bf16).rearrange("p (m s t) -> p m s t", m=4, s=3)
        q_st = part(H * T // 2).bitcast(bf16).rearrange("p (h t) -> p h t", h=H)
        k_st = part(H * T // 2).bitcast(bf16).rearrange("p (h t) -> p h t", h=H)
        RU, RT = 4, 8
        p_exp = part(RU * T).rearrange("p (r t) -> p r t", r=RU)
        p_T = part(RT * T).rearrange("p (r t) -> p r t", r=RT)
        nmx = part(RU)
        t_enc = part(KF * T, True).rearrange("p (m t) -> p m t", m=KF)
        RH = 8
        hid = part(RH * T).rearrange("p (r t) -> p r t", r=RH)
        gb = part(2 * T).rearrange("p (r t) -> p r t", r=2)
        moe = part(T)
        moe_t = part(T)
        t_moe = part(KF * T).rearrange("p (m t) -> p m t", m=KF)
        dd = part(TT * D).rearrange("p (i c) -> p i c", i=TT)
        lg = part(TT * E).rearrange("p (i e) -> p i e", i=TT)
        lgd = part(TT * E).rearrange("p (i e) -> p i e", i=TT)
        above = part(TT * E * E).rearrange("p (i e f) -> p i e f", i=TT, e=E)
        same = part(TT * E * E).rearrange("p (i e f) -> p i e f", i=TT, e=E)
        rank = part(TT * E).rearrange("p (i e) -> p i e", i=TT)
        gates = part(TT * E).rearrange("p (i e) -> p i e", i=TT)
        lmax = part(TT)
        gsum = part(TT)

        def c(name, a=0, n=None):
            lo, hi = AT[name]
            return pack[:, lo + a:hi if n is None else lo + a + n]

        def c3(name, k):
            return c(name).rearrange("p (k n) -> p k n", k=k)

        ident = c("ident")
        w_qkv, w_out = c3("w_qkv", KD), c3("w_out_a", KD)
        wq, wk, wv, wo = (c3(n, KD) for n in ("wq", "wk", "wv", "wo"))
        enc_w, s2c_w, dec_w = c3("enc_w", KD), c3("s2c_w", KF), c3("dec_w", KF)
        we1, we2 = c3("we1", E), c("we2").rearrange("p (e k m) -> p e k m", e=E, k=2)
        pair_sel = c3("pair_sel", E // 2)
        offset_mask = c3("offset_mask", 2 * NG)

        bank = [ctx.enter_context(nc.psum_tensor(f"bank{i}", [P, T], fp32)) for i in range(8)]
        full = [ctx.enter_context(nc.semaphore(f"bank{i}_full")) for i in range(8)]
        free = [ctx.enter_context(nc.semaphore(f"bank{i}_read")) for i in range(8)]
        sem = {n: ctx.enter_context(nc.semaphore(n)) for n in SIGNALS}
        pack_loaded = ctx.enter_context(nc.semaphore("pack_loaded"))
        setup_dve = ctx.enter_context(nc.semaphore("setup_dve"))
        setup_pool = ctx.enter_context(nc.semaphore("setup_pool"))
        setup_pe = ctx.enter_context(nc.semaphore("setup_pe"))
        setup_band = ctx.enter_context(nc.semaphore("setup_band"))

        SETTLED = (setup_band, 2 * TT * 16)

        def nth(b, name, k, call=0):
            per, calls = SIGNALS[name]
            return sem[name], b * (per * calls) + (call * per + k)

        def place(name, call=0, of=free):
            n, _ = FILLS[name][call]
            return bank[n], of[n]

        def bank_full(b, name, call=0):
            n, before = FILLS[name][call]
            return full[n], b * USES[n] + (before + 1)

        def bank_read(b, name, call=0):
            n, before = FILLS[name][call]
            return free[n], b * USES[n] + (before + 2)

        def bank_free(b, name, call=0):
            n, before = FILLS[name][call]
            return free[n], b * USES[n] + (before + 1)

        def latest(names, call=0):
            last = {FILLS[name][call][0]: name for name in sorted(names, key=lambda x: FILLS[x][call][1])}
            return list(last.values())

        def covered(name, others, call=0):
            return [x for x in latest(others, call) if FILLS[x][call][0] != FILLS[name][call][0]]

        def product_used(b, n):
            if n in LAST:
                return bank_full(b, ("sT", LAST.index(n)))
            return nth(b, "prod_used", sum(k not in LAST for k in range(n + 1)))

        def quad_done(b, quad):
            if quad % 4 == 3:
                return bank_full(b, ("oT", quad // 4), 1)
            return nth(b, "pv_done", 3 * (quad // 4) + quad % 4 + 1)

        block = ctx.enter_context(nc.Block())

        @block.sync
        def _(sp):
            sp.dma_start(pack[:], pack_dram).then_inc(pack_loaded, 16)
            sp.wait_ge(setup_pool, 1)
            w = (BW + 1) * H // 2
            for i in range(TT):
                for n in range(2):
                    dst = band_dram[i, :].rearrange("(t r) -> t r", t=P)[:, n * w:(n + 1) * w]
                    sp.dma_start(dst, band[:, 0, :, :].rearrange("p s h -> p (s h)")[:, 0:w]).then_inc(setup_band, 16)
            sp.wait_ge(setup_band, 2 * TT * 16)
            with sp.Fori(0, NB) as b:
                sp.wait_ge(*SETTLED)
                sp.wait_ge(sem["x_free"], b + 1)
                sp.dma_start(x_in[:], x_dram[bass.ds(b, 1), :, :].rearrange("o (i p) n -> p (o i) n", p=P)
                             ).then_inc(sem["x_loaded"], 16)
                sp.wait_ge(*SETTLED)
                sp.wait_ge(*bank_read(b, ("v", 0)))
                sp.wait_ge(*SETTLED)
                sp.wait_ge(*bank_read(b, ("v", 1)))
                sp.dma_start(v_96[0:96, 1:TT], V[32:P, 0:TT - 1]).then_inc(sem["vs_shifted"], 16)
                sp.dma_start(v_96[96:P, :], V[0:32, :]).then_inc(sem["vs_shifted"], 16)
                sp.dma_start(v_near[0:NEAR - 1, 0:2], V[P - NEAR + 1:P, 0:2]).then_inc(sem["vs_shifted"], 16)
                sp.dma_start(v_near[0:NEAR - 1, 2:TT], V[P - NEAR + 1:P, 2:TT]).then_inc(sem["vs_shifted"], 16)
                for i in range(TT + 1):
                    if i < TT:
                        sp.wait_ge(*SETTLED)
                        sp.wait_ge(*nth(b, "pa_ready", i + 1))
                        dst = band_dram[i, :].rearrange("(t r) -> t r", t=P)[:, 0:NEAR * H]
                        sp.dma_start(dst, p_nat[:, i % 2, 0:NEAR, :].rearrange("p j h -> p (j h)")
                                     ).then_inc(sem["band_written" + PARITY[i % 2]], 16)
                    if i >= 1:
                        k = i - 1
                        sp.wait_ge(*SETTLED)
                        sp.wait_ge(*nth(b, "band_written" + PARITY[k % 2], 16 * (k // 2 + 1)))
                        if k >= 2:
                            sp.wait_ge(*SETTLED)
                            sp.wait_ge(*bank_full(b, ("pB", k - 2, 1) if k > 2 else ("pA", k - 2, 3)))
                        src = band_dram[k, 0:P * BW * H].rearrange("(t r) -> t r", t=P)
                        sp.dma_start(band[:, k % 2, :, :].rearrange("p s h -> p (s h)"), src
                                     ).then_inc(sem["band_read" + PARITY[k % 2]], 16)
                for m in range(4):
                    sp.wait_ge(*SETTLED)
                    sp.wait_ge(*nth(b, "mid_ready", m + 1))
                    sp.wait_ge(*SETTLED)
                    sp.wait_ge(*nth(b, "lo_ready", m + 1))
                    for s in range(3):
                        sp.dma_start(split_dram[m, s], split[:, m, s, :]).then_inc(sem["split_written"], 16)
                sp.wait_ge(*SETTLED)
                sp.wait_ge(*nth(b, "split_written", 16 * 12))
                for slot, (sq, sk) in enumerate([(0, 0), (0, 1), (1, 0), (1, 1), (0, 2), (2, 0)]):
                    for half, (st, s) in enumerate([(q_st, sq), (k_st, sk)]):
                        for m in range(2):
                            src = split_dram[2 * half + m, s].rearrange("(h d) t -> d h t", d=HD)
                            sp.dma_start(st[slot * HD:(slot + 1) * HD, m * HPT:(m + 1) * HPT, :], src
                                         ).then_inc(sem["stack_read"], 16)

        @block.gpsimd
        def _(pool):
            nc.gpsimd.memset(band[:], 0.0).then_inc(setup_pool, 1)
            nc.gpsimd.memset(V[:], 0.0).then_inc(setup_pool, 1)
            nc.gpsimd.memset(v_96[:, 0], 0.0).then_inc(setup_pool, 1)
            nc.gpsimd.memset(minus_half[:], -0.5).then_inc(setup_pool, 1)
            pool.wait_ge(setup_pool, 4)
            nc.gpsimd.memset(V[:, :, :, HD:HD + 1], 1.0).then_inc(setup_pool, 1)
            pool.wait_ge(setup_pool, 5)

            def power(b, call):
                pool.wait_ge(*nth(b, "ln_var", 1, call))
                nc.gpsimd.tensor_tensor(rstd[:], var_eps[:], minus_half[:], ALU.pow).then_inc(sem["ln_rstd"], 1)

            with pool.Fori(0, NB) as b:
                step = [0]

                def link(ins):
                    step[0] += 1
                    ins.then_inc(sem["pool_step"], 1)
                    pool.wait_ge(*nth(b, "pool_step", step[0]))

                power(b, 0)
                for x in latest([("qk", m) for m in range(4)]):
                    pool.wait_ge(*bank_read(b, x))
                pool.wait_ge(setup_dve, DVE_SETUP)
                for k, n in enumerate(BY_POOL):
                    hf, at = PRODUCTS[n][0], PAD - SLOTS[slot(n)]
                    if k >= RP:
                        pool.wait_ge(*product_used(b, BY_POOL[k - RP]))
                    nc.gpsimd.tensor_tensor(prod_p[:, k % RP, :], qT[:, hf, :], kT[:, hf, at:at + T],
                                            ALU.mult).then_inc(sem["prod_pool"], 1)
                pool.wait_ge(*nth(b, "vs_shifted", 64))
                for i in range(TT):
                    pool.wait_ge(*nth(b, "pa_ready", i + 1))
                    if i >= 2:
                        pool.wait_ge(*nth(b, "oN_ready", i - 1))
                    out = far[:, i % 2]

                    def p_of(s):
                        return p_nat[:, i % 2, s, :].unsqueeze(2).broadcast_to([P, H, HD])

                    terms = [(NEAR, v_96[:, i, :, 0:HD])]
                    if i >= 1:
                        terms.append((NEAR + 1, V[:, i - 1, :, 0:HD]))
                    if i >= 3:
                        terms.append((NEAR + 2, V[:, i - 3, :, 0:HD]))
                    for n, (s, v) in enumerate(terms):
                        last = nc.gpsimd.tensor_tensor(out if n == 0 else far_t, v, p_of(s), ALU.mult)
                        if n:
                            link(last)
                            last = nc.gpsimd.tensor_tensor(out, out, far_t, ALU.add)
                        if n < len(terms) - 1:
                            link(last)
                    last.then_inc(sem["far_ready"], 1)
                for call in range(1, 6):
                    power(b, call)
                assert step[0] == SIGNALS["pool_step"][0], step[0]

        @block.scalar
        def _(act):
            act.wait_ge(setup_dve, DVE_SETUP)

            def read_xnT(b, call):
                for k in range(KD):
                    act.wait_ge(*bank_full(b, ("xnT", k), call))
                    ps, read = place(("xnT", k), call)
                    nc.scalar.copy(xnT[:, k, :], ps[:]).then_inc(read, 1)

            def read_v(b, call):
                for n in range(2):
                    act.wait_ge(*bank_full(b, ("v", n), call))
                    ps, read = place(("v", n), call)
                    nc.scalar.copy(V[:, 2 * n:2 * n + 2, :, 0:HD],
                                   ps[:].rearrange("p (i h d) -> p i h d", i=2, h=H)).then_inc(read, 1)

            def read_oT(b, i, call):
                act.wait_ge(*bank_full(b, ("oT", i), call))
                ps, read = place(("oT", i), call)
                nc.scalar.copy(oTs[:, i % 2, :], ps[:]).then_inc(read, 1)

            def read_oNT(b, i, call):
                act.wait_ge(*bank_full(b, ("oNT", i), call))
                ps, read = place(("oNT", i), call)
                nc.scalar.copy(oNT[:, i % 2, :, :], ps[:, 0:KD * P].rearrange("p (k t) -> p k t", k=KD)
                               ).then_inc(read, 1)

            def p_local(b, i):
                act.wait_ge(*bank_read(b, ("tS", i, 0)))
                act.wait_ge(*bank_read(b, ("tS", i, 1)))
                nc.scalar.activation(p_nat[:, i % 2], p_nat[:, i % 2], ACT.Exp).then_inc(sem["pa_ready"], 1)

            def local_attention(b):
                read_xnT(b, 0)
                for m in range(4):
                    act.wait_ge(*bank_full(b, ("qk", m)))
                    ps, read = place(("qk", m))
                    dst = qT[:, m, :] if m < KD else kT[:, m - KD, PAD:PAD + T]
                    nc.scalar.copy(dst, ps[:]).then_inc(read, 1)
                read_v(b, 0)
                p_local(b, 0)
                p_local(b, 1)
                for i in range(TT):
                    for q in range(4):
                        act.wait_ge(*bank_full(b, ("pA", i, q)))
                        ps, read = place(("pA", i, q))
                        nc.scalar.copy(ptA[:, 4 * q:4 * q + 4, :], ps[:].rearrange("p (h t) -> p h t", h=4)
                                       ).then_inc(read, 1)
                    if i + 2 < TT:
                        p_local(b, i + 2)
                    read_oT(b, i, 0)
                    read_oNT(b, i, 0)

            def causal_attention(b):
                read_xnT(b, 2)
                for m in range(4):
                    act.wait_ge(*bank_full(b, ("qk", m), 1))
                    ps, read = place(("qk", m), 1)
                    if m < KD:
                        nc.scalar.activation(q32[:, m, :], ps[:], ACT.Identity, bias=q_bias[:, m:m + 1],
                                             scale=0.25).then_inc(read, 1)
                    else:
                        nc.scalar.activation(q32[:, m, :], ps[:], ACT.Identity, bias=c("bk", m - KD, 1)
                                             ).then_inc(read, 1)
                for m in range(4):
                    act.wait_ge(*bank_read(b, ("qk", m), 1))
                    nc.scalar.copy(split[:, m, 0, :], q32[:, m, :]).then_inc(sem["hi_ready"], 1)
                for m in range(4):
                    act.wait_ge(*nth(b, "r1_ready", m + 1))
                    nc.scalar.copy(split[:, m, 1, :], r1[:, m, :]).then_inc(sem["mid_ready"], 1)
                for kind, u in causal_steps():
                    if kind == "S":
                        q, w = u // H, (u // H + 1) * P
                        act.wait_ge(*nth(b, "max_ready", u + 1))
                        for x in covered(("S", u), [("T", u - RU)]) if u >= RU else ():
                            act.wait_ge(*bank_full(b, x))
                        act.wait_ge(*bank_full(b, ("S", u)))
                        ps, read = place(("S", u))
                        nc.scalar.activation(p_exp[:, u % RU, 0:w], ps[:, 0:w], ACT.Exp,
                                             bias=nmx[:, u % RU:u % RU + 1]).then_inc(read, 1)
                    elif kind == "T" and u % 3 == 0:
                        w = (u // H + 1) * P
                        act.wait_ge(*bank_full(b, ("T", u)))
                        ps, read = place(("T", u))
                        if u >= RT:
                            act.wait_ge(*quad_done(b, (u - RT) // 4))
                        nc.scalar.copy(p_T[:, u % RT, 0:w], ps[:, 0:w]).then_inc(read, 1)
                    elif kind == "O":
                        read_oT(b, u, 1)
                        read_oNT(b, u, 1)

            def experts(b, f):
                read_xnT(b, 1 + 2 * f)
                for m in range(KF):
                    act.wait_ge(*bank_full(b, ("enc", m), f))
                    ps, read = place(("enc", m), f)
                    nc.scalar.activation(t_enc[:, m, :], ps[:], ACT.Tanh, bias=half_enc_b[:, m:m + 1], scale=0.5
                                         ).then_inc(read, 1)
                act.wait_ge(*bank_full(b, "cont", f))
                ps, read = place("cont", f)
                nc.scalar.activation(cont[0:M, :], ps[0:M, :], ACT.Identity, bias=s2c_bias[0:M, :]).then_inc(read, 1)
                act.wait_ge(*bank_full(b, "rh", f))
                ps, read = place("rh", f)
                nc.scalar.activation(rh[0:M, :], ps[0:M, :], ACT.Tanh).then_inc(read, 1)
                for p in range(E // 2):
                    for n in range(4 * p, 4 * p + 4):
                        for x in covered(("hid", n), [("eo", (n - RH) // 4)], f) if n >= RH else ():
                            act.wait_ge(*bank_full(b, x, f))
                        act.wait_ge(*bank_full(b, ("hid", n), f))
                        ps, read = place(("hid", n), f)
                        nc.scalar.activation(hid[:, n % RH, :], ps[:], ACT.Relu).then_inc(read, 1)
                        if n == 1:
                            act.wait_ge(*nth(b, "lgd_ready", 1, f))
                            nc.scalar.activation(lgd[:], lgd[:], ACT.Exp).then_inc(sem["gexp_ready"], 1)
                    if p == 0:
                        act.wait_ge(*bank_full(b, "gT", f))
                        ps, read = place("gT", f)
                        nc.scalar.copy(gT[0:E, :], ps[0:E, :]).then_inc(read, 1)
                    act.wait_ge(*bank_full(b, ("gb", p), f))
                    ps, read = place(("gb", p), f)
                    if p >= 2:
                        act.wait_ge(*bank_read(b, ("eo", p - 2), f))
                    nc.scalar.copy(gb[:, p % 2, :], ps[:]).then_inc(read, 1)
                for m in range(KF):
                    act.wait_ge(*bank_full(b, ("c2s", m), f))
                    ps, read = place(("c2s", m), f)
                    nc.scalar.activation(t_moe[:, m, :], ps[:], ACT.Tanh, bias=half_c2s_b[:, m:m + 1], scale=0.5
                                         ).then_inc(read, 1)
                for n in range(TT // 2):
                    act.wait_ge(*bank_read(b, ("dec", n), f))
                    for i in (2 * n, 2 * n + 1):
                        nc.scalar.activation(dd[:, i, :], dd[:, i, :], ACT.Tanh, scale=0.5
                                             ).then_inc(sem["dect_ready"], 1)

            with act.Fori(0, NB) as b:
                local_attention(b)
                experts(b, 0)
                causal_attention(b)
                experts(b, 1)
                act.wait_ge(*nth(b, "y_ready", 1))
                act.dma_start(out_dram[bass.ds(b, 1), :, :].rearrange("o (i p) n -> p (o i) n", p=P), x_res[:]
                              ).then_inc(sem["y_stored"], 16)
            act.wait_ge(sem["y_stored"], 16 * NB + 16)

        @block.vector
        def _(dve):
            setup = [0]

            def once(ins):
                setup[0] += 1
                ins.then_inc(setup_dve, 1)
                dve.wait_ge(setup_dve, setup[0])

            for n, s in enumerate(free + [sem["x_free"]]):
                nc.vector.memset(scrap[:, n:n + 1], 0.0).then_inc(s, 1)
            nc.vector.memset(scrap[:, 9:10], 0.0).then_inc(sem["y_stored"], 16)
            once(nc.vector.memset(ones[:], 1.0))
            once(nc.vector.memset(kT[:, :, 0:PAD], 0.0))
            for t in (cont, rh, gT):
                once(nc.vector.memset(t[:], 0.0))
            once(nc.vector.memset(cont[M:M + 1, :], 1.0))
            once(nc.vector.memset(rh[M:M + 1, :], 1.0))
            dve.wait_ge(pack_loaded, 16)
            once(nc.vector.tensor_scalar(c("se"), c("se"), 1.0, HD ** -0.5, ALU.add, ALU.mult))
            once(nc.vector.tensor_tensor(
                slot_w[:].rearrange("p (a r) d -> p a r d", r=4),
                c3("slot_mask", 4).unsqueeze(1).broadcast_to([P, J // 4, 4, HS]),
                c("se").rearrange("p (a r) -> p a r", r=4).unsqueeze(3).broadcast_to([P, J // 4, 4, HS]), ALU.mult))
            for g in range(2 * NG):
                once(nc.vector.tensor_scalar(offset_mask[:, g, :], offset_mask[:, g, :], c("pos_bias", g, 1), None,
                                             ALU.add))
            for k in range(KD):
                once(nc.vector.tensor_scalar(w_out[:, k, :], w_out[:, k, :], c("gain", k, 1), None, ALU.mult))
            once(nc.vector.tensor_scalar(half_enc_b[:], c("enc_b"), 0.5, None, ALU.mult))
            once(nc.vector.tensor_scalar(half_c2s_b[:], c("c2s_b"), 0.5, None, ALU.mult))
            once(nc.vector.tensor_scalar(q_bias[:], c("bq"), HD ** -0.5, None, ALU.mult))
            once(nc.vector.tensor_copy(causal[:], c("causal")))
            once(nc.vector.tensor_copy(ident_b[:], ident))
            once(nc.vector.tensor_scalar(c("s2c_w"), c("s2c_w"), 0.5, None, ALU.mult))
            once(nc.vector.tensor_scalar(c("dec_w"), c("dec_w"), 0.5, None, ALU.mult))
            dve.wait_ge(setup_pe, 2)
            once(nc.vector.tensor_tensor(c("dec_b"), bank[0][:, 0:D], c("dec_b"), ALU.add))
            once(nc.vector.tensor_tensor(s2c_bias[0:M, :], bank[1][0:M, 0:1], c("s2c_b")[0:M, :], ALU.add))
            assert setup[0] == DVE_SETUP, setup[0]

            with dve.Fori(0, NB) as b:
                step = [0]

                def link(ins):
                    step[0] += 1
                    ins.then_inc(sem["dve_step"], 1)
                    dve.wait_ge(*nth(b, "dve_step", step[0]))

                def moments(src, call, eps, first=None):
                    for i in range(TT):
                        ins = nc.vector.bn_stats(stats[:, i, :], src[:, i, :])
                        if i == 0 and first:
                            ins.then_inc(sem[first], 1)
                        elif i == TT - 1:
                            link(ins)
                    if first:
                        dve.wait_ge(sem[first], b + 2)
                    nc.vector.memset(scrap[:, 15:16], 0.0)
                    for i in range(TT):
                        ins = nc.vector.bn_aggr(mv[:, i, :], stats[:, i, :])
                    link(ins)
                    nc.vector.tensor_scalar(var_eps[:], mv[:, :, 1], eps, None, ALU.add).then_inc(sem["ln_var"], 1)
                    dve.wait_ge(*nth(b, "ln_rstd", 1, call))

                def layer_norm(src, call, first=None):
                    moments(src, call, EPS, first)
                    for i in range(TT):
                        nc.vector.tensor_scalar(xn[:, i, :], src[:, i, :], mv[:, i, 0:1], rstd[:, i:i + 1],
                                                ALU.subtract, ALU.mult).then_inc(sem["xn_ready"], 1)

                def softmax_local(i):
                    if i >= 2:
                        dve.wait_ge(*nth(b, "band_written" + PARITY[i % 2], 16 * (i // 2)))
                        dve.wait_ge(*nth(b, "far_ready", i - 1))
                    halves = []
                    for hf in range(2):
                        dve.wait_ge(*bank_full(b, ("tS", i, hf)))
                        ps, read = place(("tS", i, hf))
                        s = ps[:, 0:J * HPT].rearrange("p (j h) -> p j h", j=J)
                        halves.append((s, read))
                        m = mx[:, i, hf * HPT:(hf + 1) * HPT]
                        link(nc.vector.tensor_reduce(m, s.rearrange("p j h -> p h j"), AX, ALU.max))
                    for hf, (s, read) in enumerate(halves):
                        m = mx[:, i, hf * HPT:(hf + 1) * HPT]
                        nc.vector.tensor_tensor(p_nat[:, i % 2, :, hf * HPT:(hf + 1) * HPT], s,
                                                m.unsqueeze(1).broadcast_to([P, J, HPT]), ALU.subtract
                                                ).then_inc(read, 1)

                def output_local(i):
                    dve.wait_ge(*bank_full(b, ("on", i)))
                    ps, read = place(("on", i))
                    o = ps[:].rearrange("p (h d) -> p h d", h=H)
                    link(nc.vector.tensor_tensor(den[:, 0, :], o[:, :, HD], far_den[:, i % 2], ALU.add))
                    link(nc.vector.reciprocal(den[:, 0, :], den[:, 0, :]))
                    dve.wait_ge(*nth(b, "far_ready", i + 1))
                    on = oN[:, i % 2, :].rearrange("p (h d) -> p h d", h=H)
                    nc.vector.tensor_tensor(on, o[:, :, 0:HD], far[:, i % 2], ALU.add).then_inc(read, 1)
                    dve.wait_ge(*bank_read(b, ("on", i)))
                    nc.vector.tensor_tensor(on, on, den[:, 0, :].unsqueeze(2).broadcast_to([P, H, HD]), ALU.mult
                                            ).then_inc(sem["oN_ready"], 1)
                    dve.wait_ge(*bank_full(b, ("pr", i)))
                    ps, read = place(("pr", i))
                    nc.vector.tensor_tensor(x_res[:, i, :], ps[:, 0:D], x_in[:, i, :], ALU.add).then_inc(read, 1)

                def output_causal(i):
                    dve.wait_ge(*bank_full(b, ("on", i), 1))
                    ps, read = place(("on", i), 1)
                    o = ps[:].rearrange("p (h d) -> p h d", h=H)
                    link(nc.vector.reciprocal(den[:, 0, :], o[:, :, HD]))
                    on = oN[:, i % 2, :].rearrange("p (h d) -> p h d", h=H)
                    nc.vector.tensor_tensor(on, o[:, :, 0:HD], den[:, 0, :].unsqueeze(2).broadcast_to([P, H, HD]),
                                            ALU.mult).then_inc(read, 1)
                    dve.wait_ge(*bank_full(b, ("pr", i), 1))
                    ps, read = place(("pr", i), 1)
                    nc.vector.tensor_tensor(x_res[:, i, :], ps[:, 0:D], x_res[:, i, :], ALU.add).then_inc(read, 1)
                    dve.wait_ge(*bank_read(b, ("pr", i), 1))
                    link(nc.vector.tensor_tensor(x_res[:, i, :], x_res[:, i, :], c("bo"), ALU.add))

                def local_attention():
                    dve.wait_ge(*nth(b, "x_loaded", 16))
                    layer_norm(x_in, 0)
                    for x in latest([("qk", m) for m in range(4)]):
                        dve.wait_ge(*bank_read(b, x))
                    k = 0
                    for n in range(2 * J):
                        if n in BY_DVE:
                            hf, at = PRODUCTS[n][0], PAD - SLOTS[slot(n)]
                            if k >= RD:
                                dve.wait_ge(*product_used(b, BY_DVE[k - RD]))
                            nc.vector.tensor_tensor(prod_d[:, k % RD, :], qT[:, hf, :], kT[:, hf, at:at + T],
                                                    ALU.mult).then_inc(sem["prod_dve"], 1)
                            k += 1
                        for g in range(2 * NG):
                            if n == READ_AT[g]:
                                read_scores(g)
                    dve.wait_ge(sem["y_stored"], b * 16 + 16)
                    softmax_local(0)
                    softmax_local(1)
                    for i in range(TT):
                        dve.wait_ge(*nth(b, "pa_ready", i + 1))
                        link(nc.vector.tensor_reduce(
                            far_den[:, i % 2], p_nat[:, i % 2, NEAR:J, :].rearrange("p j h -> p h j"), AX, ALU.add))
                        if i + 2 < TT:
                            softmax_local(i + 2)
                        if i > 0:
                            for q in range(2):
                                dve.wait_ge(*bank_full(b, ("pB", i, q)))
                                ps, read = place(("pB", i, q))
                                nc.vector.tensor_copy(ptB[0:NEAR - 1, 8 * q:8 * q + 8, :],
                                                      ps[0:NEAR - 1, 0:8 * (NEAR - 1)].rearrange(
                                                          "p (h t) -> p h t", h=8)).then_inc(read, 1)
                        output_local(i)

                def read_scores(g):
                    rows = GROUP_J[g % NG] * HPT
                    dve.wait_ge(*bank_full(b, ("sT", g)))
                    ps, read = place(("sT", g))
                    nc.vector.tensor_tensor(sT[0:rows, g, :], ps[0:rows, :], offset_mask[0:rows, g, :], ALU.add
                                            ).then_inc(read, 1)

                def causal_attention():
                    dve.wait_ge(*bank_read(b, ("pr", TT - 1)))
                    layer_norm(x_res, 3)
                    for n in range(2):
                        dve.wait_ge(*bank_full(b, ("v", n), 1))
                        ps, read = place(("v", n), 1)
                        for i in range(2):
                            ins = nc.vector.tensor_tensor(
                                V[:, 2 * n + i, :, 0:HD], ps[:, i * D:(i + 1) * D].rearrange("p (h d) -> p h d", h=H),
                                c("bv").rearrange("p (h d) -> p h d", h=H), ALU.add)
                        ins.then_inc(read, 1)
                    for m in range(4):
                        dve.wait_ge(*nth(b, "hi_ready", m + 1))
                        nc.vector.tensor_tensor(r1[:, m, :], q32[:, m, :], split[:, m, 0, :], ALU.subtract
                                                ).then_inc(sem["r1_ready"], 1)
                    for m in range(4):
                        dve.wait_ge(*nth(b, "mid_ready", m + 1))
                        nc.vector.tensor_tensor(split[:, m, 2, :], r1[:, m, :], split[:, m, 1, :], ALU.subtract
                                                ).then_inc(sem["lo_ready"], 1)
                    for kind, u in causal_steps():
                        if kind == "S":
                            w = (u // H + 1) * P
                            dve.wait_ge(*bank_full(b, ("S", u)))
                            ps, _ = place(("S", u))
                            if u >= RU:
                                dve.wait_ge(*bank_read(b, ("S", u - RU)))
                            nc.vector.tensor_reduce(nmx[:, u % RU:u % RU + 1], ps[:, 0:w], AX, ALU.max, negate=True
                                                    ).then_inc(sem["max_ready"], 1)
                        elif kind == "T" and u % 3:
                            w = (u // H + 1) * P
                            dve.wait_ge(*bank_full(b, ("T", u)))
                            ps, read = place(("T", u))
                            if u >= RT:
                                dve.wait_ge(*quad_done(b, (u - RT) // 4))
                            nc.vector.tensor_copy(p_T[:, u % RT, 0:w], ps[:, 0:w]).then_inc(read, 1)
                        elif kind == "O":
                            output_causal(u)

                def experts(f):
                    layer_norm(x_res, 1 + 3 * f, "x_free" if f == 0 else None)
                    dve.wait_ge(*bank_full(b, "lg", f))
                    ps, read = place("lg", f)
                    nc.vector.tensor_copy(lg[:], ps[:, 0:TT * E].rearrange("p (i e) -> p i e", i=TT)
                                          ).then_inc(read, 1)
                    dve.wait_ge(*bank_read(b, "lg", f))
                    link(nc.vector.tensor_reduce(lmax[:], lg[:], AX, ALU.max))
                    nc.vector.tensor_tensor(lgd[:], lg[:], lmax[:].unsqueeze(2).broadcast_to([P, TT, E]),
                                            ALU.subtract).then_inc(sem["lgd_ready"], 1)
                    other = lg[:].unsqueeze(2).broadcast_to([P, TT, E, E])
                    own = lg[:].unsqueeze(3).broadcast_to([P, TT, E, E])
                    before = c("before").rearrange("p (e f) -> p e f", e=E).unsqueeze(1).broadcast_to([P, TT, E, E])
                    nc.vector.tensor_tensor(above[:], other, own, ALU.is_gt)
                    link(nc.vector.tensor_tensor(same[:], other, own, ALU.is_equal))
                    link(nc.vector.tensor_tensor(same[:], same[:], before, ALU.mult))
                    link(nc.vector.tensor_tensor(above[:], above[:], same[:], ALU.add))
                    link(nc.vector.tensor_reduce(rank[:], above[:], AX, ALU.add))
                    link(nc.vector.tensor_scalar(rank[:], rank[:], 1.5, None, ALU.is_lt))
                    dve.wait_ge(*nth(b, "gexp_ready", 1, f))
                    link(nc.vector.tensor_tensor(gates[:], lgd[:], rank[:], ALU.mult))
                    link(nc.vector.tensor_reduce(gsum[:], gates[:], AX, ALU.add))
                    link(nc.vector.reciprocal(gsum[:], gsum[:]))
                    nc.vector.tensor_tensor(gates[:], gates[:], gsum[:].unsqueeze(2).broadcast_to([P, TT, E]),
                                            ALU.mult).then_inc(sem["gates_ready"], 1)
                    for p in range(E // 2):
                        dve.wait_ge(*bank_full(b, ("eo", p), f))
                        ps, read = place(("eo", p), f)
                        dve.wait_ge(*bank_read(b, ("gb", p), f))
                        nc.vector.scalar_tensor_tensor(
                            out=moe[:] if p == 0 else moe_t[:], in0=ps[:], scalar=c("be2", p, 1),
                            in1=gb[:, p % 2, :], op0=ALU.add, op1=ALU.mult).then_inc(read, 1)
                        if p > 0:
                            dve.wait_ge(*bank_read(b, ("eo", p), f))
                            ins = nc.vector.tensor_tensor(moe[:], moe[:], moe_t[:], ALU.add)
                            if p == E // 2 - 1:
                                ins.then_inc(sem["moe_ready"], 1)
                            else:
                                link(ins)
                    for n in range(TT // 2):
                        dve.wait_ge(*bank_full(b, ("dec", n), f))
                        ps, read = place(("dec", n), f)
                        nc.vector.tensor_tensor(dd[:, 2 * n:2 * n + 2, :], ps[:].rearrange("p (i c) -> p i c", i=2),
                                                c("dec_b").unsqueeze(1).broadcast_to([P, 2, D]), ALU.add
                                                ).then_inc(read, 1)
                    dve.wait_ge(*nth(b, "dect_ready", TT, f))
                    moments(dd, 2 + 3 * f, 4 * EPS)
                    for i in range(TT):
                        ins = nc.vector.tensor_scalar(dd[:, i, :], dd[:, i, :], mv[:, i, 0:1], rstd[:, i:i + 1],
                                                      ALU.subtract, ALU.mult)
                    link(ins)
                    link(nc.vector.tensor_tensor(dd[:], dd[:], c("ln_g").unsqueeze(1).broadcast_to([P, TT, D]),
                                                 ALU.mult))
                    link(nc.vector.tensor_tensor(dd[:], dd[:], c("ln_b").unsqueeze(1).broadcast_to([P, TT, D]),
                                                 ALU.add))
                    ins = nc.vector.tensor_tensor(x_res[:], x_res[:], dd[:], ALU.add)
                    if f == 1:
                        ins.then_inc(sem["y_ready"], 1)
                    else:
                        link(ins)

                local_attention()
                dve.wait_ge(*bank_read(b, ("pr", TT - 1)))
                experts(0)
                causal_attention()
                experts(1)
                assert step[0] == SIGNALS["dve_step"][0], step[0]

        @block.tensor
        def _(pe):
            pe.wait_ge(setup_dve, DVE_SETUP - 2)
            for k in range(KF):
                ins = nc.tensor.matmul(bank[0][:, 0:D], ones[:], dec_w[:, k, :], start=k == 0, stop=k == KF - 1)
            ins.then_inc(setup_pe, 1)
            for k in range(KF):
                ins = nc.tensor.matmul(bank[1][0:M, 0:1], s2c_w[:, k, :], ones[:, 0:1], start=k == 0,
                                       stop=k == KF - 1)
            ins.then_inc(setup_pe, 1)
            pe.wait_ge(setup_dve, DVE_SETUP)
            pe.wait_ge(setup_pool, 5)

            def product(b, name, call, out, pairs, read=()):
                for x in covered(name, read, call):
                    pe.wait_ge(*bank_read(b, x, call))
                pe.wait_ge(*bank_free(b, name, call))
                ps, full_ = place(name, call, full)
                for n, (w, x) in enumerate(pairs):
                    ins = nc.tensor.matmul(out(ps), w, x, start=n == 0, stop=n == len(pairs) - 1)
                ins.then_inc(full_, 1)

            def turn_xn(b, call):
                pe.wait_ge(*nth(b, "xn_ready", TT, call))
                for k in range(KD):
                    pe.wait_ge(*bank_free(b, ("xnT", k), call))
                    ps, full_ = place(("xnT", k), call, full)
                    for i in range(TT):
                        ins = nc.tensor.transpose(ps[:, i * P:(i + 1) * P], xn[:, i, k * P:(k + 1) * P], ident)
                    ins.then_inc(full_, 1)
                for x in latest([("xnT", k) for k in range(KD)], call):
                    pe.wait_ge(*bank_read(b, x, call))

            def queries_keys_values(b, call, w_of, v_of):
                for m in range(4):
                    product(b, ("qk", m), call, lambda ps: ps[:], [(w_of(m, k), xnT[:, k, :]) for k in range(KD)])
                for n in range(2):
                    pe.wait_ge(*bank_free(b, ("v", n), call))
                    ps, full_ = place(("v", n), call, full)
                    for i in range(2):
                        at = (2 * n + i) * P
                        for k in range(KD):
                            ins = nc.tensor.matmul(ps[:, i * D:(i + 1) * D], xnT[:, k, at:at + P], v_of(k),
                                                   start=k == 0, stop=k == KD - 1)
                    ins.then_inc(full_, 1)

            def output(b, i, call, w):
                for x in covered(("on", i), [("oT", i)], call):
                    pe.wait_ge(*bank_read(b, x, call))
                pe.wait_ge(*bank_free(b, ("on", i), call))
                ps, full_ = place(("on", i), call, full)
                for g in range(4):
                    ins = nc.tensor.transpose(ps[:, g * P:(g + 1) * P], oTs[:, i % 2, g * P:(g + 1) * P], ident)
                ins.then_inc(full_, 1)
                if call == 0:
                    pe.wait_ge(*nth(b, "oN_ready", i + 1))
                for x in covered(("oNT", i), [("on", i)], call):
                    pe.wait_ge(*bank_read(b, x, call))
                pe.wait_ge(*bank_free(b, ("oNT", i), call))
                ps, full_ = place(("oNT", i), call, full)
                for k in range(KD):
                    ins = nc.tensor.transpose(ps[:, k * P:(k + 1) * P], oN[:, i % 2, k * P:(k + 1) * P], ident)
                ins.then_inc(full_, 1)
                product(b, ("pr", i), call, lambda ps: ps[:, 0:D], [(oNT[:, i % 2, k, :], w[:, k, :]) for k in range(KD)],
                        read=[("oNT", i)])

            def turn_scores(b, i):
                for hf in range(2):
                    for x in covered(("tS", i, hf), [("sT", hf * NG + g) for g in range(NG)]):
                        pe.wait_ge(*bank_read(b, x))
                    pe.wait_ge(*bank_free(b, ("tS", i, hf)))
                    ps, full_ = place(("tS", i, hf), 0, full)
                    for g in range(NG):
                        rows = GROUP_J[g] * HPT
                        ins = nc.tensor.transpose(ps[:, g * P:g * P + rows], sT[0:rows, hf * NG + g, i * P:(i + 1) * P],
                                                  ident[0:rows, 0:rows])
                    ins.then_inc(full_, 1)

            def local_attention(b):
                turn_xn(b, 0)
                queries_keys_values(b, 0, lambda m, k: w_qkv[:, k, m * P:(m + 1) * P],
                                    lambda k: w_qkv[:, k, 2 * D:3 * D])
                kd, kp = 0, 0
                for n, (hf, g, col, r) in enumerate(PRODUCTS):
                    if n in FIRST:
                        pe.wait_ge(*bank_free(b, ("sT", hf * NG + g)))
                        ps, full_ = place(("sT", hf * NG + g), 0, full)
                    if n in BY_POOL:
                        kp += 1
                        pe.wait_ge(*nth(b, "prod_pool", kp))
                        src = prod_p[:, (kp - 1) % RP, :]
                    else:
                        kd += 1
                        pe.wait_ge(*nth(b, "prod_dve", kd))
                        src = prod_d[:, (kd - 1) % RD, :]
                    ins = nc.tensor.matmul(ps[HS * col:HS * (col + 1), :], slot_w[:, slot(n), :], src,
                                           start=r == 0, stop=r == 3)
                    ins.then_inc(full_ if n in LAST else sem["prod_used"], 1)
                turn_scores(b, 0)
                turn_scores(b, 1)
                pe.wait_ge(*nth(b, "vs_shifted", 64))
                for i in range(TT):
                    if i + 2 < TT:
                        turn_scores(b, i + 2)
                    pe.wait_ge(*nth(b, "band_read" + PARITY[i % 2], 16 * (i // 2 + 1)))
                    for q in range(4):
                        pe.wait_ge(*bank_free(b, ("pA", i, q)))
                        ps, full_ = place(("pA", i, q), 0, full)
                        for h in range(4 * q, 4 * q + 4):
                            ins = nc.tensor.transpose(ps[:, (h % 4) * P:(h % 4 + 1) * P],
                                                      band[:, i % 2, NEAR - 1:BW, h], ident)
                        ins.then_inc(full_, 1)
                    w = NEAR - 1
                    for q in range(2 if i > 0 else 0):
                        pe.wait_ge(*SETTLED)
                        pe.wait_ge(*bank_free(b, ("pB", i, q)))
                        ps, full_ = place(("pB", i, q), 0, full)
                        for h in range(8 * q, 8 * q + 8):
                            ins = nc.tensor.transpose(ps[0:w, (h % 8) * w:(h % 8 + 1) * w],
                                                      band[0:w, i % 2, 0:w, h], ident[0:w, 0:w])
                        ins.then_inc(full_, 1)
                    for x in covered(("oT", i), [("pA", i, q) for q in range(4)]
                                          + [("pB", i, q) for q in range(2 if i > 0 else 0)]):
                        pe.wait_ge(*bank_read(b, x))
                    pe.wait_ge(*bank_free(b, ("oT", i)))
                    ps, full_ = place(("oT", i), 0, full)
                    for g in range(4):
                        for col in range(4):
                            ins = nc.tensor.matmul(ps[HS * col:HS * (col + 1), g * P:(g + 1) * P],
                                                   V[:, i, 4 * g + col, :], ptA[:, 4 * g + col, :],
                                                   start=True, stop=True)
                        for col in range(4 if i > 0 else 0):
                            ins = nc.tensor.matmul(ps[HS * col:HS * (col + 1), g * P:g * P + w],
                                                   v_near[0:w, i - 1, 4 * g + col, :], ptB[0:w, 4 * g + col, :],
                                                   start=False, stop=True, skip_group_check=True)
                    ins.then_inc(full_, 1)
                    output(b, i, 0, w_out)

            def causal_attention(b):
                turn_xn(b, 2)
                queries_keys_values(b, 1, lambda m, k: (wq, wk)[m // KD][:, k, (m % KD) * P:(m % KD + 1) * P],
                                    lambda k: wv[:, k, :])
                pe.wait_ge(*bank_read(b, ("v", 0), 1))
                pe.wait_ge(*bank_read(b, ("v", 1), 1))
                pe.wait_ge(*nth(b, "stack_read", 16 * 24))
                K = 6 * HD
                for kind, u in causal_steps():
                    if kind == "S":
                        q, h = u // H, u % H
                        w = (q + 1) * P
                        pe.wait_ge(*bank_free(b, ("S", u)))
                        ps, full_ = place(("S", u), 0, full)
                        nc.tensor.matmul(ps[:, 0:w], q_st[0:K, h, q * P:w], k_st[0:K, h, 0:w], start=True, stop=False,
                                         skip_group_check=True)
                        nc.tensor.matmul(ps[:, q * P:w], ident_b[:], causal[:], start=False, stop=True,
                                         skip_group_check=True).then_inc(full_, 1)
                    elif kind == "T":
                        for x in covered(("T", u), [("S", u)]):
                            pe.wait_ge(*bank_read(b, x))
                        pe.wait_ge(*bank_free(b, ("T", u)))
                        ps, full_ = place(("T", u), 0, full)
                        for k in range(u // H + 1):
                            ins = nc.tensor.transpose(ps[:, k * P:(k + 1) * P], p_exp[:, u % RU, k * P:(k + 1) * P],
                                                      ident)
                        ins.then_inc(full_, 1)
                    elif kind == "V":
                        q, g = u // 4, u % 4
                        for x in latest([("T", 4 * u + n) for n in range(4)]):
                            pe.wait_ge(*bank_read(b, x))
                        if g == 0:
                            pe.wait_ge(*bank_free(b, ("oT", q), 1))
                            ps_o, full_o = place(("oT", q), 1, full)
                        for k in range(q + 1):
                            for col in range(4):
                                ins = nc.tensor.matmul(ps_o[HS * col:HS * (col + 1), g * P:(g + 1) * P],
                                                       V[:, k, 4 * g + col, :],
                                                       p_T[:, (4 * u + col) % RT, k * P:(k + 1) * P],
                                                       start=k == 0, stop=k == q)
                        ins.then_inc(full_o if g == 3 else sem["pv_done"], 1)
                    else:
                        output(b, u, 1, wo)

            def experts(b, f):
                turn_xn(b, 1 + 2 * f)
                for m in range(KF):
                    product(b, ("enc", m), f, lambda ps: ps[:],
                            [(enc_w[:, k, m * P:(m + 1) * P], xnT[:, k, :]) for k in range(KD)])
                product(b, "cont", f, lambda ps: ps[0:M, :], [(s2c_w[:, k, :], t_enc[:, k, :]) for k in range(KF)],
                        read=[("enc", m) for m in range(KF)])
                product(b, "rh", f, lambda ps: ps[0:M, :], [(c("rw1"), cont[:])], read=["cont"])
                for x in covered("lg", ["rh"], f):
                    pe.wait_ge(*bank_read(b, x, f))
                pe.wait_ge(*bank_free(b, "lg", f))
                ps, full_ = place("lg", f, full)
                for i in range(TT):
                    ins = nc.tensor.matmul(ps[:, i * E:(i + 1) * E], rh[:, i * P:(i + 1) * P], c("rw2"), start=True,
                                           stop=True)
                ins.then_inc(full_, 1)
                for p in range(E // 2):
                    for n in range(4 * p, 4 * p + 4):
                        product(b, ("hid", n), f, lambda ps: ps[:],
                                [(we1[:, n // 2, (n % 2) * P:(n % 2 + 1) * P], cont[:])])
                    if p == 0:
                        pe.wait_ge(*nth(b, "gates_ready", 1, f))
                        pe.wait_ge(*bank_free(b, "gT", f))
                        ps, full_ = place("gT", f, full)
                        for i in range(TT):
                            ins = nc.tensor.transpose(ps[0:E, i * P:(i + 1) * P], gates[:, i, :], ident)
                        ins.then_inc(full_, 1)
                    product(b, ("gb", p), f, lambda ps: ps[:], [(pair_sel[:, p, :], gT[:])], read=["gT"])
                    for x in covered(("eo", p), [("hid", n) for n in range(4 * p, 4 * p + 4)], f):
                        pe.wait_ge(*bank_read(b, x, f))
                    pe.wait_ge(*bank_free(b, ("eo", p), f))
                    ps, full_ = place(("eo", p), f, full)
                    for k in range(2):
                        for e in range(2):
                            ins = nc.tensor.matmul(ps[M * e:M * (e + 1), :], we2[:, 2 * p + e, k, :],
                                                   hid[:, (4 * p + 2 * e + k) % RH, :], start=k == 0, stop=k == 1)
                    ins.then_inc(full_, 1)
                pe.wait_ge(*nth(b, "moe_ready", 1, f))
                for m in range(KF):
                    product(b, ("c2s", m), f, lambda ps: ps[:], [(c("c2s_w", m * P, P), moe)])
                for n in range(TT // 2):
                    for x in covered(("dec", n), [("c2s", m) for m in range(KF)], f):
                        pe.wait_ge(*bank_read(b, x, f))
                    pe.wait_ge(*bank_free(b, ("dec", n), f))
                    ps, full_ = place(("dec", n), f, full)
                    for i in range(2):
                        at = (2 * n + i) * P
                        for k in range(KF):
                            ins = nc.tensor.matmul(ps[:, i * D:(i + 1) * D], t_moe[:, k, at:at + P], dec_w[:, k, :],
                                                   start=k == 0, stop=k == KF - 1)
                    ins.then_inc(full_, 1)

            with pe.Fori(0, NB) as b:
                local_attention(b)
                experts(b, 0)
                causal_attention(b)
                experts(b, 1)


def lay_out(a):
    def rows(w, k):
        return w.reshape(k, P, -1).transpose(1, 0, 2).reshape(P, -1)

    def padded(w):
        out = np.zeros((P,) + w.shape[1:], np.float32)
        out[:w.shape[0]] = w
        return out.reshape(P, -1)

    def spread(v):
        return np.broadcast_to(v[None, :], (P, v.shape[0]))

    A, B, F = ({k[len(p):]: v for k, v in a.items() if k.startswith(p)} for p in ("L0_attn_a_", "L0_attn_b_", "L0_ffn_"))
    row = np.arange(P)
    slot_mask = np.zeros((P, 4, HS), np.float32)
    for r in range(4):
        slot_mask[row, r, HPT * r + row // HD] = 1.0
    mask = np.zeros((P, 2, NG, T), np.float32)
    bias = np.zeros((P, 2, NG), np.float32)
    for g, n in enumerate(GROUP_J):
        for j in range(n):
            at = slice(j * HPT, (j + 1) * HPT)
            mask[at, :, g, :SLOTS[16 * g + j]] = NEG
            for hf in range(2):
                bias[at, hf, g] = A["pos_bias"][REF_OF[16 * g + j], hf * HPT:(hf + 1) * HPT]
    pair = np.zeros((P, E // 2, P), np.float32)
    for e in range(E):
        pair[e, e // 2, (e % 2) * M:(e % 2 + 1) * M] = 1.0
    parts = {
        "ident": np.eye(P, dtype=np.float32), "slot_mask": slot_mask, "offset_mask": mask, "pos_bias": bias,
        "se": np.tile(A["scale_embed"][REF_OF].T, (HPT, 1)), "w_qkv": rows(A["w_qkv"], KD),
        "w_out_a": rows(A["w_out"], KD), "gain": np.repeat(A["if_gain"], HD).reshape(KD, P).T,
        "wq": rows(B["Wq"], KD), "wk": rows(B["Wk"], KD), "wv": rows(B["Wv"], KD), "wo": rows(B["Wo"], KD),
        "bq": B["bq"].reshape(KD, P).T, "bk": B["bk"].reshape(KD, P).T, "bv": spread(B["bv"]), "bo": spread(B["bo"]),
        "enc_w": rows(F["enc_W"], KD), "enc_b": F["enc_b"].reshape(KF, P).T, "s2c_w": rows(F["s2c_W"], KF),
        "s2c_b": padded(F["s2c_b"][:, None]), "rw1": padded(np.concatenate([F["rW1"], F["rb1"][None]])),
        "rw2": padded(np.concatenate([F["rW2"], F["rb2"][None]])),
        "we1": padded(np.concatenate([F["We1"].transpose(1, 0, 2), F["be1"][None]])),
        "we2": F["We2"].reshape(E, 2, P, M).transpose(2, 0, 1, 3), "be2": F["be2"].reshape(E // 2, 2 * M).T,
        "c2s_w": np.concatenate([F["c2s_W"], F["c2s_W"]]), "c2s_b": F["c2s_b"].reshape(KF, P).T,
        "dec_w": rows(F["dec_W"], KF), "dec_b": spread(F["dec_b"]), "ln_g": spread(F["ln_g"]),
        "ln_b": spread(F["ln_b"]), "pair_sel": pair,
        "before": np.broadcast_to(np.tril(np.ones((E, E), np.float32), -1).reshape(1, -1), (P, E * E)),
        "causal": np.triu(np.full((P, P), NEG, np.float32), 1),
    }
    return np.concatenate([np.ascontiguousarray(parts[n]).reshape(P, w) for n, w in PACK], axis=1)


def kernel(**inputs):
    import concourse.bacc as _bacc
    from concourse.bass_utils import run_bass_kernel_spmd as _run

    a = {k: np.asarray(v) for k, v in inputs.items()}
    arrays = {"x": np.ascontiguousarray(a["L0_attn_a_x"]), "pack": np.ascontiguousarray(lay_out(a))}
    nc = _bacc.Bacc("TRN2", target_bir_lowering=False, num_devices=1)
    args = [nc.dram_tensor(n, v.shape, mybir.dt.float32, kind="ExternalInput").ap() for n, v in arrays.items()]
    args.append(nc.dram_tensor("out", (NB, T, D), mybir.dt.float32, kind="ExternalOutput").ap())
    build(nc, *args)
    r = _run(nc, [arrays], core_ids=[0])
    return r.results[0]["out"]
```

```python
import concourse.bass as bass
from concourse import mybir
from concourse.alu_op_type import AluOpType as ALU
from contextlib import ExitStack
from collections import namedtuple
import numpy as np

P = 128
NB, T, D = 8, 512, 256
TT = T // P
KD = D // P
H, HD = 16, 16
HS = 32
HPT = P // HD
NEAR = 41
SLOTS = [NEAR - 1 - s for s in range(NEAR)] + [96, 128, 384]
REF_OF = [NEAR - 1 - s for s in range(NEAR)] + [42, 41, 43]
J = len(SLOTS)
GROUP_J = [16, 16, 12]
NG = len(GROUP_J)
PAD = 384
BW = P + NEAR - 1
FF, M, E, EH = 512, 64, 8, 256
KF = FF // P
NEG = -1.0e30
EPS = 1e-5

PACK_A = [("ident", P), ("pos_bias", 2 * NG), ("w_qkv", KD * 3 * D), ("w_out_a", KD * D), ("gain", KD)]
PACK_B = [
    ("wq", KD * D), ("wk", KD * D), ("wv", KD * D), ("wo", KD * D), ("bq", KD), ("bk", KD), ("bv", D), ("bo", D),
    ("enc_w", KD * FF), ("enc_b", KF), ("s2c_w", KF * M), ("s2c_b", 1), ("rw1", M), ("rw2", E),
    ("we1", E * EH), ("we2", E * 2 * M), ("be2", E // 2), ("c2s_w", FF), ("c2s_b", KF),
    ("dec_w", KF * D), ("dec_b", D), ("ln_g", D), ("ln_b", D), ("pair_sel", (E // 2) * P), ("before", E * E),
]
PACK_S = [("slot_mask", 4 * HS), ("se", J), ("is_slot", NG * P), ("ahead", T), ("causal", P), ("causal_T", P)]


def columns(names):
    at, n = {}, 0
    for name, w in names:
        at[name] = (n, n + w)
        n += w
    return at, n


AT, KEPT_W = columns(PACK_A + PACK_B)
AT_S, SETUP_W = columns(PACK_S)
A_W = sum(w for _, w in PACK_A)

Call = namedtuple("Call", "stage i a b f batch")
IN_PAIR = {"A": 2, "B": 2, "F": 4}
SHARED = {"A": "AB", "B": "AB", "F": "F"}

NORM_PHASES = [("stats", 3), ("pow", 1), ("xn", 2), ("turn", 3)]
TILES = [
    ("tS", 0), ("tS", 1), ("p", 0), ("p", 1), ("keys", 0), ("tS", 2), ("oT", 0), ("p", 2), ("on", 0),
    ("keys", 1), ("oNT", 0), ("tS", 3), ("pr", 0), ("oT", 1), ("p", 3), ("on", 1),
    ("keys", 2), ("oNT", 1), ("pr", 1), ("oT", 2), ("on", 2),
    ("keys", 3), ("oNT", 2), ("pr", 2), ("oT", 3), ("on", 3), ("oNT", 3), ("pr", 3),
]
TILE_WEIGHTS = {"tS": 3, "p": 2, "keys": 4, "oT": 4, "on": 3, "oNT": 2, "pr": 2}
OUTPUTS = [("on", 0), ("on", 1), ("oNT", 0), ("pr", 0), ("on", 2), ("oNT", 1), ("pr", 1), ("on", 3), ("oNT", 2),
           ("pr", 2), ("oNT", 3), ("pr", 3)]
PHASES = {
    "A": NORM_PHASES + [("qkv", 11)] + [(("prod", n), 4) for n in range(11)]
         + [(x, 12 if x == ("keys", 0) else TILE_WEIGHTS[x[0]]) for x in TILES],
    "B": NORM_PHASES + [("qkv", 11), ("split", 10)] + [(("max", n), 25 if n == 0 else 3) for n in range(H // 2)]
         + [("maxT", 3)] + [(("step", n), 8 if n == 0 else 3) for n in range(4 * TT + 1)] + [(x, 2) for x in OUTPUTS],
    "F": NORM_PHASES + [(("enc", m), 2) for m in range(KF)] + [("cont", 5), ("rh", 2), ("lg", 3)]
         + [x for p in range(E // 2) for x in [(("hid", 4 * p + n), 1) for n in range(4)]
            + ([("gT", 1)] if p == 0 else []) + [(("gb", p), 1), (("eo", p), 3)]]
         + [(("c2s", m), 2) for m in range(KF)] + [(("dec", n), 4) for n in range(TT // 2)]
         + [("stats_2", 4), ("pow_2", 1), ("close", 6)],
}


def merged(stages):
    order = []
    for s in stages:
        total, done = sum(w for _, w in PHASES[s]), 0
        for name, w in PHASES[s]:
            done += w
            order.append((done / total, s, name))
    return [(s, name) for _, s, name in sorted(order, key=lambda x: x[0])]


def together(**programs):
    ahead = {s: next(p, None) for s, p in programs.items()}
    for s, name in merged(list(programs)):
        if ahead[s] == name:
            ahead[s] = next(programs[s], None)
    assert not any(ahead.values()), ahead


BANKS = {"A": ([0, 1, 2, 3], [4]), "B": ([0, 1, 2, 3], [4]), "F": ([5, 6, 7], [])}

SHARE = [[(0,), (1,), (2,), (3,)], [(0,), (1,), (2,), (3,)], [(0, 1), (2, 3)], [(0, 1, 2, 3)]]
QUADS = H // 4
STEPS = [(g, k) for g in range(QUADS) for k in range(TT)]
MAX_FILLS = [[(3, 0)], [(2, 0), (0, 3 * P)], [(1, 0)]]


def plan():
    order = {"A": [("xnT", 0), ("xnT", 1)], "B": [("xnT", 0), ("xnT", 1)], "F": [("xnT", 0), ("xnT", 1)]}
    qkv = [("qk", m) for m in range(4)] + [("v", n) for n in range(2)]
    a = order["A"]
    a.extend(qkv + [("sT", g) for g in range(2 * NG)])
    for kind, i in TILES:
        if kind == "tS":
            a.extend([("tS", i, 0), ("tS", i, 1)])
        elif kind == "keys":
            a.extend([("pA", i, q) for q in range(4)] + [("pB", i, q) for q in range(2) if i > 0])
        elif kind != "p":
            a.append((kind, i))
    b = order["B"]
    b.extend(qkv)
    for h in range(H):
        b.extend([("S", h, n) for n in range(len(MAX_FILLS))])
        if h == HPT + 1:
            b.append(("mT", 0))
    b.append(("mT", 1))
    for n in range(len(STEPS) + 1):
        if n < len(STEPS):
            b.extend([("ST", *STEPS[n], m) for m in range(len(SHARE[STEPS[n][1]]))])
        if n > 0 and STEPS[n - 1][1] == 0:
            b.append(("oT", STEPS[n - 1][0]))
    b.extend(OUTPUTS)
    f = order["F"]
    f.extend([("enc", m) for m in range(KF)] + ["cont", "rh", "lg"])
    for p in range(E // 2):
        f.extend([("hid", 4 * p + n) for n in range(4)])
        if p == 0:
            f.append("gT")
        f.extend([("gb", p), ("eo", p)])
    f.extend([("c2s", m) for m in range(KF)] + [("dec", n) for n in range(TT // 2)])
    fills, uses = {}, {}
    for s, names in order.items():
        turn, used, fills[s] = [0, 0], [0] * 8, {}
        for name in names:
            held = int(name[0] == "oT")
            bank = BANKS[s][held][turn[held] % len(BANKS[s][held])]
            turn[held] += 1
            fills[s][name] = (bank, used[bank])
            used[bank] += 1
        uses[s] = used
    return fills, uses


FILLS, USES = plan()

PRODUCTS = [(hf, g, col, r) for hf in range(2) for g in range(NG) for r in range(4) for col in range(GROUP_J[g] // 4)]
FIRST = [hf * J + 16 * g for hf in range(2) for g in range(NG)]
LAST = [n - 1 for n in FIRST[1:]] + [2 * J - 1]
BY_POOL = [n for n in range(2 * J) if n % 3 == 1]
BY_DVE = [n for n in range(2 * J) if n % 3 != 1]


def slot(n):
    _, g, col, r = PRODUCTS[n]
    return 16 * g + 4 * col + r


ATTN_SETUP = 9
DVE_SETUP = 22
PARITY = ("_even", "_odd")

NORM = {"var": 1, "rstd": 1, "xn_ready": TT}
SIGNALS = {
    "A": {
        **NORM, "x_loaded": 16, "vs_shifted": 64, "prod_dve": len(BY_DVE), "prod_pool": len(BY_POOL),
        "prod_used": 2 * J - len(LAST), "pa_ready": TT,
        "band_written_even": 16 * TT // 2, "band_written_odd": 16 * TT // 2,
        "band_read_even": 16 * TT // 2, "band_read_odd": 16 * TT // 2, "far_ready": TT, "oN_ready": TT,
        "dve_step": 22, "pool_step": 8,
    },
    "B": {
        **NORM, "hi_ready": 4, "r1_ready": 4, "mid_ready": 4, "lo_ready": 4,
        "split_written": 16 * 12, "stack_read": 16 * 24, "maxima_ready": 2,
        "maxima_written_even": 16, "maxima_written_odd": 16, "maxima_read_even": 16, "maxima_read_odd": 16,
        "ones_ready": 1, "pv_done": 12, "dve_step": 16,
    },
    "F": {
        **NORM, "var_2": 1, "rstd_2": 1, "lgd_ready": 1, "gexp_ready": 1, "gates_ready": 1, "dect_ready": TT,
        "moe_ready": 1, "x_ready": 1, "dve_step": 18,
    },
}


def build(nc, x_dram, kept_dram, setup_dram, out_dram):
    fp32, bf16 = mybir.dt.float32, mybir.dt.bfloat16
    ACT = mybir.ActivationFunctionType
    AX = mybir.AxisListType.X

    band_dram = nc.dram_tensor("band", (TT, P * (BW + 1) * H), fp32, kind="Internal").ap()
    maxima_dram = nc.dram_tensor("maxima", (2, 3, HPT, T), bf16, kind="Internal").ap()
    split_dram = nc.dram_tensor("splits", (4, 3, P, T), bf16, kind="Internal").ap()

    ctx = ExitStack()
    with ctx:
        def sb(name, shape, dt=fp32):
            return ctx.enter_context(nc.sbuf_tensor(name, shape, dt))

        kept = sb("kept", [P, KEPT_W])
        x_in = sb("x_in", [P, TT, D])
        x_of = [sb("x_even", [P, TT, D]), sb("x_odd", [P, TT, D])]
        v_96 = sb("v_96", [P, TT, H, HS])
        kT = sb("kT", [P, KD, PAD + T])
        cont = sb("cont", [P, T])
        rh = sb("rh", [P, T])
        gT = sb("gT", [P, T])
        V = sb("V", [P, TT, H, HS])
        slot_w = sb("slot_w", [P, J, HS])
        minus_half = sb("minus_half", [P, TT])
        ones = sb("ones", [P, P])
        half_c2s_b = sb("half_c2s_b", [P, KF])
        half_enc_b = sb("half_enc_b", [P, KF])
        q_bias = sb("q_bias", [P, KD])
        s2c_bias = sb("s2c_bias", [P, 1])
        causal = sb("causal_b", [P, P], bf16)
        causal_T = sb("causal_T", [P, P], bf16)
        ident_b = sb("ident_b", [P, P], bf16)
        is_slot = sb("is_slot", [P, NG * P], bf16)
        ahead = sb("ahead", [P, T], bf16)
        oN = sb("oN", [P, 2, D])
        oNT = sb("oNT", [P, 2, KD, P])
        den = sb("den", [P, 2, H])

        ARENA = {"AB": 15300, "F": 8850}
        arena = {k: sb("arena_" + k, [P, n]) for k, n in ARENA.items()}
        taken = {}

        def part(n, of="AB", at=None):
            a = taken.get(of, 0) if at is None else at
            taken[of] = a + n
            assert taken[of] <= ARENA[of], taken[of]
            return arena[of][:, a:a + n]

        xn_ab = sb("xn", [P, TT, D])
        xnT_ab = sb("xnT", [P, KD, T])
        oTs = xn_ab[:].rearrange("p (r a) c -> p r (a c)", r=2)
        qT = part(KD * T).rearrange("p (m t) -> p m t", m=KD)
        RD, RP = 6, 3
        prod_d = part(RD * T).rearrange("p (r t) -> p r t", r=RD)
        prod_p = part(RP * T).rearrange("p (r t) -> p r t", r=RP)
        after_products = taken["AB"]
        band = part(2 * BW * H, at=0).rearrange("p (r s h) -> p r s h", r=2, s=BW)
        sT = part(2 * NG * T, at=after_products).rearrange("p (g t) -> p g t", g=2 * NG)
        p_nat = part(2 * J * H).rearrange("p (r j h) -> p r j h", r=2, j=J)
        ptA = part(H * P).rearrange("p (h t) -> p h t", h=H)
        ptB = part(H * (NEAR - 1)).rearrange("p (h t) -> p h t", h=H)
        v_near = part((TT - 1) * H * HS).rearrange("p (i h d) -> p i h d", i=TT - 1, h=H)
        far = part(2 * D).rearrange("p (r h d) -> p r h d", r=2, h=H)
        far_t = part(D).rearrange("p (h d) -> p h d", h=H)
        mx = part(TT * H).rearrange("p (i h) -> p i h", i=TT)
        far_den = part(2 * H).rearrange("p (r h) -> p r h", r=2)
        qk32 = part(4 * T, at=0).rearrange("p (m t) -> p m t", m=4)
        split = part(4 * 3 * T // 2).bitcast(bf16).rearrange("p (m s t) -> p m s t", m=4, s=3)
        RS = 2
        p_T = part(RS * 4 * T, at=0).rearrange("p (r c q) -> p r c q", r=RS, c=4)
        oT_all = part(QUADS * T).rearrange("p (g t) -> p g t", g=QUADS)
        q_st = part(H * T // 2).bitcast(bf16).rearrange("p (h t) -> p h t", h=H)
        k_st = part(H * T // 2).bitcast(bf16).rearrange("p (h t) -> p h t", h=H)
        neg_max = part(TT * H).rearrange("p (h i) -> p h i", h=H)
        max_parts = part(2 * TT * 3 * HPT // 2).bitcast(bf16).rearrange("p (f i s h) -> p f i s h", f=2, i=TT, s=3)
        max_rest = part(TT * H).rearrange("p (h i) -> p h i", h=H)
        max_T = part(T).bitcast(bf16).rearrange("p (f t) -> p f t", f=2)
        t_enc = part(KF * T, "F").rearrange("p (m t) -> p m t", m=KF)
        t_moe = t_enc
        RH = 8
        hid_at = taken["F"]
        hid = part(RH * T, "F").rearrange("p (r t) -> p r t", r=RH)
        after_hid = taken["F"]
        xn_f = part(TT * D, "F", at=hid_at).rearrange("p (i c) -> p i c", i=TT)
        xnT_f = part(KD * T, "F").rearrange("p (k t) -> p k t", k=KD)
        dd = part(TT * D, "F", at=hid_at).rearrange("p (i c) -> p i c", i=TT)
        gb = part(2 * T, "F", at=after_hid).rearrange("p (r t) -> p r t", r=2)
        moe = part(T, "F")
        moe_t = part(T, "F")
        lg = part(TT * E, "F").rearrange("p (i e) -> p i e", i=TT)
        lgd = part(TT * E, "F").rearrange("p (i e) -> p i e", i=TT)
        above = part(TT * E * E, "F").rearrange("p (i e f) -> p i e f", i=TT, e=E)
        same = part(TT * E * E, "F").rearrange("p (i e f) -> p i e f", i=TT, e=E)
        rank = part(TT * E, "F").rearrange("p (i e) -> p i e", i=TT)
        gates = part(TT * E, "F").rearrange("p (i e) -> p i e", i=TT)
        lmax = part(TT, "F")
        gsum = part(TT, "F")
        setup_only = arena["F"][:, 0:SETUP_W]

        Norm = namedtuple("Norm", "xn xnT stats mv var rstd scrap")
        norms = {s: Norm(xn, xnT, *(sb(f"{n}_{s}", [P, *w]) for n, w in
                                    (("stats", (TT, 6)), ("mv", (TT, 2)), ("var_eps", (TT,)), ("rstd", (TT,)),
                                     ("scrap", (16,)))))
                 for s, xn, xnT in (("AB", xn_ab, xnT_ab), ("F", xn_f, xnT_f))}

        def c(name, a=0, n=None):
            lo, hi = AT[name]
            return kept[:, lo + a:hi if n is None else lo + a + n]

        def c3(name, k):
            return c(name).rearrange("p (k n) -> p k n", k=k)

        def s_only(name):
            lo, hi = AT_S[name]
            return setup_only[:, lo:hi]

        ident = c("ident")
        w_qkv, w_out = c3("w_qkv", KD), c3("w_out_a", KD)
        wq, wk, wv, wo = (c3(n, KD) for n in ("wq", "wk", "wv", "wo"))
        enc_w, s2c_w, dec_w = c3("enc_w", KD), c3("s2c_w", KF), c3("dec_w", KF)
        we1, we2 = c3("we1", E), c("we2").rearrange("p (e k m) -> p e k m", e=E, k=2)
        pair_sel = c3("pair_sel", E // 2)

        bank = [ctx.enter_context(nc.psum_tensor(f"bank{i}", [P, T], fp32)) for i in range(8)]
        full = [ctx.enter_context(nc.semaphore(f"bank{i}_full")) for i in range(8)]
        free = [ctx.enter_context(nc.semaphore(f"bank{i}_read")) for i in range(8)]
        sem = {s: {n: ctx.enter_context(nc.semaphore(f"{s}_{n}")) for n in names} for s, names in SIGNALS.items()}
        y_stored = [ctx.enter_context(nc.semaphore("y_stored" + x)) for x in PARITY]
        pack_a_loaded, pack_b_loaded, pack_s_loaded, setup_dve, setup_pool, setup_pe, setup_band = (
            ctx.enter_context(nc.semaphore(n)) for n in ("pack_a_loaded", "pack_b_loaded", "pack_s_loaded", "setup_dve",
                                                         "setup_pool", "setup_pe", "setup_band"))
        SETTLED = (pack_a_loaded, 16)

        def calls_before(u, s):
            return IN_PAIR[s], {"A": u.a, "B": u.b, "F": u.f}[s]

        def nth(u, name, k):
            per, (in_pair, ahead_) = SIGNALS[u.stage][name], calls_before(u, u.stage)
            return sem[u.stage][name], u.i * (in_pair * per) + (ahead_ * per + k)

        def fills_before(u, name):
            n, before = FILLS[u.stage][name]
            counts = [(calls_before(u, s), USES[s][n]) for s in SHARED[u.stage]]
            return n, sum(k * w for (k, _), w in counts), before + sum(a * w for (_, a), w in counts)

        def place(u, name, of=free):
            n, _ = FILLS[u.stage][name]
            return bank[n], of[n]

        def bank_full(u, name):
            n, per_pair, before = fills_before(u, name)
            return full[n], u.i * per_pair + (before + 1)

        def bank_read(u, name):
            n, per_pair, before = fills_before(u, name)
            return free[n], u.i * per_pair + (before + 2)

        def bank_free(u, name):
            n, per_pair, before = fills_before(u, name)
            return free[n], u.i * per_pair + (before + 1)

        def latest(u, names):
            fills = FILLS[u.stage]
            last = {fills[name][0]: name for name in sorted(names, key=lambda x: fills[x][1])}
            return list(last.values())

        def covered(u, name, others):
            return [x for x in latest(u, others) if FILLS[u.stage][x][0] != FILLS[u.stage][name][0]]

        def product_used(u, n):
            if n in LAST:
                return bank_full(u, ("sT", LAST.index(n)))
            return nth(u, "prod_used", sum(k not in LAST for k in range(n + 1)))

        def step_done(u, n):
            g, k = STEPS[n]
            return bank_full(u, ("oT", g)) if k == TT - 1 else nth(u, "pv_done", 3 * g + k + 1)

        def rows_of(dram, u):
            b = u.i * 2 + u.batch
            part_ = dram[b:b + 1] if isinstance(u.i, int) else dram[bass.ds(b, 1), :, :]
            return part_.rearrange("o (i p) n -> p (o i) n", p=P)

        PAIRS = NB // 2
        FIRST_A = Call("A", 0, 0, 0, 0, 0)

        def pair(i):
            return [(Call("A", i, 1, 0, 0, 1), Call("F", i, 0, 0, 0, 0)),
                    (Call("B", i, 2, 0, 0, 0), Call("F", i, 0, 0, 1, 1)),
                    (Call("B", i, 2, 1, 0, 1), Call("F", i, 0, 0, 2, 0)),
                    (Call("A", i, 2, 2, 0, 2), Call("F", i, 0, 0, 3, 1))]

        def rounds(engine, local, causal_, experts):
            def one(attn, moe_call):
                if attn.stage == "A":
                    together(A=local(attn), F=experts(moe_call))
                else:
                    together(B=causal_(attn), F=experts(moe_call))

            if PAIRS > 1:
                with engine.Fori(0, PAIRS - 1) as i:
                    for attn, moe_call in pair(i):
                        one(attn, moe_call)
            end = pair(PAIRS - 1)
            for attn, moe_call in end[0:3]:
                one(attn, moe_call)
            for _ in experts(end[3][1]):
                pass

        block = ctx.enter_context(nc.Block())

        @block.sync
        def _(sp):
            def load_x(u, batch):
                sp.dma_start(x_in[:], rows_of(x_dram, u._replace(batch=batch))).then_inc(sem["A"]["x_loaded"], 16)

            sp.dma_start(kept[:, 0:A_W], kept_dram[:, 0:A_W]).then_inc(pack_a_loaded, 16)
            load_x(FIRST_A, 0)
            sp.dma_start(setup_only, setup_dram).then_inc(pack_s_loaded, 16)
            sp.dma_start(kept[:, A_W:KEPT_W], kept_dram[:, A_W:KEPT_W]).then_inc(pack_b_loaded, 16)
            sp.wait_ge(setup_pool, 1)
            w = (BW + 1) * H // 8
            for i in range(TT):
                sp.dma_start(band_dram[i, :].rearrange("(t r w) -> t r w", t=P, r=8),
                             kT[:, 0:1, 0:w].broadcast_to([P, 8, w])).then_inc(setup_band, 16)
            sp.wait_ge(pack_a_loaded, 16)

            def local_attention(u):
                sp.wait_ge(*SETTLED)
                sp.wait_ge(*bank_read(u, ("v", 1)))
                vs_shifted = sem["A"]["vs_shifted"]
                sp.dma_start(v_96[0:96, 1:TT], V[32:P, 0:TT - 1]).then_inc(vs_shifted, 16)
                sp.dma_start(v_96[96:P, :], V[0:32, :]).then_inc(vs_shifted, 16)
                sp.dma_start(v_near[0:NEAR - 1, 0:2], V[P - NEAR + 1:P, 0:2]).then_inc(vs_shifted, 16)
                sp.dma_start(v_near[0:NEAR - 1, 2:3], V[P - NEAR + 1:P, 2:3]).then_inc(vs_shifted, 16)
                sp.wait_ge(setup_band, TT * 16)
                for i in range(TT + 1):
                    if i < TT:
                        sp.wait_ge(*SETTLED)
                        sp.wait_ge(*nth(u, "pa_ready", i + 1))
                        dst = band_dram[i, :].rearrange("(t r) -> t r", t=P)[:, 0:NEAR * H]
                        sp.dma_start(dst, p_nat[:, i % 2, 0:NEAR, :].rearrange("p j h -> p (j h)")
                                     ).then_inc(sem["A"]["band_written" + PARITY[i % 2]], 16)
                    if i >= 1:
                        k = i - 1
                        sp.wait_ge(*SETTLED)
                        sp.wait_ge(*nth(u, "band_written" + PARITY[k % 2], 16 * (k // 2 + 1)))
                        src = band_dram[k, 0:P * BW * H].rearrange("(t r) -> t r", t=P)
                        sp.dma_start(band[:, k % 2, :, :].rearrange("p s h -> p (s h)"), src
                                     ).then_inc(sem["A"]["band_read" + PARITY[k % 2]], 16)
                if not (isinstance(u.i, int) and 2 * u.i + u.batch == NB - 1):
                    sp.wait_ge(*SETTLED)
                    sp.wait_ge(*bank_read(u, ("pr", TT - 1)))
                    load_x(u, u.batch + 1)

            def causal_attention(u):
                for m in range(4):
                    sp.wait_ge(*SETTLED)
                    sp.wait_ge(*nth(u, "lo_ready", m + 1))
                    for s in range(3):
                        sp.dma_start(split_dram[m, s], split[:, m, s, :]).then_inc(sem["B"]["split_written"], 16)
                sp.wait_ge(*SETTLED)
                sp.wait_ge(*nth(u, "split_written", 16 * 12))
                for slot_, (sq, sk) in enumerate([(0, 0), (0, 1), (1, 0), (1, 1), (0, 2), (2, 0)]):
                    for half, (st, s) in enumerate([(q_st, sq), (k_st, sk)]):
                        for m in range(2):
                            src = split_dram[2 * half + m, s].rearrange("(h d) t -> d h t", d=HD)
                            sp.dma_start(st[slot_ * HD:(slot_ + 1) * HD, m * HPT:(m + 1) * HPT, :], src
                                         ).then_inc(sem["B"]["stack_read"], 16)
                for hf in range(2):
                    sp.wait_ge(*SETTLED)
                    sp.wait_ge(*bank_read(u, ("mT", hf)))
                    sp.dma_start(maxima_dram[hf].rearrange("s h t -> (s h) t"), max_T[0:3 * HPT, hf, :]
                                 ).then_inc(sem["B"]["maxima_written" + PARITY[hf]], 16)
                    sp.wait_ge(*SETTLED)
                    sp.wait_ge(*nth(u, "maxima_written" + PARITY[hf], 16))
                    sp.dma_start(q_st[6 * HD:6 * HD + 3, hf * HPT:(hf + 1) * HPT, :], maxima_dram[hf]
                                 ).then_inc(sem["B"]["maxima_read" + PARITY[hf]], 16)

            def store_y(u):
                sp.wait_ge(*SETTLED)
                sp.wait_ge(*nth(u, "x_ready", 1))
                sp.dma_start(rows_of(out_dram, u), x_of[u.batch][:]).then_inc(y_stored[u.batch], 16)

            def one(attn, moe_call):
                (local_attention if attn.stage == "A" else causal_attention)(attn)
                if moe_call.f >= 2:
                    store_y(moe_call)

            local_attention(FIRST_A)
            if PAIRS > 1:
                with sp.Fori(0, PAIRS - 1) as i:
                    for attn, moe_call in pair(i):
                        one(attn, moe_call)
            end = pair(PAIRS - 1)
            for attn, moe_call in end[0:3]:
                one(attn, moe_call)
            store_y(end[3][1])
            for s in y_stored:
                sp.wait_ge(s, 16 * PAIRS + 16)

        @block.gpsimd
        def _(pool):
            nc.gpsimd.memset(kT[:, :, 0:PAD], 0.0).then_inc(setup_pool, 1)
            nc.gpsimd.memset(V[:], 0.0).then_inc(setup_pool, 1)
            nc.gpsimd.memset(v_96[:, 0], 0.0).then_inc(setup_pool, 1)
            nc.gpsimd.memset(minus_half[:], -0.5).then_inc(setup_pool, 1)
            pool.wait_ge(setup_pool, 4)
            nc.gpsimd.memset(V[:, :, :, HD:HD + 1], 1.0).then_inc(setup_pool, 1)
            pool.wait_ge(setup_pool, 5)

            def power(u, norm, which=""):
                pool.wait_ge(*nth(u, "var" + which, 1))
                nc.gpsimd.tensor_tensor(norm.rstd[:], norm.var[:], minus_half[:], ALU.pow
                                        ).then_inc(sem[u.stage]["rstd" + which], 1)

            def local_attention(u):
                step = [0]

                def link(ins):
                    step[0] += 1
                    ins.then_inc(sem["A"]["pool_step"], 1)
                    pool.wait_ge(*nth(u, "pool_step", step[0]))

                yield "pow"
                power(u, norms["AB"])
                for k, n in enumerate(BY_POOL):
                    if k == 0 or n // 8 > BY_POOL[k - 1] // 8:
                        yield ("prod", n // 8)
                    if k == 0:
                        for x in latest(u, [("qk", m) for m in range(4)]):
                            pool.wait_ge(*bank_read(u, x))
                    hf, at = PRODUCTS[n][0], PAD - SLOTS[slot(n)]
                    if k >= RP:
                        pool.wait_ge(*product_used(u, BY_POOL[k - RP]))
                    nc.gpsimd.tensor_tensor(prod_p[:, k % RP, :], qT[:, hf, :], kT[:, hf, at:at + T],
                                            ALU.mult).then_inc(sem["A"]["prod_pool"], 1)
                for i in range(TT):
                    yield ("keys", i)
                    if i == 0:
                        pool.wait_ge(*nth(u, "vs_shifted", 64))
                    pool.wait_ge(*nth(u, "pa_ready", i + 1))
                    if i >= 2:
                        pool.wait_ge(*nth(u, "oN_ready", i - 1))
                    out = far[:, i % 2]

                    def p_of(s):
                        return p_nat[:, i % 2, s, :].unsqueeze(2).broadcast_to([P, H, HD])

                    terms = [(NEAR, v_96[:, i, :, 0:HD])]
                    if i >= 1:
                        terms.append((NEAR + 1, V[:, i - 1, :, 0:HD]))
                    if i >= 3:
                        terms.append((NEAR + 2, V[:, i - 3, :, 0:HD]))
                    for n, (s, v) in enumerate(terms):
                        last = nc.gpsimd.tensor_tensor(out if n == 0 else far_t, v, p_of(s), ALU.mult)
                        if n:
                            link(last)
                            last = nc.gpsimd.tensor_tensor(out, out, far_t, ALU.add)
                        if n < len(terms) - 1:
                            link(last)
                    last.then_inc(sem["A"]["far_ready"], 1)
                assert step[0] == SIGNALS["A"]["pool_step"], step[0]

            def causal_attention(u):
                yield "pow"
                power(u, norms["AB"])

            def experts(u):
                yield "pow"
                power(u, norms["F"])
                yield "pow_2"
                power(u, norms["F"], "_2")

            for _ in local_attention(FIRST_A):
                pass
            rounds(pool, local_attention, causal_attention, experts)

        @block.scalar
        def _(act):
            act.wait_ge(setup_dve, ATTN_SETUP)

            def read_xnT(u, norm):
                for k in range(KD):
                    act.wait_ge(*bank_full(u, ("xnT", k)))
                    ps, read = place(u, ("xnT", k))
                    nc.scalar.copy(norm.xnT[:, k, :], ps[:]).then_inc(read, 1)

            def read_oNT(u, i):
                act.wait_ge(*bank_full(u, ("oNT", i)))
                ps, read = place(u, ("oNT", i))
                nc.scalar.copy(oNT[:, i % 2, :, :], ps[:, 0:KD * P].rearrange("p (k t) -> p k t", k=KD)
                               ).then_inc(read, 1)

            def local_attention(u):
                yield "turn"
                read_xnT(u, norms["AB"])
                yield "qkv"
                for m in range(4):
                    act.wait_ge(*bank_full(u, ("qk", m)))
                    ps, read = place(u, ("qk", m))
                    dst = qT[:, m, :] if m < KD else kT[:, m - KD, PAD:PAD + T]
                    nc.scalar.copy(dst, ps[:]).then_inc(read, 1)
                for n in range(2):
                    act.wait_ge(*bank_full(u, ("v", n)))
                    ps, read = place(u, ("v", n))
                    nc.scalar.copy(V[:, 2 * n:2 * n + 2, :, 0:HD],
                                   ps[:].rearrange("p (i h d) -> p i h d", i=2, h=H)).then_inc(read, 1)
                for g in range(2 * NG):
                    yield ("prod", LAST[g] // 8)
                    rows = GROUP_J[g % NG] * HPT
                    act.wait_ge(*bank_full(u, ("sT", g)))
                    ps, read = place(u, ("sT", g))
                    nc.scalar.activation(sT[0:rows, g, :], ps[0:rows, :], ACT.Identity,
                                         bias=c("pos_bias", g, 1)[0:rows, :]).then_inc(read, 1)
                for kind, i in TILES:
                    if kind not in ("p", "keys", "oT", "oNT"):
                        continue
                    yield (kind, i)
                    if kind == "p":
                        act.wait_ge(*bank_read(u, ("tS", i, 0)))
                        act.wait_ge(*bank_read(u, ("tS", i, 1)))
                        nc.scalar.activation(p_nat[:, i % 2], p_nat[:, i % 2], ACT.Exp
                                             ).then_inc(sem["A"]["pa_ready"], 1)
                    elif kind == "keys":
                        for q in range(4):
                            act.wait_ge(*bank_full(u, ("pA", i, q)))
                            ps, read = place(u, ("pA", i, q))
                            nc.scalar.copy(ptA[:, 4 * q:4 * q + 4, :], ps[:].rearrange("p (h t) -> p h t", h=4)
                                           ).then_inc(read, 1)
                    elif kind == "oT":
                        act.wait_ge(*bank_full(u, ("oT", i)))
                        ps, read = place(u, ("oT", i))
                        nc.scalar.copy(oTs[:, i % 2, :], ps[:]).then_inc(read, 1)
                    else:
                        read_oNT(u, i)

            def causal_attention(u):
                yield "turn"
                read_xnT(u, norms["AB"])
                yield "qkv"
                for m in range(4):
                    act.wait_ge(*bank_full(u, ("qk", m)))
                    ps, read = place(u, ("qk", m))
                    if m < KD:
                        nc.scalar.activation(qk32[:, m, :], ps[:], ACT.Identity, bias=q_bias[:, m:m + 1],
                                             scale=HD ** -0.5).then_inc(read, 1)
                    else:
                        nc.scalar.activation(qk32[:, m, :], ps[:], ACT.Identity, bias=c("bk", m - KD, 1)
                                             ).then_inc(read, 1)
                    act.wait_ge(*bank_read(u, ("qk", m)))
                    nc.scalar.copy(split[:, m, 0, :], qk32[:, m, :]).then_inc(sem["B"]["hi_ready"], 1)
                yield "split"
                for m in range(4):
                    act.wait_ge(*nth(u, "r1_ready", m + 1))
                    nc.scalar.copy(split[:, m, 1, :], qk32[:, m, :]).then_inc(sem["B"]["mid_ready"], 1)
                for hf in range(2):
                    yield ("max", HPT // 2) if hf == 0 else "maxT"
                    act.wait_ge(*bank_full(u, ("mT", hf)))
                    ps, read = place(u, ("mT", hf))
                    nc.scalar.copy(max_T[0:3 * HPT, hf, :], ps[0:3 * HPT, 0:T // 2].bitcast(bf16)).then_inc(read, 1)
                for n in range(len(STEPS) + 1):
                    yield ("step", n)
                    if n < len(STEPS):
                        g, k = STEPS[n]
                        w = T - k * P
                        if n >= RS:
                            act.wait_ge(*step_done(u, n - RS))
                        for m, cols in enumerate(SHARE[k]):
                            act.wait_ge(*bank_full(u, ("ST", g, k, m)))
                            ps, read = place(u, ("ST", g, k, m))
                            nc.scalar.activation(p_T[:, n % RS, cols[0]:cols[-1] + 1, 0:w],
                                                 ps[:, 0:len(cols) * w].rearrange("p (c q) -> p c q", c=len(cols)),
                                                 ACT.Exp).then_inc(read, 1)
                    if n > 0 and STEPS[n - 1][1] == TT - 1:
                        g = STEPS[n - 1][0]
                        act.wait_ge(*bank_full(u, ("oT", g)))
                        ps, read = place(u, ("oT", g))
                        nc.scalar.copy(oT_all[:, g, :], ps[:]).then_inc(read, 1)
                for i in range(TT):
                    yield ("oNT", i)
                    read_oNT(u, i)

            def experts(u):
                yield "turn"
                read_xnT(u, norms["F"])
                for m in range(KF):
                    yield ("enc", m)
                    act.wait_ge(*bank_full(u, ("enc", m)))
                    ps, read = place(u, ("enc", m))
                    nc.scalar.activation(t_enc[:, m, :], ps[:], ACT.Tanh, bias=half_enc_b[:, m:m + 1], scale=0.5
                                         ).then_inc(read, 1)
                yield "cont"
                act.wait_ge(*bank_full(u, "cont"))
                ps, read = place(u, "cont")
                nc.scalar.activation(cont[0:M, :], ps[0:M, :], ACT.Identity, bias=s2c_bias[0:M, :]).then_inc(read, 1)
                yield "rh"
                act.wait_ge(*bank_full(u, "rh"))
                ps, read = place(u, "rh")
                nc.scalar.activation(rh[0:M, :], ps[0:M, :], ACT.Tanh).then_inc(read, 1)
                for p in range(E // 2):
                    for n in range(4 * p, 4 * p + 4):
                        yield ("hid", n)
                        for x in covered(u, ("hid", n), [("eo", (n - RH) // 4)]) if n >= RH else ():
                            act.wait_ge(*bank_full(u, x))
                        act.wait_ge(*bank_full(u, ("hid", n)))
                        ps, read = place(u, ("hid", n))
                        nc.scalar.activation(hid[:, n % RH, :], ps[:], ACT.Relu).then_inc(read, 1)
                        if n == 1:
                            act.wait_ge(*nth(u, "lgd_ready", 1))
                            nc.scalar.activation(lgd[:], lgd[:], ACT.Exp).then_inc(sem["F"]["gexp_ready"], 1)
                    if p == 0:
                        yield "gT"
                        act.wait_ge(*bank_full(u, "gT"))
                        ps, read = place(u, "gT")
                        nc.scalar.copy(gT[0:E, :], ps[0:E, :]).then_inc(read, 1)
                    yield ("gb", p)
                    act.wait_ge(*bank_full(u, ("gb", p)))
                    ps, read = place(u, ("gb", p))
                    if p >= 2:
                        act.wait_ge(*bank_read(u, ("eo", p - 2)))
                    nc.scalar.copy(gb[:, p % 2, :], ps[:]).then_inc(read, 1)
                for m in range(KF):
                    yield ("c2s", m)
                    act.wait_ge(*bank_full(u, ("c2s", m)))
                    ps, read = place(u, ("c2s", m))
                    nc.scalar.activation(t_moe[:, m, :], ps[:], ACT.Tanh, bias=half_c2s_b[:, m:m + 1], scale=0.5
                                         ).then_inc(read, 1)
                for n in range(TT // 2):
                    yield ("dec", n)
                    act.wait_ge(*bank_read(u, ("dec", n)))
                    for i in (2 * n, 2 * n + 1):
                        nc.scalar.activation(dd[:, i, :], dd[:, i, :], ACT.Tanh, scale=0.5
                                             ).then_inc(sem["F"]["dect_ready"], 1)

            for _ in local_attention(FIRST_A):
                pass
            act.wait_ge(setup_dve, DVE_SETUP)
            rounds(act, local_attention, causal_attention, experts)

        @block.vector
        def _(dve):
            setup = [0]

            def once(ins):
                setup[0] += 1
                ins.then_inc(setup_dve, 1)
                dve.wait_ge(setup_dve, setup[0])

            scrap = norms["AB"].scrap
            for n, s in enumerate(free):
                nc.vector.memset(scrap[:, n:n + 1], 0.0).then_inc(s, 1)
            for n, s in enumerate(y_stored):
                nc.vector.memset(scrap[:, 8 + n:9 + n], 0.0).then_inc(s, 16)
            dve.wait_ge(pack_a_loaded, 16)
            for k in range(KD):
                once(nc.vector.tensor_scalar(w_out[:, k, :], w_out[:, k, :], c("gain", k, 1), None, ALU.mult))
            once(nc.vector.tensor_copy(ident_b[:], ident))
            dve.wait_ge(pack_s_loaded, 16)
            once(nc.vector.tensor_scalar(s_only("se"), s_only("se"), 1.0, HD ** -0.5, ALU.add, ALU.mult))
            once(nc.vector.tensor_tensor(
                slot_w[:].rearrange("p (a r) d -> p a r d", r=4),
                s_only("slot_mask").rearrange("p (r d) -> p r d", r=4).unsqueeze(1).broadcast_to([P, J // 4, 4, HS]),
                s_only("se").rearrange("p (a r) -> p a r", r=4).unsqueeze(3).broadcast_to([P, J // 4, 4, HS]),
                ALU.mult))
            once(nc.vector.tensor_copy(is_slot[:], s_only("is_slot")))
            once(nc.vector.tensor_copy(ahead[:], s_only("ahead")))
            once(nc.vector.tensor_copy(causal[:], s_only("causal")))
            once(nc.vector.tensor_copy(causal_T[:], s_only("causal_T")))
            assert setup[0] == ATTN_SETUP, setup[0]

            step = {}

            def link(u, ins):
                step[u.stage] += 1
                ins.then_inc(sem[u.stage]["dve_step"], 1)
                dve.wait_ge(*nth(u, "dve_step", step[u.stage]))

            def counted(u):
                assert step[u.stage] == SIGNALS[u.stage]["dve_step"], (u.stage, step)

            def moments(u, src, norm, eps, which=""):
                yield "stats" + which
                if u.stage == "A":
                    dve.wait_ge(*nth(u, "x_loaded", 16))
                if which:
                    dve.wait_ge(*nth(u, "dect_ready", TT))
                for i in range(TT):
                    ins = nc.vector.bn_stats(norm.stats[:, i, :], src[:, i, :])
                link(u, ins)
                nc.vector.memset(norm.scrap[:, 15:16], 0.0)
                for i in range(TT):
                    ins = nc.vector.bn_aggr(norm.mv[:, i, :], norm.stats[:, i, :])
                link(u, ins)
                nc.vector.tensor_scalar(norm.var[:], norm.mv[:, :, 1], eps, None, ALU.add
                                        ).then_inc(sem[u.stage]["var" + which], 1)
                yield "close" if which else "xn"
                dve.wait_ge(*nth(u, "rstd" + which, 1))

            def layer_norm(u, src, norm):
                yield from moments(u, src, norm, EPS)
                for i in range(TT):
                    nc.vector.tensor_scalar(norm.xn[:, i, :], src[:, i, :], norm.mv[:, i, 0:1], norm.rstd[:, i:i + 1],
                                            ALU.subtract, ALU.mult).then_inc(sem[u.stage]["xn_ready"], 1)

            def softmax_local(u, i):
                if i >= 2:
                    dve.wait_ge(*nth(u, "band_written" + PARITY[i % 2], 16 * (i // 2)))
                    dve.wait_ge(*nth(u, "far_ready", i - 1))
                halves = []
                for hf in range(2):
                    dve.wait_ge(*bank_full(u, ("tS", i, hf)))
                    ps, read = place(u, ("tS", i, hf))
                    s = ps[:, 0:J * HPT].rearrange("p (j h) -> p j h", j=J)
                    halves.append((s, read))
                    m = mx[:, i, hf * HPT:(hf + 1) * HPT]
                    link(u, nc.vector.tensor_reduce(m, s.rearrange("p j h -> p h j"), AX, ALU.max))
                for hf, (s, read) in enumerate(halves):
                    m = mx[:, i, hf * HPT:(hf + 1) * HPT]
                    nc.vector.tensor_tensor(p_nat[:, i % 2, :, hf * HPT:(hf + 1) * HPT], s,
                                            m.unsqueeze(1).broadcast_to([P, J, HPT]), ALU.subtract
                                            ).then_inc(read, 1)

            def normalise_local(u, i):
                dve.wait_ge(*bank_full(u, ("on", i)))
                ps, read = place(u, ("on", i))
                o = ps[:].rearrange("p (h d) -> p h d", h=H)
                link(u, nc.vector.tensor_tensor(den[:, i % 2, :], o[:, :, HD], far_den[:, i % 2], ALU.add))
                link(u, nc.vector.reciprocal(den[:, i % 2, :], den[:, i % 2, :]))
                dve.wait_ge(*nth(u, "far_ready", i + 1))
                on = oN[:, i % 2, :].rearrange("p (h d) -> p h d", h=H)
                nc.vector.tensor_tensor(on, o[:, :, 0:HD], far[:, i % 2], ALU.add).then_inc(read, 1)
                dve.wait_ge(*bank_read(u, ("on", i)))
                nc.vector.tensor_tensor(on, on, den[:, i % 2, :].unsqueeze(2).broadcast_to([P, H, HD]), ALU.mult
                                        ).then_inc(sem["A"]["oN_ready"], 1)

            def local_attention(u):
                step["A"] = 0
                yield from layer_norm(u, x_in, norms["AB"])
                for k, n in enumerate(BY_DVE):
                    if k == 0 or n // 8 > BY_DVE[k - 1] // 8:
                        yield ("prod", n // 8)
                    if k == 0:
                        for x in latest(u, [("qk", m) for m in range(4)]):
                            dve.wait_ge(*bank_read(u, x))
                    hf, at = PRODUCTS[n][0], PAD - SLOTS[slot(n)]
                    if k >= RD:
                        dve.wait_ge(*product_used(u, BY_DVE[k - RD]))
                    nc.vector.tensor_tensor(prod_d[:, k % RD, :], qT[:, hf, :], kT[:, hf, at:at + T],
                                            ALU.mult).then_inc(sem["A"]["prod_dve"], 1)
                for kind, i in TILES:
                    if kind not in ("tS", "keys", "on", "pr"):
                        continue
                    yield (kind, i)
                    if kind == "tS":
                        softmax_local(u, i)
                    elif kind == "keys":
                        dve.wait_ge(*nth(u, "pa_ready", i + 1))
                        link(u, nc.vector.tensor_reduce(
                            far_den[:, i % 2], p_nat[:, i % 2, NEAR:J, :].rearrange("p j h -> p h j"), AX, ALU.add))
                        for q in range(2 if i > 0 else 0):
                            dve.wait_ge(*bank_full(u, ("pB", i, q)))
                            ps, read = place(u, ("pB", i, q))
                            nc.vector.tensor_copy(ptB[0:NEAR - 1, 8 * q:8 * q + 8, :],
                                                  ps[0:NEAR - 1, 0:8 * (NEAR - 1)].rearrange(
                                                      "p (h t) -> p h t", h=8)).then_inc(read, 1)
                    elif kind == "on":
                        normalise_local(u, i)
                    else:
                        if i == 0:
                            dve.wait_ge(y_stored[u.batch % 2], u.i * 16 + (u.batch // 2 + 1) * 16)
                        dve.wait_ge(*bank_full(u, ("pr", i)))
                        ps, read = place(u, ("pr", i))
                        nc.vector.tensor_tensor(x_of[u.batch % 2][:, i, :], ps[:, 0:D], x_in[:, i, :], ALU.add
                                                ).then_inc(read, 1)
                dve.wait_ge(*bank_read(u, ("pr", TT - 1)))
                counted(u)

            def causal_attention(u):
                step["B"] = 0
                x_ = x_of[u.batch]
                yield from layer_norm(u, x_, norms["AB"])
                nc.vector.memset(k_st[6 * HD:6 * HD + 3, :, :], 1.0).then_inc(sem["B"]["ones_ready"], 1)
                yield "qkv"
                for n in range(2):
                    dve.wait_ge(*bank_full(u, ("v", n)))
                    ps, read = place(u, ("v", n))
                    for i in range(2):
                        ins = nc.vector.tensor_tensor(
                            V[:, 2 * n + i, :, 0:HD], ps[:, i * D:(i + 1) * D].rearrange("p (h d) -> p h d", h=H),
                            c("bv").rearrange("p (h d) -> p h d", h=H), ALU.add)
                    ins.then_inc(read, 1)
                yield "split"
                for m in range(4):
                    dve.wait_ge(*nth(u, "hi_ready", m + 1))
                    nc.vector.tensor_tensor(qk32[:, m, :], qk32[:, m, :], split[:, m, 0, :], ALU.subtract
                                            ).then_inc(sem["B"]["r1_ready"], 1)
                for m in range(4):
                    dve.wait_ge(*nth(u, "mid_ready", m + 1))
                    nc.vector.tensor_tensor(split[:, m, 2, :], qk32[:, m, :], split[:, m, 1, :], ALU.subtract
                                            ).then_inc(sem["B"]["lo_ready"], 1)
                for h in range(H):
                    if h % 2 == 0:
                        yield ("max", h // 2)
                    for n, tiles in enumerate(MAX_FILLS):
                        dve.wait_ge(*bank_full(u, ("S", h, n)))
                        ps, read = place(u, ("S", h, n))
                        for i, at in tiles:
                            ins = nc.vector.tensor_reduce(neg_max[:, h, i:i + 1], ps[:, at:at + (i + 1) * P], AX,
                                                          ALU.max, negate=True)
                        ins.then_inc(read, 1)
                    if h % HPT == HPT - 1:
                        hf = h // HPT
                        nm = neg_max[:, hf * HPT:h + 1, :].rearrange("p h i -> p i h")
                        rest = max_rest[:, hf * HPT:h + 1, :].rearrange("p h i -> p i h")
                        for x in latest(u, [("S", h, n) for n in range(len(MAX_FILLS))]):
                            dve.wait_ge(*bank_read(u, x))
                        link(u, nc.vector.tensor_copy(max_parts[:, hf, :, 0, :], nm))
                        link(u, nc.vector.tensor_tensor(rest, nm, max_parts[:, hf, :, 0, :], ALU.subtract))
                        link(u, nc.vector.tensor_copy(max_parts[:, hf, :, 1, :], rest))
                        nc.vector.tensor_tensor(max_parts[:, hf, :, 2, :], rest, max_parts[:, hf, :, 1, :],
                                                ALU.subtract).then_inc(sem["B"]["maxima_ready"], 1)
                for kind, i in OUTPUTS:
                    if kind == "on":
                        yield (kind, i)
                        dve.wait_ge(*bank_full(u, ("on", i)))
                        ps, read = place(u, ("on", i))
                        o = ps[:].rearrange("p (h d) -> p h d", h=H)
                        link(u, nc.vector.reciprocal(den[:, i % 2, :], o[:, :, HD]))
                        on = oN[:, i % 2, :].rearrange("p (h d) -> p h d", h=H)
                        nc.vector.tensor_tensor(on, o[:, :, 0:HD], den[:, i % 2, :].unsqueeze(2).broadcast_to([P, H, HD]),
                                                ALU.mult).then_inc(read, 1)
                    elif kind == "pr":
                        yield (kind, i)
                        dve.wait_ge(*bank_full(u, ("pr", i)))
                        ps, read = place(u, ("pr", i))
                        nc.vector.tensor_tensor(x_[:, i, :], ps[:, 0:D], x_[:, i, :], ALU.add).then_inc(read, 1)
                        dve.wait_ge(*bank_read(u, ("pr", i)))
                        link(u, nc.vector.tensor_tensor(x_[:, i, :], x_[:, i, :], c("bo"), ALU.add))
                counted(u)

            def experts(u):
                step["F"] = 0
                x_ = x_of[u.batch]
                yield from layer_norm(u, x_, norms["F"])
                yield "lg"
                dve.wait_ge(*bank_full(u, "lg"))
                ps, read = place(u, "lg")
                nc.vector.tensor_copy(lg[:], ps[:, 0:TT * E].rearrange("p (i e) -> p i e", i=TT)
                                      ).then_inc(read, 1)
                dve.wait_ge(*bank_read(u, "lg"))
                link(u, nc.vector.tensor_reduce(lmax[:], lg[:], AX, ALU.max))
                nc.vector.tensor_tensor(lgd[:], lg[:], lmax[:].unsqueeze(2).broadcast_to([P, TT, E]),
                                        ALU.subtract).then_inc(sem["F"]["lgd_ready"], 1)
                other = lg[:].unsqueeze(2).broadcast_to([P, TT, E, E])
                own = lg[:].unsqueeze(3).broadcast_to([P, TT, E, E])
                before = c("before").rearrange("p (e f) -> p e f", e=E).unsqueeze(1).broadcast_to([P, TT, E, E])
                nc.vector.tensor_tensor(above[:], other, own, ALU.is_gt)
                link(u, nc.vector.tensor_tensor(same[:], other, own, ALU.is_equal))
                link(u, nc.vector.tensor_tensor(same[:], same[:], before, ALU.mult))
                link(u, nc.vector.tensor_tensor(above[:], above[:], same[:], ALU.add))
                link(u, nc.vector.tensor_reduce(rank[:], above[:], AX, ALU.add))
                link(u, nc.vector.tensor_scalar(rank[:], rank[:], 1.5, None, ALU.is_lt))
                yield ("hid", 2)
                dve.wait_ge(*nth(u, "gexp_ready", 1))
                link(u, nc.vector.tensor_tensor(gates[:], lgd[:], rank[:], ALU.mult))
                link(u, nc.vector.tensor_reduce(gsum[:], gates[:], AX, ALU.add))
                link(u, nc.vector.reciprocal(gsum[:], gsum[:]))
                nc.vector.tensor_tensor(gates[:], gates[:], gsum[:].unsqueeze(2).broadcast_to([P, TT, E]),
                                        ALU.mult).then_inc(sem["F"]["gates_ready"], 1)
                for p in range(E // 2):
                    yield ("eo", p)
                    dve.wait_ge(*bank_full(u, ("eo", p)))
                    ps, read = place(u, ("eo", p))
                    dve.wait_ge(*bank_read(u, ("gb", p)))
                    nc.vector.scalar_tensor_tensor(
                        out=moe[:] if p == 0 else moe_t[:], in0=ps[:], scalar=c("be2", p, 1),
                        in1=gb[:, p % 2, :], op0=ALU.add, op1=ALU.mult).then_inc(read, 1)
                    if p > 0:
                        dve.wait_ge(*bank_read(u, ("eo", p)))
                        ins = nc.vector.tensor_tensor(moe[:], moe[:], moe_t[:], ALU.add)
                        if p == E // 2 - 1:
                            ins.then_inc(sem["F"]["moe_ready"], 1)
                        else:
                            link(u, ins)
                for n in range(TT // 2):
                    yield ("dec", n)
                    dve.wait_ge(*bank_full(u, ("dec", n)))
                    ps, read = place(u, ("dec", n))
                    nc.vector.tensor_tensor(dd[:, 2 * n:2 * n + 2, :], ps[:].rearrange("p (i c) -> p i c", i=2),
                                            c("dec_b").unsqueeze(1).broadcast_to([P, 2, D]), ALU.add
                                            ).then_inc(read, 1)
                norm = norms["F"]
                yield from moments(u, dd, norm, 4 * EPS, "_2")
                for i in range(TT):
                    ins = nc.vector.tensor_scalar(dd[:, i, :], dd[:, i, :], norm.mv[:, i, 0:1], norm.rstd[:, i:i + 1],
                                                  ALU.subtract, ALU.mult)
                link(u, ins)
                link(u, nc.vector.tensor_tensor(dd, dd, c("ln_g").unsqueeze(1).broadcast_to([P, TT, D]), ALU.mult))
                link(u, nc.vector.tensor_tensor(dd, dd, c("ln_b").unsqueeze(1).broadcast_to([P, TT, D]), ALU.add))
                nc.vector.tensor_tensor(x_[:], x_[:], dd, ALU.add).then_inc(sem["F"]["x_ready"], 1)
                dve.wait_ge(*nth(u, "x_ready", 1))
                counted(u)

            for _ in local_attention(FIRST_A):
                pass
            once(nc.vector.memset(ones[:], 1.0))
            for t in (cont, rh, gT):
                once(nc.vector.memset(t[:], 0.0))
            once(nc.vector.memset(cont[M:M + 1, :], 1.0))
            once(nc.vector.memset(rh[M:M + 1, :], 1.0))
            dve.wait_ge(pack_b_loaded, 16)
            once(nc.vector.tensor_scalar(half_enc_b[:], c("enc_b"), 0.5, None, ALU.mult))
            once(nc.vector.tensor_scalar(half_c2s_b[:], c("c2s_b"), 0.5, None, ALU.mult))
            once(nc.vector.tensor_scalar(q_bias[:], c("bq"), HD ** -0.5, None, ALU.mult))
            once(nc.vector.tensor_scalar(c("s2c_w"), c("s2c_w"), 0.5, None, ALU.mult))
            once(nc.vector.tensor_scalar(c("dec_w"), c("dec_w"), 0.5, None, ALU.mult))
            dve.wait_ge(setup_pe, 2)
            once(nc.vector.tensor_tensor(c("dec_b"), bank[5][:, 0:D], c("dec_b"), ALU.add))
            once(nc.vector.tensor_tensor(s2c_bias[0:M, :], bank[6][0:M, 0:1], c("s2c_b")[0:M, :], ALU.add))
            assert setup[0] == DVE_SETUP, setup[0]
            rounds(dve, local_attention, causal_attention, experts)

        @block.tensor
        def _(pe):
            pe.wait_ge(setup_dve, ATTN_SETUP)
            pe.wait_ge(setup_pool, 5)

            def product(u, name, out, pairs, read=()):
                for x in covered(u, name, read):
                    pe.wait_ge(*bank_read(u, x))
                pe.wait_ge(*bank_free(u, name))
                ps, full_ = place(u, name, full)
                for n, (w, x) in enumerate(pairs):
                    ins = nc.tensor.matmul(out(ps), w, x, start=n == 0, stop=n == len(pairs) - 1)
                ins.then_inc(full_, 1)

            def turn_xn(u, norm):
                pe.wait_ge(*nth(u, "xn_ready", TT))
                for k in range(KD):
                    pe.wait_ge(*bank_free(u, ("xnT", k)))
                    ps, full_ = place(u, ("xnT", k), full)
                    for i in range(TT):
                        ins = nc.tensor.transpose(ps[:, i * P:(i + 1) * P], norm.xn[:, i, k * P:(k + 1) * P], ident)
                    ins.then_inc(full_, 1)

            def xnT_read(u):
                for x in latest(u, [("xnT", k) for k in range(KD)]):
                    pe.wait_ge(*bank_read(u, x))

            def queries_keys_values(u, w_of, v_of):
                xnT_read(u)
                for m in range(4):
                    product(u, ("qk", m), lambda ps: ps[:], [(w_of(m, k), xnT_ab[:, k, :]) for k in range(KD)])
                for n in range(2):
                    pe.wait_ge(*bank_free(u, ("v", n)))
                    ps, full_ = place(u, ("v", n), full)
                    for i in range(2):
                        at = (2 * n + i) * P
                        for k in range(KD):
                            ins = nc.tensor.matmul(ps[:, i * D:(i + 1) * D], xnT_ab[:, k, at:at + P], v_of(k),
                                                   start=k == 0, stop=k == KD - 1)
                    ins.then_inc(full_, 1)

            def output(u, kind, i, src, w):
                if kind == "on":
                    for x in covered(u, ("on", i), [("oT", i)] if u.stage == "A" else [("oT", g) for g in range(QUADS)]):
                        pe.wait_ge(*bank_read(u, x))
                    pe.wait_ge(*bank_free(u, ("on", i)))
                    ps, full_ = place(u, ("on", i), full)
                    for g in range(4):
                        ins = nc.tensor.transpose(ps[:, g * P:(g + 1) * P], src(g), ident)
                    ins.then_inc(full_, 1)
                elif kind == "oNT":
                    if u.stage == "A":
                        pe.wait_ge(*nth(u, "oN_ready", i + 1))
                    for x in covered(u, ("oNT", i), [("on", i)]):
                        pe.wait_ge(*bank_read(u, x))
                    pe.wait_ge(*bank_free(u, ("oNT", i)))
                    ps, full_ = place(u, ("oNT", i), full)
                    for k in range(KD):
                        ins = nc.tensor.transpose(ps[:, k * P:(k + 1) * P], oN[:, i % 2, k * P:(k + 1) * P], ident)
                    ins.then_inc(full_, 1)
                else:
                    product(u, ("pr", i), lambda ps: ps[:, 0:D],
                            [(oNT[:, i % 2, k, :], w[:, k, :]) for k in range(KD)], read=[("oNT", i)])

            def turn_scores(u, i):
                for hf in range(2):
                    for x in covered(u, ("tS", i, hf), [("sT", hf * NG + g) for g in range(NG)]):
                        pe.wait_ge(*bank_read(u, x))
                    pe.wait_ge(*bank_free(u, ("tS", i, hf)))
                    ps, full_ = place(u, ("tS", i, hf), full)
                    for g in range(NG):
                        rows = GROUP_J[g] * HPT
                        ins = nc.tensor.transpose(ps[:, g * P:g * P + rows], sT[0:rows, hf * NG + g, i * P:(i + 1) * P],
                                                  ident[0:rows, 0:rows])
                    ins.then_inc(full_, 1)

            def local_attention(u):
                yield "turn"
                turn_xn(u, norms["AB"])
                yield "qkv"
                queries_keys_values(u, lambda m, k: w_qkv[:, k, m * P:(m + 1) * P], lambda k: w_qkv[:, k, 2 * D:3 * D])
                kd, kp = 0, 0
                for n, (hf, g, col, r) in enumerate(PRODUCTS):
                    if n % 8 == 0:
                        yield ("prod", n // 8)
                    if n in FIRST:
                        pe.wait_ge(*bank_free(u, ("sT", hf * NG + g)))
                        ps, full_ = place(u, ("sT", hf * NG + g), full)
                        rows = GROUP_J[g] * HPT
                        nc.tensor.matmul(ps[0:rows, :], is_slot[:, g * P:g * P + rows], ahead[:], start=True,
                                         stop=False, skip_group_check=True)
                    if n in BY_POOL:
                        kp += 1
                        pe.wait_ge(*nth(u, "prod_pool", kp))
                        src = prod_p[:, (kp - 1) % RP, :]
                    else:
                        kd += 1
                        pe.wait_ge(*nth(u, "prod_dve", kd))
                        src = prod_d[:, (kd - 1) % RD, :]
                    ins = nc.tensor.matmul(ps[HS * col:HS * (col + 1), :], slot_w[:, slot(n), :], src,
                                           start=False, stop=r == 3, skip_group_check=True)
                    ins.then_inc(full_ if n in LAST else sem["A"]["prod_used"], 1)
                w = NEAR - 1
                for kind, i in TILES:
                    if kind == "p":
                        continue
                    yield (kind, i)
                    if kind == "tS":
                        turn_scores(u, i)
                    elif kind == "keys":
                        if i == 0:
                            pe.wait_ge(*nth(u, "vs_shifted", 64))
                        pe.wait_ge(*nth(u, "band_read" + PARITY[i % 2], 16 * (i // 2 + 1)))
                        for q in range(4):
                            pe.wait_ge(*bank_free(u, ("pA", i, q)))
                            ps, full_ = place(u, ("pA", i, q), full)
                            for h in range(4 * q, 4 * q + 4):
                                ins = nc.tensor.transpose(ps[:, (h % 4) * P:(h % 4 + 1) * P],
                                                          band[:, i % 2, NEAR - 1:BW, h], ident)
                            ins.then_inc(full_, 1)
                        for q in range(2 if i > 0 else 0):
                            pe.wait_ge(*bank_free(u, ("pB", i, q)))
                            ps, full_ = place(u, ("pB", i, q), full)
                            nc.tensor.matmul(ps[:, 0:P], ident_b[:], causal[:], start=True, stop=True)
                            for h in range(8 * q, 8 * q + 8):
                                ins = nc.tensor.transpose(ps[0:w, (h % 8) * w:(h % 8 + 1) * w],
                                                          band[0:w, i % 2, 0:w, h], ident[0:w, 0:w])
                            ins.then_inc(full_, 1)
                    elif kind == "oT":
                        for x in covered(u, ("oT", i), [("pA", i, q) for q in range(4)]
                                         + [("pB", i, q) for q in range(2 if i > 0 else 0)]):
                            pe.wait_ge(*bank_read(u, x))
                        pe.wait_ge(*bank_free(u, ("oT", i)))
                        ps, full_ = place(u, ("oT", i), full)
                        for g in range(4):
                            for col in range(4):
                                ins = nc.tensor.matmul(ps[HS * col:HS * (col + 1), g * P:(g + 1) * P],
                                                       V[:, i, 4 * g + col, :], ptA[:, 4 * g + col, :],
                                                       start=True, stop=True)
                            for col in range(4 if i > 0 else 0):
                                ins = nc.tensor.matmul(ps[HS * col:HS * (col + 1), g * P:g * P + w],
                                                       v_near[0:w, i - 1, 4 * g + col, :], ptB[0:w, 4 * g + col, :],
                                                       start=False, stop=True, skip_group_check=True)
                        ins.then_inc(full_, 1)
                    else:
                        output(u, kind, i, lambda g: oTs[:, i % 2, g * P:(g + 1) * P], w_out)

            def turn_maxima(u, hf):
                pe.wait_ge(*nth(u, "maxima_ready", hf + 1))
                pe.wait_ge(*bank_free(u, ("mT", hf)))
                ps, full_ = place(u, ("mT", hf), full)
                nc.tensor.matmul(ps[:, 0:P], ident_b[:], causal[:], start=True, stop=True)
                for i in range(TT):
                    ins = nc.tensor.transpose(ps[0:3 * HPT, i * P // 2:(i + 1) * P // 2].bitcast(bf16),
                                              max_parts[:, hf, i, :, :].rearrange("p s h -> p (s h)"), ident_b[:])
                ins.then_inc(full_, 1)

            def causal_attention(u):
                yield "turn"
                turn_xn(u, norms["AB"])
                yield "qkv"
                queries_keys_values(u, lambda m, k: (wq, wk)[m // KD][:, k, (m % KD) * P:(m % KD + 1) * P],
                                    lambda k: wv[:, k, :])
                K = 6 * HD
                for h in range(H):
                    if h % 2 == 0:
                        yield ("max", h // 2)
                    if h == 0:
                        pe.wait_ge(*nth(u, "stack_read", 16 * 24))
                    for n, tiles in enumerate(MAX_FILLS):
                        pe.wait_ge(*bank_free(u, ("S", h, n)))
                        ps, full_ = place(u, ("S", h, n), full)
                        for i, at in tiles:
                            nc.tensor.matmul(ps[:, at:at + (i + 1) * P], q_st[0:K, h, i * P:(i + 1) * P],
                                             k_st[0:K, h, 0:(i + 1) * P], start=True, stop=False,
                                             skip_group_check=True)
                            ins = nc.tensor.matmul(ps[:, at + i * P:at + (i + 1) * P], ident_b[:], causal[:],
                                                   start=False, stop=True, skip_group_check=True)
                        ins.then_inc(full_, 1)
                    if h == HPT + 1:
                        turn_maxima(u, 0)
                yield "maxT"
                turn_maxima(u, 1)
                for n in range(len(STEPS) + 1):
                    yield ("step", n)
                    if n == 0:
                        pe.wait_ge(*nth(u, "ones_ready", 1))
                        for x in latest(u, [("v", 0), ("v", 1)]):
                            pe.wait_ge(*bank_read(u, x))
                    if n < len(STEPS):
                        g, k = STEPS[n]
                        w = T - k * P
                        if k == 0 and g % 2 == 0:
                            pe.wait_ge(*nth(u, "maxima_read" + PARITY[g // 2], 16))
                        for m, cols in enumerate(SHARE[k]):
                            pe.wait_ge(*bank_free(u, ("ST", g, k, m)))
                            ps, full_ = place(u, ("ST", g, k, m), full)
                            for at, col in enumerate(cols):
                                h = 4 * g + col
                                nc.tensor.matmul(ps[:, at * w:(at + 1) * w], k_st[0:K + 3, h, k * P:(k + 1) * P],
                                                 q_st[0:K + 3, h, k * P:T], start=True, stop=False,
                                                 skip_group_check=True)
                                ins = nc.tensor.matmul(ps[:, at * w:at * w + P], ident_b[:], causal_T[:],
                                                       start=False, stop=True, skip_group_check=True)
                            ins.then_inc(full_, 1)
                    if n > 0:
                        g, k = STEPS[n - 1]
                        w = T - k * P
                        for x in latest(u, [("ST", g, k, m) for m in range(len(SHARE[k]))]):
                            pe.wait_ge(*bank_read(u, x))
                        if k == 0:
                            pe.wait_ge(*bank_free(u, ("oT", g)))
                            ps_o, full_o = place(u, ("oT", g), full)
                        for col in range(4):
                            ins = nc.tensor.matmul(ps_o[HS * col:HS * (col + 1), k * P:T], V[:, k, 4 * g + col, :],
                                                   p_T[:, (n - 1) % RS, col, 0:w], start=k == 0, stop=k == TT - 1,
                                                   skip_group_check=True)
                        ins.then_inc(full_o if k == TT - 1 else sem["B"]["pv_done"], 1)
                for kind, i in OUTPUTS:
                    yield (kind, i)
                    output(u, kind, i, lambda g: oT_all[:, g, i * P:(i + 1) * P], wo)

            def experts(u):
                yield "turn"
                turn_xn(u, norms["F"])
                for m in range(KF):
                    yield ("enc", m)
                    if m == 0:
                        xnT_read(u)
                    product(u, ("enc", m), lambda ps: ps[:],
                            [(enc_w[:, k, m * P:(m + 1) * P], xnT_f[:, k, :]) for k in range(KD)])
                yield "cont"
                product(u, "cont", lambda ps: ps[0:M, :], [(s2c_w[:, k, :], t_enc[:, k, :]) for k in range(KF)],
                        read=[("enc", m) for m in range(KF)])
                yield "rh"
                product(u, "rh", lambda ps: ps[0:M, :], [(c("rw1"), cont[:])], read=["cont"])
                yield "lg"
                for x in covered(u, "lg", ["rh"]):
                    pe.wait_ge(*bank_read(u, x))
                pe.wait_ge(*bank_free(u, "lg"))
                ps, full_ = place(u, "lg", full)
                for i in range(TT):
                    ins = nc.tensor.matmul(ps[:, i * E:(i + 1) * E], rh[:, i * P:(i + 1) * P], c("rw2"), start=True,
                                           stop=True)
                ins.then_inc(full_, 1)
                for p in range(E // 2):
                    for n in range(4 * p, 4 * p + 4):
                        yield ("hid", n)
                        product(u, ("hid", n), lambda ps: ps[:],
                                [(we1[:, n // 2, (n % 2) * P:(n % 2 + 1) * P], cont[:])])
                    if p == 0:
                        yield "gT"
                        pe.wait_ge(*nth(u, "gates_ready", 1))
                        pe.wait_ge(*bank_free(u, "gT"))
                        ps, full_ = place(u, "gT", full)
                        for i in range(TT):
                            ins = nc.tensor.transpose(ps[0:E, i * P:(i + 1) * P], gates[:, i, :], ident)
                        ins.then_inc(full_, 1)
                    yield ("gb", p)
                    product(u, ("gb", p), lambda ps: ps[:], [(pair_sel[:, p, :], gT[:])], read=["gT"])
                    yield ("eo", p)
                    for x in covered(u, ("eo", p), [("hid", n) for n in range(4 * p, 4 * p + 4)]):
                        pe.wait_ge(*bank_read(u, x))
                    pe.wait_ge(*bank_free(u, ("eo", p)))
                    ps, full_ = place(u, ("eo", p), full)
                    for k in range(2):
                        for e in range(2):
                            ins = nc.tensor.matmul(ps[M * e:M * (e + 1), :], we2[:, 2 * p + e, k, :],
                                                   hid[:, (4 * p + 2 * e + k) % RH, :], start=k == 0, stop=k == 1)
                    ins.then_inc(full_, 1)
                for m in range(KF):
                    yield ("c2s", m)
                    if m == 0:
                        pe.wait_ge(*nth(u, "moe_ready", 1))
                    product(u, ("c2s", m), lambda ps: ps[:], [(c("c2s_w", m * P, P), moe)])
                for n in range(TT // 2):
                    yield ("dec", n)
                    for x in covered(u, ("dec", n), [("c2s", m) for m in range(KF)]):
                        pe.wait_ge(*bank_read(u, x))
                    pe.wait_ge(*bank_free(u, ("dec", n)))
                    ps, full_ = place(u, ("dec", n), full)
                    for i in range(2):
                        at = (2 * n + i) * P
                        for k in range(KF):
                            ins = nc.tensor.matmul(ps[:, i * D:(i + 1) * D], t_moe[:, k, at:at + P], dec_w[:, k, :],
                                                   start=k == 0, stop=k == KF - 1)
                    ins.then_inc(full_, 1)

            for _ in local_attention(FIRST_A):
                pass
            pe.wait_ge(setup_dve, DVE_SETUP - 2)
            for k in range(KF):
                ins = nc.tensor.matmul(bank[5][:, 0:D], ones[:], dec_w[:, k, :], start=k == 0, stop=k == KF - 1)
            ins.then_inc(setup_pe, 1)
            for k in range(KF):
                ins = nc.tensor.matmul(bank[6][0:M, 0:1], s2c_w[:, k, :], ones[:, 0:1], start=k == 0,
                                       stop=k == KF - 1)
            ins.then_inc(setup_pe, 1)
            pe.wait_ge(setup_dve, DVE_SETUP)
            rounds(pe, local_attention, causal_attention, experts)


def lay_out(a):
    def rows(w, k):
        return w.reshape(k, P, -1).transpose(1, 0, 2).reshape(P, -1)

    def padded(w):
        out = np.zeros((P,) + w.shape[1:], np.float32)
        out[:w.shape[0]] = w
        return out.reshape(P, -1)

    def spread(v):
        return np.broadcast_to(v[None, :], (P, v.shape[0]))

    A, B, F = ({k[len(p):]: v for k, v in a.items() if k.startswith(p)} for p in ("L0_attn_a_", "L0_attn_b_", "L0_ffn_"))
    row = np.arange(P)
    slot_mask = np.zeros((P, 4, HS), np.float32)
    for r in range(4):
        slot_mask[row, r, HPT * r + row // HD] = 1.0
    is_slot = np.zeros((P, NG, P), np.float32)
    ahead = np.zeros((P, T), np.float32)
    bias = np.zeros((P, 2, NG), np.float32)
    for g, n in enumerate(GROUP_J):
        for j in range(n):
            at = slice(j * HPT, (j + 1) * HPT)
            is_slot[16 * g + j, g, at] = 1.0
            ahead[16 * g + j, :SLOTS[16 * g + j]] = NEG
            for hf in range(2):
                bias[at, hf, g] = A["pos_bias"][REF_OF[16 * g + j], hf * HPT:(hf + 1) * HPT]
    pair_ = np.zeros((P, E // 2, P), np.float32)
    for e in range(E):
        pair_[e, e // 2, (e % 2) * M:(e % 2 + 1) * M] = 1.0
    parts = {
        "ident": np.eye(P, dtype=np.float32), "slot_mask": slot_mask, "is_slot": is_slot, "ahead": ahead,
        "pos_bias": bias,
        "se": np.tile(A["scale_embed"][REF_OF].T, (HPT, 1)), "w_qkv": rows(A["w_qkv"], KD),
        "w_out_a": rows(A["w_out"], KD), "gain": np.repeat(A["if_gain"], HD).reshape(KD, P).T,
        "wq": rows(B["Wq"], KD), "wk": rows(B["Wk"], KD), "wv": rows(B["Wv"], KD), "wo": rows(B["Wo"], KD),
        "bq": B["bq"].reshape(KD, P).T, "bk": B["bk"].reshape(KD, P).T, "bv": spread(B["bv"]), "bo": spread(B["bo"]),
        "enc_w": rows(F["enc_W"], KD), "enc_b": F["enc_b"].reshape(KF, P).T, "s2c_w": rows(F["s2c_W"], KF),
        "s2c_b": padded(F["s2c_b"][:, None]), "rw1": padded(np.concatenate([F["rW1"], F["rb1"][None]])),
        "rw2": padded(np.concatenate([F["rW2"], F["rb2"][None]])),
        "we1": padded(np.concatenate([F["We1"].transpose(1, 0, 2), F["be1"][None]])),
        "we2": F["We2"].reshape(E, 2, P, M).transpose(2, 0, 1, 3), "be2": F["be2"].reshape(E // 2, 2 * M).T,
        "c2s_w": np.concatenate([F["c2s_W"], F["c2s_W"]]), "c2s_b": F["c2s_b"].reshape(KF, P).T,
        "dec_w": rows(F["dec_W"], KF), "dec_b": spread(F["dec_b"]), "ln_g": spread(F["ln_g"]),
        "ln_b": spread(F["ln_b"]), "pair_sel": pair_,
        "before": np.broadcast_to(np.tril(np.ones((E, E), np.float32), -1).reshape(1, -1), (P, E * E)),
        "causal": np.triu(np.full((P, P), NEG, np.float32), 1),
        "causal_T": np.tril(np.full((P, P), NEG, np.float32), -1),
    }
    return tuple(np.concatenate([np.ascontiguousarray(parts[n]).reshape(P, w) for n, w in names], axis=1)
                 for names in (PACK_A + PACK_B, PACK_S))


def kernel(**inputs):
    import concourse.bacc as _bacc
    from concourse.bass_utils import run_bass_kernel_spmd as _run

    a = {k: np.asarray(v) for k, v in inputs.items()}
    kept, setup_ = lay_out(a)
    arrays = {"x": np.ascontiguousarray(a["L0_attn_a_x"]), "kept_pack": kept, "setup_pack": setup_}
    nc = _bacc.Bacc("TRN2", target_bir_lowering=False, num_devices=1)
    args = [nc.dram_tensor(n, v.shape, mybir.dt.float32, kind="ExternalInput").ap() for n, v in arrays.items()]
    args.append(nc.dram_tensor("out", (NB, T, D), mybir.dt.float32, kind="ExternalOutput").ap())
    build(nc, *args)
    r = _run(nc, [arrays], core_ids=[0])
    return r.results[0]["out"]
```

```python
import concourse.bass as bass
from concourse import mybir
from concourse.alu_op_type import AluOpType as ALU
from contextlib import ExitStack
from collections import namedtuple
import numpy as np

P = 128
NB, T, D = 8, 512, 256
TT = T // P
KD = D // P
H, HD = 16, 16
HS = 32
HPT = P // HD
NEAR = 41
SLOTS = [NEAR - 1 - s for s in range(NEAR)] + [96, 128, 384]
REF_OF = [NEAR - 1 - s for s in range(NEAR)] + [42, 41, 43]
J = len(SLOTS)
GROUP_J = [16, 16, 12]
NG = len(GROUP_J)
PAD = 384
BW = P + NEAR - 1
FF, M, E, EH = 512, 64, 8, 256
KF = FF // P
NEG = -1.0e30
EPS = 1e-5

PACK_A = [("ident", P), ("pos_bias", 2 * NG), ("w_qkv", KD * 3 * D), ("w_out_a", KD * D), ("gain", KD)]
PACK_B = [
    ("wq", KD * D), ("wk", KD * D), ("wv", KD * D), ("wo", KD * D), ("bq", KD), ("bk", KD), ("bv", D), ("bo", D),
    ("enc_w", KD * FF), ("enc_b", KF), ("s2c_w", KF * 2 * M), ("s2c_b", 1), ("rw1", M), ("rb1", 1), ("rw2", E),
    ("be1", 2 * E), ("we2", E * 2 * M), ("be2", E // 2), ("c2s_w", FF), ("c2s_b", KF),
    ("dec_w", KF * D), ("dec_b", D), ("ln_g", D), ("ln_b", D), ("before", E * E),
]
PACK_S = [("pair_sel", (E // 2) * P), ("slot_mask", 4 * HS), ("se", J), ("is_slot", NG * P), ("ahead", T), ("causal", P),
          ("causal_T", P), ("we1", E * EH)]


def columns(names):
    at, n = {}, 0
    for name, w in names:
        at[name] = (n, n + w)
        n += w
    return at, n


AT, KEPT_W = columns(PACK_A + PACK_B)
AT_S, SETUP_W = columns(PACK_S)
A_W = sum(w for _, w in PACK_A)
S_W = SETUP_W - E * EH

Call = namedtuple("Call", "stage i a b f batch")
IN_PAIR = {"A": 2, "B": 2, "F": 4}
SHARED = {"A": "AB", "B": "AB", "F": "F"}

NORM_PHASES = ["stats", "pow", "xn", "turn"]
TILES = [
    ("tS", 0), ("tS", 1), ("p", 0), ("p", 1), ("keys", 0), ("tS", 2), ("oT", 0), ("p", 2), ("on", 0),
    ("keys", 1), ("oNT", 0), ("tS", 3), ("pr", 0), ("oT", 1), ("p", 3), ("on", 1),
    ("keys", 2), ("oNT", 1), ("pr", 1), ("oT", 2), ("on", 2),
    ("keys", 3), ("oNT", 2), ("pr", 2), ("oT", 3), ("on", 3), ("oNT", 3), ("pr", 3),
]
OUTPUTS = [("on", 0), ("on", 1), ("oNT", 0), ("pr", 0), ("on", 2), ("oNT", 1), ("pr", 1), ("on", 3), ("oNT", 2),
           ("pr", 2), ("oNT", 3), ("pr", 3)]
EXPERTS = [
    *[("hid", n) for n in range(6)], ("gT", 0), ("hid", 6), ("gb", 0), ("hid", 7), ("eo", 0),
    ("hid", 8), ("gb", 1), ("hid", 9), ("eo", 1), ("hid", 10), ("hid", 11), ("hid", 12), ("gb", 2), ("hid", 13),
    ("eo", 2), ("hid", 14), ("hid", 15), ("gb", 3), ("eo", 3),
]
PHASES = {
    "A": NORM_PHASES + ["qkv"] + [("prod", n) for n in range(11)] + TILES,
    "B": NORM_PHASES + ["qkv", "split"] + [("max", n) for n in range(H // 2)] + ["maxT"]
         + [("step", n) for n in range(4 * TT + 1)] + OUTPUTS,
    "F": NORM_PHASES + [("enc", m) for m in range(KF)] + ["cont", "rh", "lg"] + EXPERTS
         + [("c2s", m) for m in range(KF)] + [("dec", n) for n in range(TT // 2)] + ["stats_2", "pow_2", "close"],
}
WEIGHTS = {
    "A": [
        3, 1, 2, 3, 11, 4, 4, 4, 4, 4, 4, 4, 4, 4, 4, 4, 3, 3, 2, 2, 12, 3, 4, 1.4, 2.1, 4, 2, 3, 2, 4, 1.4,
        3, 4, 2, 4, 4, 3, 4, 2, 2, 4, 3, 2, 2,
    ],
    "B": [
        3, 1, 2, 3, 11, 10, 30, 3, 3, 3, 1.5, 3, 3, 3, 3, 8, 3, 3, 3, 3, 3, 3, 3, 4.2, 3, 3, 3, 3, 3, 3, 3,
        3, 2, 2, 4, 2, 2, 2, 2, 2, 2, 2, 2, 2,
    ],
    "F beside A": [
        3, 1, 2, 3, 2, 2, 2, 2, 5, 2, 3, 1, 1, 2, 1, 1, 1, 1, 1, 1, 1, 3, 1, 1, 1, 3, 1, 1, 1, 1, 1, 3, 1,
        1, 1, 3, 2, 2, 2, 2, 4, 4, 4, 1, 6,
    ],
    "F beside B": [
        3, 1, 2, 3, 2, 2, 2, 2, 5, 2, 3, 1, 1, 2, 1, 1, 1, 1, 0.5, 1, 1, 3, 1, 1, 1, 3, 1, 1, 1, 1, 1, 3, 1,
        1, 1, 3, 2, 2, 2, 2, 4, 4, 4, 1, 6,
    ],
}
SPAN = {"A": (0, 1), "B": (0, 1), "F": (0.056, 0.916)}


def merged(stages):
    order = []
    for s in stages:
        weights = WEIGHTS["F beside " + stages[0] if s == "F" else s]
        total, done = sum(weights), 0
        for name, w in zip(PHASES[s], weights, strict=True):
            done += w
            first, span = SPAN[s]
            order.append((first + span * done / total, s, name))
    return [(s, name) for _, s, name in sorted(order, key=lambda x: x[0])]


def together(**programs):
    ahead = {s: next(p, None) for s, p in programs.items()}
    for s, name in merged(list(programs)):
        if ahead[s] == name:
            ahead[s] = next(programs[s], None)
    assert not any(ahead.values()), ahead


BANKS = {"A": ([0, 1, 2, 3], [4]), "B": ([0, 1, 2, 3], [4]), "F": ([5, 6, 7], [])}

SHARE = [[(0,), (1,), (2,), (3,)], [(0,), (1,), (2,), (3,)], [(0, 1), (2, 3)], [(0, 1, 2, 3)]]
QUADS = H // 4
STEPS = [(g, k) for g in range(QUADS) for k in range(TT)]
MAX_FILLS = [[(3, 0)], [(2, 0), (0, 3 * P)], [(1, 0)]]


def plan():
    order = {"A": [("xnT", 0), ("xnT", 1)], "B": [("xnT", 0), ("xnT", 1)], "F": [("xnT", 0), ("xnT", 1)]}
    qkv = [("qk", m) for m in range(4)] + [("v", n) for n in range(2)]
    a = order["A"]
    a.extend(qkv + [("sT", g) for g in range(2 * NG)])
    for kind, i in TILES:
        if kind == "tS":
            a.extend([("tS", i, 0), ("tS", i, 1)])
        elif kind == "keys":
            a.extend([("pA", i, q) for q in range(4)] + [("pB", i, q) for q in range(2) if i > 0])
        elif kind != "p":
            a.append((kind, i))
    b = order["B"]
    b.extend(qkv)
    for h in range(H):
        b.extend([("S", h, n) for n in range(len(MAX_FILLS))])
        if h == HPT + 1:
            b.append(("mT", 0))
    b.append(("mT", 1))
    for n in range(len(STEPS) + 1):
        if n < len(STEPS):
            b.extend([("ST", *STEPS[n], m) for m in range(len(SHARE[STEPS[n][1]]))])
        if n > 0 and STEPS[n - 1][1] == 0:
            b.append(("oT", STEPS[n - 1][0]))
    b.extend(OUTPUTS)
    f = order["F"]
    f.extend([("enc", m) for m in range(KF)] + ["cont", "rh", "lg"] + EXPERTS)
    f.extend([("c2s", m) for m in range(KF)] + [("dec", n) for n in range(TT // 2)])
    fills, uses = {}, {}
    for s, names in order.items():
        turn, used, fills[s] = [0, 0], [0] * 8, {}
        for name in names:
            held = int(name[0] == "oT")
            bank = BANKS[s][held][turn[held] % len(BANKS[s][held])]
            turn[held] += 1
            fills[s][name] = (bank, used[bank])
            used[bank] += 1
        uses[s] = used
    return fills, uses


FILLS, USES = plan()

PRODUCTS = [(hf, g, col, r) for hf in range(2) for g in range(NG) for r in range(4) for col in range(GROUP_J[g] // 4)]
FIRST = [hf * J + 16 * g for hf in range(2) for g in range(NG)]
LAST = [n - 1 for n in FIRST[1:]] + [2 * J - 1]
BY_POOL = [n for n in range(2 * J) if n % 3 == 1]
BY_DVE = [n for n in range(2 * J) if n % 3 != 1]


def slot(n):
    _, g, col, r = PRODUCTS[n]
    return 16 * g + 4 * col + r


ATTN_SETUP = 11
DVE_SETUP = 25
PARITY = ("_even", "_odd")

NORM = {"var": 1, "rstd": 1, "xn_ready": TT}
SIGNALS = {
    "A": {
        **NORM, "x_loaded": 16, "vs_shifted": 64, "prod_dve": len(BY_DVE), "prod_pool": len(BY_POOL),
        "prod_used": 2 * J - len(LAST), "pa_ready": TT,
        "band_written_even": 16 * TT // 2, "band_written_odd": 16 * TT // 2,
        "band_read_even": 16 * TT // 2, "band_read_odd": 16 * TT // 2, "far_ready": TT, "oN_ready": TT,
        "dve_step": 22, "pool_step": 8,
    },
    "B": {
        **NORM, "hi_ready": 4, "r1_ready": 4, "mid_ready": 4, "lo_ready": 4,
        "split_written": 16 * 3, "stack_read": 16 * 13, "maxima_ready": 2,
        "maxima_written_even": 16, "maxima_written_odd": 16, "maxima_read_even": 16, "maxima_read_odd": 16,
        "pv_done": 12, "dve_step": 16,
    },
    "F": {
        **NORM, "var_2": 1, "rstd_2": 1, "lgd_ready": 1, "gexp_ready": 1, "gates_ready": 1, "dect_ready": TT,
        "moe_ready": 1, "cont_lo_ready": 1, "x_ready": 1, "dve_step": 21,
    },
}


def build(nc, x_dram, kept_dram, setup_dram, out_dram):
    fp32, bf16, fp32r = mybir.dt.float32, mybir.dt.bfloat16, mybir.dt.float32r
    ACT = mybir.ActivationFunctionType
    AX = mybir.AxisListType.X

    band_dram = nc.dram_tensor("band", (TT, P * (BW + 1) * H), fp32, kind="Internal").ap()
    maxima_dram = nc.dram_tensor("maxima", (2, 3, HPT, T), bf16, kind="Internal").ap()
    split_dram = nc.dram_tensor("splits", (3, 4 * P, T), bf16, kind="Internal").ap()

    ctx = ExitStack()
    with ctx:
        def sb(name, shape, dt=fp32):
            return ctx.enter_context(nc.sbuf_tensor(name, shape, dt))

        kept = sb("kept", [P, KEPT_W])
        x_in = sb("x_in", [P, TT, D])
        x_of = [sb("x_even", [P, TT, D]), sb("x_odd", [P, TT, D])]
        v_96 = sb("v_96", [P, TT, H, HS])
        kT = sb("kT", [P, KD, PAD + T])
        cont_hi = sb("cont_hi", [P, T], fp32r)[:]
        cont_lo = sb("cont_lo", [P, T], fp32r)[:]
        we1 = sb("we1", [P, E, EH], fp32r)
        rh = sb("rh", [P, T])
        gT = sb("gT", [P, T], bf16)
        V = sb("V", [P, TT, H, HS])
        slot_w = sb("slot_w", [P, J, HS])
        minus_half = sb("minus_half", [P, TT])
        ones = sb("ones", [P, P])
        half_c2s_b = sb("half_c2s_b", [P, KF])
        half_enc_b = sb("half_enc_b", [P, KF])
        q_bias = sb("q_bias", [P, KD])
        s2c_bias = sb("s2c_bias", [P, 1])
        causal = sb("causal_b", [P, P], bf16)
        causal_T = sb("causal_T", [P, P], bf16)
        ident_b = sb("ident_b", [P, P], bf16)
        pair_sel = sb("pair_sel", [P, E // 2, P], bf16)
        ones_b = sb("ones_b", [P, P], bf16)
        is_slot = sb("is_slot", [P, NG * P], bf16)
        ahead = sb("ahead", [P, T], bf16)
        oN = sb("oN", [P, 2, D])
        oNT = sb("oNT", [P, 2, KD, P])
        den = sb("den", [P, 2, H])

        ARENA = {"AB": 15300, "F": 8890}
        arena = {k: sb("arena_" + k, [P, n]) for k, n in ARENA.items()}
        taken = {}

        def part(n, of="AB", at=None):
            a = taken.get(of, 0) if at is None else at
            taken[of] = a + n
            assert taken[of] <= ARENA[of], taken[of]
            return arena[of][:, a:a + n]

        xn_ab = sb("xn", [P, TT, D])
        xnT_ab = sb("xnT", [P, KD, T])
        oTs = xn_ab[:].rearrange("p (r a) c -> p r (a c)", r=2)
        qT = part(KD * T).rearrange("p (m t) -> p m t", m=KD)
        RD, RP = 6, 3
        prod_d = part(RD * T).rearrange("p (r t) -> p r t", r=RD)
        prod_p = part(RP * T).rearrange("p (r t) -> p r t", r=RP)
        after_products = taken["AB"]
        band = part(2 * BW * H, at=0).rearrange("p (r s h) -> p r s h", r=2, s=BW)
        sT = part(2 * NG * T, at=after_products).rearrange("p (g t) -> p g t", g=2 * NG)
        p_nat = part(2 * J * H).rearrange("p (r j h) -> p r j h", r=2, j=J)
        ptA = part(H * P).rearrange("p (h t) -> p h t", h=H)
        ptB = part(H * (NEAR - 1)).rearrange("p (h t) -> p h t", h=H)
        v_near = part((TT - 1) * H * HS).rearrange("p (i h d) -> p i h d", i=TT - 1, h=H)
        far = part(2 * D).rearrange("p (r h d) -> p r h d", r=2, h=H)
        far_t = part(D).rearrange("p (h d) -> p h d", h=H)
        mx = part(TT * H).rearrange("p (i h) -> p i h", i=TT)
        far_den = part(2 * H).rearrange("p (r h) -> p r h", r=2)
        qk32 = part(4 * T, at=0).rearrange("p (m t) -> p m t", m=4)
        split = part(4 * 3 * T // 2).bitcast(bf16).rearrange("p (m s t) -> p m s t", m=4, s=3)
        RS = 2
        p_T = part(RS * 4 * T, at=0).rearrange("p (r c q) -> p r c q", r=RS, c=4)
        oT_all = part(QUADS * T).rearrange("p (g t) -> p g t", g=QUADS)
        q_st = part(H * T // 2).bitcast(bf16).rearrange("p (h t) -> p h t", h=H)
        k_st = part(H * T // 2).bitcast(bf16).rearrange("p (h t) -> p h t", h=H)
        neg_max = part(TT * H).rearrange("p (h i) -> p h i", h=H)
        max_parts = part(2 * TT * 3 * HPT // 2).bitcast(bf16).rearrange("p (f i s h) -> p f i s h", f=2, i=TT, s=3)
        max_rest = part(TT * H).rearrange("p (h i) -> p h i", h=H)
        max_T = part(T).bitcast(bf16).rearrange("p (f t) -> p f t", f=2)
        t_enc = part(KF * T, "F").rearrange("p (m t) -> p m t", m=KF)
        t_moe = t_enc
        RH = 8
        cont = part(T, "F", at=0)
        taken["F"] = KF * T
        hid_at = taken["F"]
        hid = part(RH * T, "F").rearrange("p (r t) -> p r t", r=RH)
        after_hid = taken["F"]
        xn_f = part(TT * D, "F", at=hid_at).rearrange("p (i c) -> p i c", i=TT)
        xnT_f = part(KD * T, "F").rearrange("p (k t) -> p k t", k=KD)
        dd = part(TT * D, "F", at=hid_at).rearrange("p (i c) -> p i c", i=TT)
        gb = part(2 * T, "F", at=after_hid).rearrange("p (r t) -> p r t", r=2)
        moe = part(T, "F")
        moe_t = part(T, "F")
        lg = part(TT * E, "F").rearrange("p (i e) -> p i e", i=TT)
        lgd = part(TT * E, "F").rearrange("p (i e) -> p i e", i=TT)
        above = part(TT * E * E, "F").rearrange("p (i e f) -> p i e f", i=TT, e=E)
        same = part(TT * E * E, "F").rearrange("p (i e f) -> p i e f", i=TT, e=E)
        rank = part(TT * E, "F").rearrange("p (i e) -> p i e", i=TT)
        gates = part(TT * E, "F").rearrange("p (i e) -> p i e", i=TT)
        gate_parts = part(TT * 3 * E // 2, "F").bitcast(bf16).rearrange("p (i s e) -> p i s e", i=TT, s=3)
        lmax = part(TT, "F")
        gsum = part(TT, "F")
        setup_only = arena["F"][:, 0:SETUP_W]

        Norm = namedtuple("Norm", "xn xnT stats mv var rstd scrap")
        norms = {s: Norm(xn, xnT, *(sb(f"{n}_{s}", [P, *w]) for n, w in
                                    (("stats", (TT, 6)), ("mv", (TT, 2)), ("var_eps", (TT,)), ("rstd", (TT,)),
                                     ("scrap", (16,)))))
                 for s, xn, xnT in (("AB", xn_ab, xnT_ab), ("F", xn_f, xnT_f))}

        def c(name, a=0, n=None):
            lo, hi = AT[name]
            return kept[:, lo + a:hi if n is None else lo + a + n]

        def c3(name, k):
            return c(name).rearrange("p (k n) -> p k n", k=k)

        def s_only(name):
            lo, hi = AT_S[name]
            return setup_only[:, lo:hi]

        ident = c("ident")
        w_qkv, w_out = c3("w_qkv", KD), c3("w_out_a", KD)
        wq, wk, wv, wo = (c3(n, KD) for n in ("wq", "wk", "wv", "wo"))
        enc_w, s2c_w, dec_w = c3("enc_w", KD), c3("s2c_w", KF), c3("dec_w", KF)
        we2 = c("we2").rearrange("p (e k m) -> p e k m", e=E, k=2)

        bank = [ctx.enter_context(nc.psum_tensor(f"bank{i}", [P, T], fp32)) for i in range(8)]
        full = [ctx.enter_context(nc.semaphore(f"bank{i}_full")) for i in range(8)]
        free = [ctx.enter_context(nc.semaphore(f"bank{i}_read")) for i in range(8)]
        sem = {s: {n: ctx.enter_context(nc.semaphore(f"{s}_{n}")) for n in names} for s, names in SIGNALS.items()}
        y_stored = [ctx.enter_context(nc.semaphore("y_stored" + x)) for x in PARITY]
        pack_a_loaded, pack_b_loaded, pack_s_loaded, setup_dve, setup_pool, setup_pe, setup_band = (
            ctx.enter_context(nc.semaphore(n)) for n in ("pack_a_loaded", "pack_b_loaded", "pack_s_loaded", "setup_dve",
                                                         "setup_pool", "setup_pe", "setup_band"))
        SETTLED = (pack_a_loaded, 16)

        def calls_before(u, s):
            return IN_PAIR[s], {"A": u.a, "B": u.b, "F": u.f}[s]

        def nth(u, name, k):
            per, (in_pair, ahead_) = SIGNALS[u.stage][name], calls_before(u, u.stage)
            return sem[u.stage][name], u.i * (in_pair * per) + (ahead_ * per + k)

        def fills_before(u, name):
            n, before = FILLS[u.stage][name]
            counts = [(calls_before(u, s), USES[s][n]) for s in SHARED[u.stage]]
            return n, sum(k * w for (k, _), w in counts), before + sum(a * w for (_, a), w in counts)

        def place(u, name, of=free):
            n, _ = FILLS[u.stage][name]
            return bank[n], of[n]

        def bank_full(u, name):
            n, per_pair, before = fills_before(u, name)
            return full[n], u.i * per_pair + (before + 1)

        def bank_read(u, name):
            n, per_pair, before = fills_before(u, name)
            return free[n], u.i * per_pair + (before + 2)

        def bank_free(u, name):
            n, per_pair, before = fills_before(u, name)
            return free[n], u.i * per_pair + (before + 1)

        def latest(u, names):
            fills = FILLS[u.stage]
            last = {fills[name][0]: name for name in sorted(names, key=lambda x: fills[x][1])}
            return list(last.values())

        def covered(u, name, others):
            return [x for x in latest(u, others) if FILLS[u.stage][x][0] != FILLS[u.stage][name][0]]

        def product_used(u, n):
            if n in LAST:
                return bank_full(u, ("sT", LAST.index(n)))
            return nth(u, "prod_used", sum(k not in LAST for k in range(n + 1)))

        def step_done(u, n):
            g, k = STEPS[n]
            return bank_full(u, ("oT", g)) if k == TT - 1 else nth(u, "pv_done", 3 * g + k + 1)

        def rows_of(dram, u):
            b = u.i * 2 + u.batch
            part_ = dram[b:b + 1] if isinstance(u.i, int) else dram[bass.ds(b, 1), :, :]
            return part_.rearrange("o (i p) n -> p (o i) n", p=P)

        PAIRS = NB // 2
        FIRST_A = Call("A", 0, 0, 0, 0, 0)

        def pair(i):
            return [(Call("A", i, 1, 0, 0, 1), Call("F", i, 0, 0, 0, 0)),
                    (Call("B", i, 2, 0, 0, 0), Call("F", i, 0, 0, 1, 1)),
                    (Call("B", i, 2, 1, 0, 1), Call("F", i, 0, 0, 2, 0)),
                    (Call("A", i, 2, 2, 0, 2), Call("F", i, 0, 0, 3, 1))]

        def rounds(engine, local, causal_, experts):
            def one(attn, moe_call):
                if attn.stage == "A":
                    together(A=local(attn), F=experts(moe_call))
                else:
                    together(B=causal_(attn), F=experts(moe_call))

            if PAIRS > 1:
                with engine.Fori(0, PAIRS - 1) as i:
                    for attn, moe_call in pair(i):
                        one(attn, moe_call)
            end = pair(PAIRS - 1)
            for attn, moe_call in end[0:3]:
                one(attn, moe_call)
            for _ in experts(end[3][1]):
                pass

        block = ctx.enter_context(nc.Block())

        @block.sync
        def _(sp):
            def load_x(u, batch):
                sp.dma_start(x_in[:], rows_of(x_dram, u._replace(batch=batch))).then_inc(sem["A"]["x_loaded"], 16)

            sp.dma_start(kept[:, 0:A_W], kept_dram[:, 0:A_W]).then_inc(pack_a_loaded, 16)
            load_x(FIRST_A, 0)
            sp.dma_start(setup_only[:, 0:S_W], setup_dram[:, 0:S_W]).then_inc(pack_s_loaded, 16)
            sp.dma_start(setup_only[:, S_W:SETUP_W], setup_dram[:, S_W:SETUP_W]).then_inc(pack_b_loaded, 16)
            sp.dma_start(kept[:, A_W:KEPT_W], kept_dram[:, A_W:KEPT_W]).then_inc(pack_b_loaded, 16)
            sp.wait_ge(setup_pool, 1)
            w = (BW + 1) * H // 8
            for i in range(TT):
                sp.dma_start(band_dram[i, :].rearrange("(t r w) -> t r w", t=P, r=8),
                             kT[:, 0:1, 0:w].broadcast_to([P, 8, w])).then_inc(setup_band, 16)
            sp.wait_ge(pack_a_loaded, 16)

            def local_attention(u):
                sp.wait_ge(*SETTLED)
                sp.wait_ge(*bank_read(u, ("v", 1)))
                vs_shifted = sem["A"]["vs_shifted"]
                sp.dma_start(v_96[0:96, 1:TT], V[32:P, 0:TT - 1]).then_inc(vs_shifted, 16)
                sp.dma_start(v_96[96:P, :], V[0:32, :]).then_inc(vs_shifted, 16)
                sp.dma_start(v_near[0:NEAR - 1, 0:2], V[P - NEAR + 1:P, 0:2]).then_inc(vs_shifted, 16)
                sp.dma_start(v_near[0:NEAR - 1, 2:3], V[P - NEAR + 1:P, 2:3]).then_inc(vs_shifted, 16)
                sp.wait_ge(setup_band, TT * 16)
                for k, written in ((0, True), (1, True), (0, False), (1, False), (2, True), (2, False), (3, True),
                                   (3, False)):
                    sp.wait_ge(*SETTLED)
                    if written:
                        sp.wait_ge(*nth(u, "pa_ready", k + 1))
                        dst = band_dram[k, :].rearrange("(t r) -> t r", t=P)[:, 0:NEAR * H]
                        sp.dma_start(dst, p_nat[:, k % 2, 0:NEAR, :].rearrange("p j h -> p (j h)")
                                     ).then_inc(sem["A"]["band_written" + PARITY[k % 2]], 16)
                    else:
                        sp.wait_ge(*nth(u, "band_written" + PARITY[k % 2], 16 * (k // 2 + 1)))
                        src = band_dram[k, 0:P * BW * H].rearrange("(t r) -> t r", t=P)
                        sp.dma_start(band[:, k % 2, :, :].rearrange("p s h -> p (s h)"), src
                                     ).then_inc(sem["A"]["band_read" + PARITY[k % 2]], 16)
                if not (isinstance(u.i, int) and 2 * u.i + u.batch == NB - 1):
                    sp.wait_ge(*SETTLED)
                    sp.wait_ge(*bank_read(u, ("pr", TT - 1)))
                    load_x(u, u.batch + 1)

            def causal_attention(u):
                for s in range(3):
                    sp.wait_ge(*SETTLED)
                    sp.wait_ge(*nth(u, ("hi_ready", "mid_ready", "lo_ready")[s], 4))
                    sp.dma_start(split_dram[s].rearrange("(m p) t -> p m t", p=P), split[:, :, s, :]
                                 ).then_inc(sem["B"]["split_written"], 16)
                sp.wait_ge(*SETTLED)
                sp.wait_ge(*nth(u, "split_written", 16 * 3))
                for slot_, parts in enumerate([(0, 0), (0, 1), (1, 0), (1, 1), (0, 2), (2, 0)]):
                    for half, st in enumerate([q_st, k_st]):
                        src = split_dram[parts[half], half * KD * P:(half + 1) * KD * P]
                        sp.dma_start(st[slot_ * HD:(slot_ + 1) * HD, :, :], src.rearrange("(h d) t -> d h t", d=HD)
                                     ).then_inc(sem["B"]["stack_read"], 16)
                sp.dma_start(k_st[6 * HD:6 * HD + 3, :, :].rearrange("p h (n t) -> p (h n) t", t=P),
                             ones_b[0:3, :].unsqueeze(1).broadcast_to([3, H * TT, P])
                             ).then_inc(sem["B"]["stack_read"], 16)
                for hf in range(2):
                    sp.wait_ge(*SETTLED)
                    sp.wait_ge(*bank_read(u, ("mT", hf)))
                    sp.dma_start(maxima_dram[hf].rearrange("s h t -> (s h) t"), max_T[0:3 * HPT, hf, :]
                                 ).then_inc(sem["B"]["maxima_written" + PARITY[hf]], 16)
                    sp.wait_ge(*SETTLED)
                    sp.wait_ge(*nth(u, "maxima_written" + PARITY[hf], 16))
                    sp.dma_start(q_st[6 * HD:6 * HD + 3, hf * HPT:(hf + 1) * HPT, :], maxima_dram[hf]
                                 ).then_inc(sem["B"]["maxima_read" + PARITY[hf]], 16)

            def store_y(u):
                sp.wait_ge(*SETTLED)
                sp.wait_ge(*nth(u, "x_ready", 1))
                sp.dma_start(rows_of(out_dram, u), x_of[u.batch][:]).then_inc(y_stored[u.batch], 16)

            def one(attn, moe_call):
                (local_attention if attn.stage == "A" else causal_attention)(attn)
                if moe_call.f >= 2:
                    store_y(moe_call)

            local_attention(FIRST_A)
            if PAIRS > 1:
                with sp.Fori(0, PAIRS - 1) as i:
                    for attn, moe_call in pair(i):
                        one(attn, moe_call)
            end = pair(PAIRS - 1)
            for attn, moe_call in end[0:3]:
                one(attn, moe_call)
            store_y(end[3][1])
            for s in y_stored:
                sp.wait_ge(s, 16 * PAIRS + 16)

        @block.gpsimd
        def _(pool):
            nc.gpsimd.memset(kT[:, :, 0:PAD], 0.0).then_inc(setup_pool, 1)
            nc.gpsimd.memset(V[:], 0.0).then_inc(setup_pool, 1)
            nc.gpsimd.memset(v_96[:, 0], 0.0).then_inc(setup_pool, 1)
            nc.gpsimd.memset(minus_half[:], -0.5).then_inc(setup_pool, 1)
            pool.wait_ge(setup_pool, 4)
            nc.gpsimd.memset(V[:, :, :, HD:HD + 1], 1.0).then_inc(setup_pool, 1)
            pool.wait_ge(setup_pool, 5)

            def power(u, norm, which=""):
                pool.wait_ge(*nth(u, "var" + which, 1))
                nc.gpsimd.tensor_tensor(norm.rstd[:], norm.var[:], minus_half[:], ALU.pow
                                        ).then_inc(sem[u.stage]["rstd" + which], 1)

            def local_attention(u):
                step = [0]

                def link(ins):
                    step[0] += 1
                    ins.then_inc(sem["A"]["pool_step"], 1)
                    pool.wait_ge(*nth(u, "pool_step", step[0]))

                yield "pow"
                power(u, norms["AB"])
                for k, n in enumerate(BY_POOL):
                    if k == 0 or n // 8 > BY_POOL[k - 1] // 8:
                        yield ("prod", n // 8)
                    if k == 0:
                        for x in latest(u, [("qk", m) for m in range(4)]):
                            pool.wait_ge(*bank_read(u, x))
                    hf, at = PRODUCTS[n][0], PAD - SLOTS[slot(n)]
                    if k >= RP:
                        pool.wait_ge(*product_used(u, BY_POOL[k - RP]))
                    nc.gpsimd.tensor_tensor(prod_p[:, k % RP, :], qT[:, hf, :], kT[:, hf, at:at + T],
                                            ALU.mult).then_inc(sem["A"]["prod_pool"], 1)
                for i in range(TT):
                    yield ("keys", i)
                    if i == 0:
                        pool.wait_ge(*nth(u, "vs_shifted", 64))
                    pool.wait_ge(*nth(u, "pa_ready", i + 1))
                    if i >= 2:
                        pool.wait_ge(*nth(u, "oN_ready", i - 1))
                    out = far[:, i % 2]

                    def p_of(s):
                        return p_nat[:, i % 2, s, :].unsqueeze(2).broadcast_to([P, H, HD])

                    terms = [(NEAR, v_96[:, i, :, 0:HD])]
                    if i >= 1:
                        terms.append((NEAR + 1, V[:, i - 1, :, 0:HD]))
                    if i >= 3:
                        terms.append((NEAR + 2, V[:, i - 3, :, 0:HD]))
                    for n, (s, v) in enumerate(terms):
                        last = nc.gpsimd.tensor_tensor(out if n == 0 else far_t, v, p_of(s), ALU.mult)
                        if n:
                            link(last)
                            last = nc.gpsimd.tensor_tensor(out, out, far_t, ALU.add)
                        if n < len(terms) - 1:
                            link(last)
                    last.then_inc(sem["A"]["far_ready"], 1)
                assert step[0] == SIGNALS["A"]["pool_step"], step[0]

            def causal_attention(u):
                yield "pow"
                power(u, norms["AB"])

            def experts(u):
                yield "pow"
                power(u, norms["F"])
                yield "pow_2"
                power(u, norms["F"], "_2")

            for _ in local_attention(FIRST_A):
                pass
            rounds(pool, local_attention, causal_attention, experts)

        @block.scalar
        def _(act):
            act.wait_ge(setup_dve, ATTN_SETUP)

            def read_xnT(u, norm):
                for k in range(KD):
                    act.wait_ge(*bank_full(u, ("xnT", k)))
                    ps, read = place(u, ("xnT", k))
                    nc.scalar.copy(norm.xnT[:, k, :], ps[:]).then_inc(read, 1)

            def read_oNT(u, i):
                act.wait_ge(*bank_full(u, ("oNT", i)))
                ps, read = place(u, ("oNT", i))
                nc.scalar.copy(oNT[:, i % 2, :, :], ps[:, 0:KD * P].rearrange("p (k t) -> p k t", k=KD)
                               ).then_inc(read, 1)

            def local_attention(u):
                yield "turn"
                read_xnT(u, norms["AB"])
                yield "qkv"
                for m in range(4):
                    act.wait_ge(*bank_full(u, ("qk", m)))
                    ps, read = place(u, ("qk", m))
                    dst = qT[:, m, :] if m < KD else kT[:, m - KD, PAD:PAD + T]
                    nc.scalar.copy(dst, ps[:]).then_inc(read, 1)
                for n in range(2):
                    act.wait_ge(*bank_full(u, ("v", n)))
                    ps, read = place(u, ("v", n))
                    nc.scalar.copy(V[:, 2 * n:2 * n + 2, :, 0:HD],
                                   ps[:].rearrange("p (i h d) -> p i h d", i=2, h=H)).then_inc(read, 1)
                for g in range(2 * NG):
                    yield ("prod", LAST[g] // 8)
                    rows = GROUP_J[g % NG] * HPT
                    act.wait_ge(*bank_full(u, ("sT", g)))
                    ps, read = place(u, ("sT", g))
                    nc.scalar.activation(sT[0:rows, g, :], ps[0:rows, :], ACT.Identity,
                                         bias=c("pos_bias", g, 1)[0:rows, :]).then_inc(read, 1)
                for kind, i in TILES:
                    if kind not in ("p", "keys", "oT", "oNT"):
                        continue
                    yield (kind, i)
                    if kind == "p":
                        act.wait_ge(*bank_read(u, ("tS", i, 0)))
                        act.wait_ge(*bank_read(u, ("tS", i, 1)))
                        nc.scalar.activation(p_nat[:, i % 2], p_nat[:, i % 2], ACT.Exp
                                             ).then_inc(sem["A"]["pa_ready"], 1)
                    elif kind == "keys":
                        for q in range(4):
                            act.wait_ge(*bank_full(u, ("pA", i, q)))
                            ps, read = place(u, ("pA", i, q))
                            nc.scalar.copy(ptA[:, 4 * q:4 * q + 4, :], ps[:].rearrange("p (h t) -> p h t", h=4)
                                           ).then_inc(read, 1)
                    elif kind == "oT":
                        act.wait_ge(*bank_full(u, ("oT", i)))
                        ps, read = place(u, ("oT", i))
                        nc.scalar.copy(oTs[:, i % 2, :], ps[:]).then_inc(read, 1)
                    else:
                        read_oNT(u, i)

            def causal_attention(u):
                yield "turn"
                read_xnT(u, norms["AB"])
                yield "qkv"
                for m in range(4):
                    act.wait_ge(*bank_full(u, ("qk", m)))
                    ps, read = place(u, ("qk", m))
                    if m < KD:
                        nc.scalar.activation(qk32[:, m, :], ps[:], ACT.Identity, bias=q_bias[:, m:m + 1],
                                             scale=HD ** -0.5).then_inc(read, 1)
                    else:
                        nc.scalar.activation(qk32[:, m, :], ps[:], ACT.Identity, bias=c("bk", m - KD, 1)
                                             ).then_inc(read, 1)
                    act.wait_ge(*bank_read(u, ("qk", m)))
                    nc.scalar.copy(split[:, m, 0, :], qk32[:, m, :]).then_inc(sem["B"]["hi_ready"], 1)
                yield "split"
                for m in range(4):
                    act.wait_ge(*nth(u, "r1_ready", m + 1))
                    nc.scalar.copy(split[:, m, 1, :], qk32[:, m, :]).then_inc(sem["B"]["mid_ready"], 1)
                for hf in range(2):
                    yield ("max", HPT // 2) if hf == 0 else "maxT"
                    act.wait_ge(*bank_full(u, ("mT", hf)))
                    ps, read = place(u, ("mT", hf))
                    nc.scalar.copy(max_T[0:3 * HPT, hf, :], ps[0:3 * HPT, 0:T // 2].bitcast(bf16)).then_inc(read, 1)
                for n in range(len(STEPS) + 1):
                    yield ("step", n)
                    if n < len(STEPS):
                        g, k = STEPS[n]
                        w = T - k * P
                        if n >= RS:
                            act.wait_ge(*step_done(u, n - RS))
                        for m, cols in enumerate(SHARE[k]):
                            act.wait_ge(*bank_full(u, ("ST", g, k, m)))
                            ps, read = place(u, ("ST", g, k, m))
                            nc.scalar.activation(p_T[:, n % RS, cols[0]:cols[-1] + 1, 0:w],
                                                 ps[:, 0:len(cols) * w].rearrange("p (c q) -> p c q", c=len(cols)),
                                                 ACT.Exp).then_inc(read, 1)
                    if n > 0 and STEPS[n - 1][1] == TT - 1:
                        g = STEPS[n - 1][0]
                        act.wait_ge(*bank_full(u, ("oT", g)))
                        ps, read = place(u, ("oT", g))
                        nc.scalar.copy(oT_all[:, g, :], ps[:]).then_inc(read, 1)
                for i in range(TT):
                    yield ("oNT", i)
                    read_oNT(u, i)

            def experts(u):
                yield "turn"
                read_xnT(u, norms["F"])
                for m in range(KF):
                    yield ("enc", m)
                    act.wait_ge(*bank_full(u, ("enc", m)))
                    ps, read = place(u, ("enc", m))
                    nc.scalar.activation(t_enc[:, m, :], ps[:], ACT.Tanh, bias=half_enc_b[:, m:m + 1], scale=0.5
                                         ).then_inc(read, 1)
                yield "cont"
                act.wait_ge(*bank_full(u, "cont"))
                ps, read = place(u, "cont")
                nc.scalar.activation(cont, ps[:], ACT.Identity, bias=s2c_bias[:])
                nc.scalar.activation(cont_hi, ps[:], ACT.Identity, bias=s2c_bias[:]).then_inc(read, 1)
                yield "rh"
                act.wait_ge(*bank_full(u, "rh"))
                ps, read = place(u, "rh")
                nc.scalar.activation(rh[0:M, :], ps[0:M, :], ACT.Tanh, bias=c("rb1")[0:M, :]).then_inc(read, 1)
                for kind, n in EXPERTS:
                    if kind == "eo":
                        continue
                    yield (kind, n)
                    if kind == "hid":
                        for x in covered(u, ("hid", n), [("eo", (n - RH) // 4)]) if n >= RH else ():
                            act.wait_ge(*bank_full(u, x))
                        act.wait_ge(*bank_full(u, ("hid", n)))
                        ps, read = place(u, ("hid", n))
                        nc.scalar.activation(hid[:, n % RH, :], ps[:], ACT.Relu, bias=c("be1", n, 1)).then_inc(read, 1)
                        if n == 3:
                            act.wait_ge(*nth(u, "lgd_ready", 1))
                            nc.scalar.activation(lgd, lgd, ACT.Exp).then_inc(sem["F"]["gexp_ready"], 1)
                    elif kind == "gT":
                        act.wait_ge(*bank_full(u, ("gT", 0)))
                        ps, read = place(u, ("gT", 0))
                        nc.scalar.copy(gT[0:3 * E, :], ps[0:3 * E, 0:T // 2].bitcast(bf16)).then_inc(read, 1)
                    else:
                        act.wait_ge(*bank_full(u, ("gb", n)))
                        ps, read = place(u, ("gb", n))
                        if n >= 2:
                            act.wait_ge(*bank_read(u, ("eo", n - 2)))
                        nc.scalar.copy(gb[:, n % 2, :], ps[:]).then_inc(read, 1)
                for m in range(KF):
                    yield ("c2s", m)
                    act.wait_ge(*bank_full(u, ("c2s", m)))
                    ps, read = place(u, ("c2s", m))
                    nc.scalar.activation(t_moe[:, m, :], ps[:], ACT.Tanh, bias=half_c2s_b[:, m:m + 1], scale=0.5
                                         ).then_inc(read, 1)
                for n in range(TT // 2):
                    yield ("dec", n)
                    act.wait_ge(*bank_read(u, ("dec", n)))
                    for i in (2 * n, 2 * n + 1):
                        nc.scalar.activation(dd[:, i, :], dd[:, i, :], ACT.Tanh, scale=0.5
                                             ).then_inc(sem["F"]["dect_ready"], 1)

            for _ in local_attention(FIRST_A):
                pass
            act.wait_ge(setup_dve, DVE_SETUP)
            rounds(act, local_attention, causal_attention, experts)

        @block.vector
        def _(dve):
            setup = [0]

            def once(ins):
                setup[0] += 1
                ins.then_inc(setup_dve, 1)
                dve.wait_ge(setup_dve, setup[0])

            scrap = norms["AB"].scrap
            for n, s in enumerate(free):
                nc.vector.memset(scrap[:, n:n + 1], 0.0).then_inc(s, 1)
            for n, s in enumerate(y_stored):
                nc.vector.memset(scrap[:, 8 + n:9 + n], 0.0).then_inc(s, 16)
            once(nc.vector.memset(ones_b[:], 1.0))
            dve.wait_ge(pack_a_loaded, 16)
            for k in range(KD):
                once(nc.vector.tensor_scalar(w_out[:, k, :], w_out[:, k, :], c("gain", k, 1), None, ALU.mult))
            once(nc.vector.tensor_copy(ident_b[:], ident))
            dve.wait_ge(pack_s_loaded, 16)
            once(nc.vector.tensor_scalar(s_only("se"), s_only("se"), 1.0, HD ** -0.5, ALU.add, ALU.mult))
            once(nc.vector.tensor_tensor(
                slot_w[:].rearrange("p (a r) d -> p a r d", r=4),
                s_only("slot_mask").rearrange("p (r d) -> p r d", r=4).unsqueeze(1).broadcast_to([P, J // 4, 4, HS]),
                s_only("se").rearrange("p (a r) -> p a r", r=4).unsqueeze(3).broadcast_to([P, J // 4, 4, HS]),
                ALU.mult))
            once(nc.vector.tensor_copy(is_slot[:], s_only("is_slot")))
            once(nc.vector.tensor_copy(pair_sel[:].rearrange("p n m -> p (n m)"), s_only("pair_sel")))
            once(nc.vector.tensor_copy(ahead[:], s_only("ahead")))
            once(nc.vector.tensor_copy(causal[:], s_only("causal")))
            once(nc.vector.tensor_copy(causal_T[:], s_only("causal_T")))
            assert setup[0] == ATTN_SETUP, setup[0]

            step = {}

            def link(u, ins):
                step[u.stage] += 1
                ins.then_inc(sem[u.stage]["dve_step"], 1)
                dve.wait_ge(*nth(u, "dve_step", step[u.stage]))

            def counted(u):
                assert step[u.stage] == SIGNALS[u.stage]["dve_step"], (u.stage, step)

            def moments(u, src, norm, eps, which=""):
                yield "stats" + which
                if u.stage == "A":
                    dve.wait_ge(*nth(u, "x_loaded", 16))
                if which:
                    dve.wait_ge(*nth(u, "dect_ready", TT))
                for i in range(TT):
                    ins = nc.vector.bn_stats(norm.stats[:, i, :], src[:, i, :])
                link(u, ins)
                nc.vector.memset(norm.scrap[:, 15:16], 0.0)
                for i in range(TT):
                    ins = nc.vector.bn_aggr(norm.mv[:, i, :], norm.stats[:, i, :])
                link(u, ins)
                nc.vector.tensor_scalar(norm.var[:], norm.mv[:, :, 1], eps, None, ALU.add
                                        ).then_inc(sem[u.stage]["var" + which], 1)
                yield "close" if which else "xn"
                dve.wait_ge(*nth(u, "rstd" + which, 1))

            def layer_norm(u, src, norm):
                yield from moments(u, src, norm, EPS)
                for i in range(TT):
                    nc.vector.tensor_scalar(norm.xn[:, i, :], src[:, i, :], norm.mv[:, i, 0:1], norm.rstd[:, i:i + 1],
                                            ALU.subtract, ALU.mult).then_inc(sem[u.stage]["xn_ready"], 1)

            def softmax_local(u, i):
                if i >= 2:
                    dve.wait_ge(*nth(u, "band_written" + PARITY[i % 2], 16 * (i // 2)))
                    dve.wait_ge(*nth(u, "far_ready", i - 1))
                halves = []
                for hf in range(2):
                    dve.wait_ge(*bank_full(u, ("tS", i, hf)))
                    ps, read = place(u, ("tS", i, hf))
                    s = ps[:, 0:J * HPT].rearrange("p (j h) -> p j h", j=J)
                    halves.append((s, read))
                    m = mx[:, i, hf * HPT:(hf + 1) * HPT]
                    link(u, nc.vector.tensor_reduce(m, s.rearrange("p j h -> p h j"), AX, ALU.max))
                for hf, (s, read) in enumerate(halves):
                    m = mx[:, i, hf * HPT:(hf + 1) * HPT]
                    nc.vector.tensor_tensor(p_nat[:, i % 2, :, hf * HPT:(hf + 1) * HPT], s,
                                            m.unsqueeze(1).broadcast_to([P, J, HPT]), ALU.subtract
                                            ).then_inc(read, 1)

            def normalise_local(u, i):
                dve.wait_ge(*bank_full(u, ("on", i)))
                ps, read = place(u, ("on", i))
                o = ps[:].rearrange("p (h d) -> p h d", h=H)
                link(u, nc.vector.tensor_tensor(den[:, i % 2, :], o[:, :, HD], far_den[:, i % 2], ALU.add))
                link(u, nc.vector.reciprocal(den[:, i % 2, :], den[:, i % 2, :]))
                dve.wait_ge(*nth(u, "far_ready", i + 1))
                on = oN[:, i % 2, :].rearrange("p (h d) -> p h d", h=H)
                nc.vector.tensor_tensor(on, o[:, :, 0:HD], far[:, i % 2], ALU.add).then_inc(read, 1)
                dve.wait_ge(*bank_read(u, ("on", i)))
                nc.vector.tensor_tensor(on, on, den[:, i % 2, :].unsqueeze(2).broadcast_to([P, H, HD]), ALU.mult
                                        ).then_inc(sem["A"]["oN_ready"], 1)

            def local_attention(u):
                step["A"] = 0
                yield from layer_norm(u, x_in, norms["AB"])
                for k, n in enumerate(BY_DVE):
                    if k == 0 or n // 8 > BY_DVE[k - 1] // 8:
                        yield ("prod", n // 8)
                    if k == 0:
                        for x in latest(u, [("qk", m) for m in range(4)]):
                            dve.wait_ge(*bank_read(u, x))
                    hf, at = PRODUCTS[n][0], PAD - SLOTS[slot(n)]
                    if k >= RD:
                        dve.wait_ge(*product_used(u, BY_DVE[k - RD]))
                    nc.vector.tensor_tensor(prod_d[:, k % RD, :], qT[:, hf, :], kT[:, hf, at:at + T],
                                            ALU.mult).then_inc(sem["A"]["prod_dve"], 1)
                for kind, i in TILES:
                    if kind not in ("tS", "keys", "on", "pr"):
                        continue
                    yield (kind, i)
                    if kind == "tS":
                        softmax_local(u, i)
                    elif kind == "keys":
                        dve.wait_ge(*nth(u, "pa_ready", i + 1))
                        link(u, nc.vector.tensor_reduce(
                            far_den[:, i % 2], p_nat[:, i % 2, NEAR:J, :].rearrange("p j h -> p h j"), AX, ALU.add))
                        for q in range(2 if i > 0 else 0):
                            dve.wait_ge(*bank_full(u, ("pB", i, q)))
                            ps, read = place(u, ("pB", i, q))
                            nc.vector.tensor_copy(ptB[0:NEAR - 1, 8 * q:8 * q + 8, :],
                                                  ps[0:NEAR - 1, 0:8 * (NEAR - 1)].rearrange(
                                                      "p (h t) -> p h t", h=8)).then_inc(read, 1)
                    elif kind == "on":
                        normalise_local(u, i)
                    else:
                        if i == 0:
                            dve.wait_ge(y_stored[u.batch % 2], u.i * 16 + (u.batch // 2 + 1) * 16)
                        dve.wait_ge(*bank_full(u, ("pr", i)))
                        ps, read = place(u, ("pr", i))
                        nc.vector.tensor_tensor(x_of[u.batch % 2][:, i, :], ps[:, 0:D], x_in[:, i, :], ALU.add
                                                ).then_inc(read, 1)
                dve.wait_ge(*bank_read(u, ("pr", TT - 1)))
                counted(u)

            def causal_attention(u):
                step["B"] = 0
                x_ = x_of[u.batch]
                yield from layer_norm(u, x_, norms["AB"])
                yield "qkv"
                for n in range(2):
                    dve.wait_ge(*bank_full(u, ("v", n)))
                    ps, read = place(u, ("v", n))
                    for i in range(2):
                        ins = nc.vector.tensor_tensor(
                            V[:, 2 * n + i, :, 0:HD], ps[:, i * D:(i + 1) * D].rearrange("p (h d) -> p h d", h=H),
                            c("bv").rearrange("p (h d) -> p h d", h=H), ALU.add)
                    ins.then_inc(read, 1)
                yield "split"
                for m in range(4):
                    dve.wait_ge(*nth(u, "hi_ready", m + 1))
                    nc.vector.tensor_tensor(qk32[:, m, :], qk32[:, m, :], split[:, m, 0, :], ALU.subtract
                                            ).then_inc(sem["B"]["r1_ready"], 1)
                for m in range(4):
                    dve.wait_ge(*nth(u, "mid_ready", m + 1))
                    nc.vector.tensor_tensor(split[:, m, 2, :], qk32[:, m, :], split[:, m, 1, :], ALU.subtract
                                            ).then_inc(sem["B"]["lo_ready"], 1)
                for h in range(H):
                    if h % 2 == 0:
                        yield ("max", h // 2)
                    for n, tiles in enumerate(MAX_FILLS):
                        dve.wait_ge(*bank_full(u, ("S", h, n)))
                        ps, read = place(u, ("S", h, n))
                        for i, at in tiles:
                            ins = nc.vector.tensor_reduce(neg_max[:, h, i:i + 1], ps[:, at:at + (i + 1) * P], AX,
                                                          ALU.max, negate=True)
                        ins.then_inc(read, 1)
                    if h % HPT == HPT - 1:
                        hf = h // HPT
                        nm = neg_max[:, hf * HPT:h + 1, :].rearrange("p h i -> p i h")
                        rest = max_rest[:, hf * HPT:h + 1, :].rearrange("p h i -> p i h")
                        for x in latest(u, [("S", h, n) for n in range(len(MAX_FILLS))]):
                            dve.wait_ge(*bank_read(u, x))
                        link(u, nc.vector.tensor_copy(max_parts[:, hf, :, 0, :], nm))
                        link(u, nc.vector.tensor_tensor(rest, nm, max_parts[:, hf, :, 0, :], ALU.subtract))
                        link(u, nc.vector.tensor_copy(max_parts[:, hf, :, 1, :], rest))
                        nc.vector.tensor_tensor(max_parts[:, hf, :, 2, :], rest, max_parts[:, hf, :, 1, :],
                                                ALU.subtract).then_inc(sem["B"]["maxima_ready"], 1)
                for kind, i in OUTPUTS:
                    if kind == "on":
                        yield (kind, i)
                        dve.wait_ge(*bank_full(u, ("on", i)))
                        ps, read = place(u, ("on", i))
                        o = ps[:].rearrange("p (h d) -> p h d", h=H)
                        link(u, nc.vector.reciprocal(den[:, i % 2, :], o[:, :, HD]))
                        on = oN[:, i % 2, :].rearrange("p (h d) -> p h d", h=H)
                        nc.vector.tensor_tensor(on, o[:, :, 0:HD], den[:, i % 2, :].unsqueeze(2).broadcast_to([P, H, HD]),
                                                ALU.mult).then_inc(read, 1)
                    elif kind == "pr":
                        yield (kind, i)
                        dve.wait_ge(*bank_full(u, ("pr", i)))
                        ps, read = place(u, ("pr", i))
                        nc.vector.tensor_tensor(x_[:, i, :], ps[:, 0:D], x_[:, i, :], ALU.add).then_inc(read, 1)
                        dve.wait_ge(*bank_read(u, ("pr", i)))
                        link(u, nc.vector.tensor_tensor(x_[:, i, :], x_[:, i, :], c("bo"), ALU.add))
                counted(u)

            def experts(u):
                step["F"] = 0
                x_ = x_of[u.batch]
                yield from layer_norm(u, x_, norms["F"])
                yield "rh"
                dve.wait_ge(*bank_read(u, "cont"))
                nc.vector.tensor_tensor(cont_lo, cont, cont_hi.bitcast(fp32), ALU.subtract
                                        ).then_inc(sem["F"]["cont_lo_ready"], 1)
                yield ("hid", 1)
                dve.wait_ge(*bank_full(u, "lg"))
                ps, read = place(u, "lg")
                nc.vector.tensor_copy(lg[:], ps[:, 0:TT * E].rearrange("p (i e) -> p i e", i=TT)
                                      ).then_inc(read, 1)
                dve.wait_ge(*bank_read(u, "lg"))
                link(u, nc.vector.tensor_reduce(lmax[:], lg[:], AX, ALU.max))
                nc.vector.tensor_tensor(lgd[:], lg[:], lmax[:].unsqueeze(2).broadcast_to([P, TT, E]),
                                        ALU.subtract).then_inc(sem["F"]["lgd_ready"], 1)
                other = lg[:].unsqueeze(2).broadcast_to([P, TT, E, E])
                own = lg[:].unsqueeze(3).broadcast_to([P, TT, E, E])
                before = c("before").rearrange("p (e f) -> p e f", e=E).unsqueeze(1).broadcast_to([P, TT, E, E])
                nc.vector.tensor_tensor(above[:], other, own, ALU.is_gt)
                link(u, nc.vector.tensor_tensor(same[:], other, own, ALU.is_equal))
                link(u, nc.vector.tensor_tensor(same[:], same[:], before, ALU.mult))
                link(u, nc.vector.tensor_tensor(above[:], above[:], same[:], ALU.add))
                link(u, nc.vector.tensor_reduce(rank[:], above[:], AX, ALU.add))
                link(u, nc.vector.tensor_scalar(rank[:], rank[:], 1.5, None, ALU.is_lt))
                yield ("hid", 4)
                dve.wait_ge(*nth(u, "gexp_ready", 1))
                link(u, nc.vector.tensor_tensor(gates[:], lgd[:], rank[:], ALU.mult))
                link(u, nc.vector.tensor_reduce(gsum[:], gates[:], AX, ALU.add))
                link(u, nc.vector.reciprocal(gsum[:], gsum[:]))
                link(u, nc.vector.tensor_tensor(gates[:], gates[:], gsum[:].unsqueeze(2).broadcast_to([P, TT, E]),
                                                ALU.mult))
                link(u, nc.vector.tensor_copy(gate_parts[:, :, 0, :], gates))
                link(u, nc.vector.tensor_tensor(gates, gates, gate_parts[:, :, 0, :], ALU.subtract))
                link(u, nc.vector.tensor_copy(gate_parts[:, :, 1, :], gates))
                nc.vector.tensor_tensor(gate_parts[:, :, 2, :], gates, gate_parts[:, :, 1, :], ALU.subtract
                                        ).then_inc(sem["F"]["gates_ready"], 1)
                link(u, nc.vector.tensor_tensor(x_[:], x_[:], c("ln_b").unsqueeze(1).broadcast_to([P, TT, D]),
                                                ALU.add))
                for p in range(E // 2):
                    yield ("eo", p)
                    dve.wait_ge(*bank_full(u, ("eo", p)))
                    ps, read = place(u, ("eo", p))
                    dve.wait_ge(*bank_read(u, ("gb", p)))
                    nc.vector.scalar_tensor_tensor(
                        out=moe[:] if p == 0 else moe_t[:], in0=ps[:], scalar=c("be2", p, 1),
                        in1=gb[:, p % 2, :], op0=ALU.add, op1=ALU.mult).then_inc(read, 1)
                    if p > 0:
                        dve.wait_ge(*bank_read(u, ("eo", p)))
                        ins = nc.vector.tensor_tensor(moe[:], moe[:], moe_t[:], ALU.add)
                        if p == E // 2 - 1:
                            ins.then_inc(sem["F"]["moe_ready"], 1)
                        else:
                            link(u, ins)
                for n in range(TT // 2):
                    yield ("dec", n)
                    dve.wait_ge(*bank_full(u, ("dec", n)))
                    ps, read = place(u, ("dec", n))
                    nc.vector.tensor_tensor(dd[:, 2 * n:2 * n + 2, :], ps[:].rearrange("p (i c) -> p i c", i=2),
                                            c("dec_b").unsqueeze(1).broadcast_to([P, 2, D]), ALU.add
                                            ).then_inc(read, 1)
                norm = norms["F"]
                yield from moments(u, dd, norm, 4 * EPS, "_2")
                for i in range(TT):
                    ins = nc.vector.scalar_tensor_tensor(out=dd[:, i, :], in0=dd[:, i, :], scalar=norm.mv[:, i, 0:1],
                                                         in1=c("ln_g"), op0=ALU.subtract, op1=ALU.mult)
                link(u, ins)
                for i in range(TT):
                    ins = nc.vector.scalar_tensor_tensor(out=x_[:, i, :], in0=dd[:, i, :],
                                                         scalar=norm.rstd[:, i:i + 1], in1=x_[:, i, :], op0=ALU.mult,
                                                         op1=ALU.add)
                ins.then_inc(sem["F"]["x_ready"], 1)
                dve.wait_ge(*nth(u, "x_ready", 1))
                counted(u)

            for _ in local_attention(FIRST_A):
                pass
            once(nc.vector.memset(ones[:], 1.0))
            for t in (rh, gT):
                once(nc.vector.memset(t[:], 0.0))
            once(nc.vector.memset(rh[M:M + 1, :], 1.0))
            dve.wait_ge(pack_b_loaded, 32)
            once(nc.vector.tensor_scalar(half_enc_b[:], c("enc_b"), 0.5, None, ALU.mult))
            once(nc.vector.tensor_scalar(half_c2s_b[:], c("c2s_b"), 0.5, None, ALU.mult))
            once(nc.vector.tensor_scalar(q_bias[:], c("bq"), HD ** -0.5, None, ALU.mult))
            once(nc.vector.tensor_scalar(c("s2c_w"), c("s2c_w"), 0.5, None, ALU.mult))
            once(nc.vector.tensor_scalar(c("dec_w"), c("dec_w"), 0.5, None, ALU.mult))
            we1_flat, rounded = we1[:].rearrange("p e n -> p (e n)"), arena["F"][:, SETUP_W:SETUP_W + E * EH]
            once(nc.vector.tensor_copy(rounded.bitcast(fp32r), s_only("we1")))
            once(nc.vector.tensor_copy(we1_flat[0:M, :], s_only("we1")[0:M, :]))
            once(nc.vector.tensor_tensor(we1_flat[M:P, :], s_only("we1")[M:P, :], rounded[M:P, :], ALU.subtract))
            dve.wait_ge(setup_pe, 2)
            once(nc.vector.tensor_tensor(c("dec_b"), bank[5][:, 0:D], c("dec_b"), ALU.add))
            once(nc.vector.tensor_tensor(s2c_bias[:], bank[6][:, 0:1], c("s2c_b"), ALU.add))
            assert setup[0] == DVE_SETUP, setup[0]
            rounds(dve, local_attention, causal_attention, experts)

        @block.tensor
        def _(pe):
            pe.wait_ge(setup_dve, ATTN_SETUP)
            pe.wait_ge(setup_pool, 5)

            def product(u, name, out, pairs, read=()):
                for x in covered(u, name, read):
                    pe.wait_ge(*bank_read(u, x))
                pe.wait_ge(*bank_free(u, name))
                ps, full_ = place(u, name, full)
                for n, (w, x) in enumerate(pairs):
                    ins = nc.tensor.matmul(out(ps), w, x, start=n == 0, stop=n == len(pairs) - 1)
                ins.then_inc(full_, 1)

            def turn_xn(u, norm):
                pe.wait_ge(*nth(u, "xn_ready", TT))
                for k in range(KD):
                    pe.wait_ge(*bank_free(u, ("xnT", k)))
                    ps, full_ = place(u, ("xnT", k), full)
                    for i in range(TT):
                        ins = nc.tensor.transpose(ps[:, i * P:(i + 1) * P], norm.xn[:, i, k * P:(k + 1) * P], ident)
                    ins.then_inc(full_, 1)

            def xnT_read(u):
                for x in latest(u, [("xnT", k) for k in range(KD)]):
                    pe.wait_ge(*bank_read(u, x))

            def queries_keys_values(u, w_of, v_of):
                xnT_read(u)
                for m in range(4):
                    product(u, ("qk", m), lambda ps: ps[:], [(w_of(m, k), xnT_ab[:, k, :]) for k in range(KD)])
                for n in range(2):
                    pe.wait_ge(*bank_free(u, ("v", n)))
                    ps, full_ = place(u, ("v", n), full)
                    for i in range(2):
                        at = (2 * n + i) * P
                        for k in range(KD):
                            ins = nc.tensor.matmul(ps[:, i * D:(i + 1) * D], xnT_ab[:, k, at:at + P], v_of(k),
                                                   start=k == 0, stop=k == KD - 1)
                    ins.then_inc(full_, 1)

            def output(u, kind, i, src, w):
                if kind == "on":
                    for x in covered(u, ("on", i), [("oT", i)] if u.stage == "A" else [("oT", g) for g in range(QUADS)]):
                        pe.wait_ge(*bank_read(u, x))
                    pe.wait_ge(*bank_free(u, ("on", i)))
                    ps, full_ = place(u, ("on", i), full)
                    for g in range(4):
                        ins = nc.tensor.transpose(ps[:, g * P:(g + 1) * P], src(g), ident)
                    ins.then_inc(full_, 1)
                elif kind == "oNT":
                    if u.stage == "A":
                        pe.wait_ge(*nth(u, "oN_ready", i + 1))
                    for x in covered(u, ("oNT", i), [("on", i)]):
                        pe.wait_ge(*bank_read(u, x))
                    pe.wait_ge(*bank_free(u, ("oNT", i)))
                    ps, full_ = place(u, ("oNT", i), full)
                    for k in range(KD):
                        ins = nc.tensor.transpose(ps[:, k * P:(k + 1) * P], oN[:, i % 2, k * P:(k + 1) * P], ident)
                    ins.then_inc(full_, 1)
                else:
                    product(u, ("pr", i), lambda ps: ps[:, 0:D],
                            [(oNT[:, i % 2, k, :], w[:, k, :]) for k in range(KD)], read=[("oNT", i)])

            def turn_scores(u, i):
                for hf in range(2):
                    for x in covered(u, ("tS", i, hf), [("sT", hf * NG + g) for g in range(NG)]):
                        pe.wait_ge(*bank_read(u, x))
                    pe.wait_ge(*bank_free(u, ("tS", i, hf)))
                    ps, full_ = place(u, ("tS", i, hf), full)
                    for g in range(NG):
                        rows = GROUP_J[g] * HPT
                        ins = nc.tensor.transpose(ps[:, g * P:g * P + rows], sT[0:rows, hf * NG + g, i * P:(i + 1) * P],
                                                  ident[0:rows, 0:rows])
                    ins.then_inc(full_, 1)

            def local_attention(u):
                yield "turn"
                turn_xn(u, norms["AB"])
                yield "qkv"
                queries_keys_values(u, lambda m, k: w_qkv[:, k, m * P:(m + 1) * P], lambda k: w_qkv[:, k, 2 * D:3 * D])
                kd, kp = 0, 0
                for n, (hf, g, col, r) in enumerate(PRODUCTS):
                    if n % 8 == 0:
                        yield ("prod", n // 8)
                    if n in FIRST:
                        pe.wait_ge(*bank_free(u, ("sT", hf * NG + g)))
                        ps, full_ = place(u, ("sT", hf * NG + g), full)
                        rows = GROUP_J[g] * HPT
                        nc.tensor.matmul(ps[0:rows, :], is_slot[:, g * P:g * P + rows], ahead[:], start=True,
                                         stop=False, skip_group_check=True)
                    if n in BY_POOL:
                        kp += 1
                        pe.wait_ge(*nth(u, "prod_pool", kp))
                        src = prod_p[:, (kp - 1) % RP, :]
                    else:
                        kd += 1
                        pe.wait_ge(*nth(u, "prod_dve", kd))
                        src = prod_d[:, (kd - 1) % RD, :]
                    ins = nc.tensor.matmul(ps[HS * col:HS * (col + 1), :], slot_w[:, slot(n), :], src,
                                           start=False, stop=r == 3, skip_group_check=True)
                    ins.then_inc(full_ if n in LAST else sem["A"]["prod_used"], 1)
                w = NEAR - 1
                for kind, i in TILES:
                    if kind == "p":
                        continue
                    yield (kind, i)
                    if kind == "tS":
                        turn_scores(u, i)
                    elif kind == "keys":
                        if i == 0:
                            pe.wait_ge(*nth(u, "vs_shifted", 64))
                        pe.wait_ge(*nth(u, "band_read" + PARITY[i % 2], 16 * (i // 2 + 1)))
                        for q in range(4):
                            pe.wait_ge(*bank_free(u, ("pA", i, q)))
                            ps, full_ = place(u, ("pA", i, q), full)
                            for h in range(4 * q, 4 * q + 4):
                                ins = nc.tensor.transpose(ps[:, (h % 4) * P:(h % 4 + 1) * P],
                                                          band[:, i % 2, NEAR - 1:BW, h], ident)
                            ins.then_inc(full_, 1)
                        for q in range(2 if i > 0 else 0):
                            pe.wait_ge(*bank_free(u, ("pB", i, q)))
                            ps, full_ = place(u, ("pB", i, q), full)
                            nc.tensor.matmul(ps[:, 0:P], ident_b[:], causal[:], start=True, stop=True)
                            for h in range(8 * q, 8 * q + 8):
                                ins = nc.tensor.transpose(ps[0:w, (h % 8) * w:(h % 8 + 1) * w],
                                                          band[0:w, i % 2, 0:w, h], ident[0:w, 0:w])
                            ins.then_inc(full_, 1)
                    elif kind == "oT":
                        for x in covered(u, ("oT", i), [("pA", i, q) for q in range(4)]
                                         + [("pB", i, q) for q in range(2 if i > 0 else 0)]):
                            pe.wait_ge(*bank_read(u, x))
                        pe.wait_ge(*bank_free(u, ("oT", i)))
                        ps, full_ = place(u, ("oT", i), full)
                        for g in range(4):
                            for col in range(4):
                                ins = nc.tensor.matmul(ps[HS * col:HS * (col + 1), g * P:(g + 1) * P],
                                                       V[:, i, 4 * g + col, :], ptA[:, 4 * g + col, :],
                                                       start=True, stop=True)
                            for col in range(4 if i > 0 else 0):
                                ins = nc.tensor.matmul(ps[HS * col:HS * (col + 1), g * P:g * P + w],
                                                       v_near[0:w, i - 1, 4 * g + col, :], ptB[0:w, 4 * g + col, :],
                                                       start=False, stop=True, skip_group_check=True)
                        ins.then_inc(full_, 1)
                    else:
                        output(u, kind, i, lambda g: oTs[:, i % 2, g * P:(g + 1) * P], w_out)

            def turn_maxima(u, hf):
                pe.wait_ge(*nth(u, "maxima_ready", hf + 1))
                pe.wait_ge(*bank_free(u, ("mT", hf)))
                ps, full_ = place(u, ("mT", hf), full)
                nc.tensor.matmul(ps[:, 0:P], ident_b[:], causal[:], start=True, stop=True)
                for i in range(TT):
                    ins = nc.tensor.transpose(ps[0:3 * HPT, i * P // 2:(i + 1) * P // 2].bitcast(bf16),
                                              max_parts[:, hf, i, :, :].rearrange("p s h -> p (s h)"), ident_b[:])
                ins.then_inc(full_, 1)

            def causal_attention(u):
                yield "turn"
                turn_xn(u, norms["AB"])
                yield "qkv"
                queries_keys_values(u, lambda m, k: (wq, wk)[m // KD][:, k, (m % KD) * P:(m % KD + 1) * P],
                                    lambda k: wv[:, k, :])
                K = 6 * HD
                for h in range(H):
                    if h % 2 == 0:
                        yield ("max", h // 2)
                    if h == 0:
                        pe.wait_ge(*nth(u, "stack_read", 16 * 13))
                    for n, tiles in enumerate(MAX_FILLS):
                        pe.wait_ge(*bank_free(u, ("S", h, n)))
                        ps, full_ = place(u, ("S", h, n), full)
                        for i, at in tiles:
                            nc.tensor.matmul(ps[:, at:at + (i + 1) * P], q_st[0:K, h, i * P:(i + 1) * P],
                                             k_st[0:K, h, 0:(i + 1) * P], start=True, stop=False,
                                             skip_group_check=True)
                            ins = nc.tensor.matmul(ps[:, at + i * P:at + (i + 1) * P], ident_b[:], causal[:],
                                                   start=False, stop=True, skip_group_check=True)
                        ins.then_inc(full_, 1)
                    if h == HPT + 1:
                        turn_maxima(u, 0)
                yield "maxT"
                turn_maxima(u, 1)
                for n in range(len(STEPS) + 1):
                    yield ("step", n)
                    if n == 0:
                        for x in latest(u, [("v", 0), ("v", 1)]):
                            pe.wait_ge(*bank_read(u, x))
                    if n < len(STEPS):
                        g, k = STEPS[n]
                        w = T - k * P
                        if k == 0 and g % 2 == 0:
                            pe.wait_ge(*nth(u, "maxima_read" + PARITY[g // 2], 16))
                        for m, cols in enumerate(SHARE[k]):
                            pe.wait_ge(*bank_free(u, ("ST", g, k, m)))
                            ps, full_ = place(u, ("ST", g, k, m), full)
                            for at, col in enumerate(cols):
                                h = 4 * g + col
                                nc.tensor.matmul(ps[:, at * w:(at + 1) * w], k_st[0:K + 3, h, k * P:(k + 1) * P],
                                                 q_st[0:K + 3, h, k * P:T], start=True, stop=False,
                                                 skip_group_check=True)
                                ins = nc.tensor.matmul(ps[:, at * w:at * w + P], ident_b[:], causal_T[:],
                                                       start=False, stop=True, skip_group_check=True)
                            ins.then_inc(full_, 1)
                    if n > 0:
                        g, k = STEPS[n - 1]
                        w = T - k * P
                        for x in latest(u, [("ST", g, k, m) for m in range(len(SHARE[k]))]):
                            pe.wait_ge(*bank_read(u, x))
                        if k == 0:
                            pe.wait_ge(*bank_free(u, ("oT", g)))
                            ps_o, full_o = place(u, ("oT", g), full)
                        for col in range(4):
                            ins = nc.tensor.matmul(ps_o[HS * col:HS * (col + 1), k * P:T], V[:, k, 4 * g + col, :],
                                                   p_T[:, (n - 1) % RS, col, 0:w], start=k == 0, stop=k == TT - 1,
                                                   skip_group_check=True)
                        ins.then_inc(full_o if k == TT - 1 else sem["B"]["pv_done"], 1)
                for kind, i in OUTPUTS:
                    yield (kind, i)
                    output(u, kind, i, lambda g: oT_all[:, g, i * P:(i + 1) * P], wo)

            def experts(u):
                yield "turn"
                turn_xn(u, norms["F"])
                for m in range(KF):
                    yield ("enc", m)
                    if m == 0:
                        xnT_read(u)
                    product(u, ("enc", m), lambda ps: ps[:],
                            [(enc_w[:, k, m * P:(m + 1) * P], xnT_f[:, k, :]) for k in range(KD)])
                yield "cont"
                product(u, "cont", lambda ps: ps[:], [(s2c_w[:, k, :], t_enc[:, k, :]) for k in range(KF)],
                        read=[("enc", m) for m in range(KF)])
                yield "rh"
                product(u, "rh", lambda ps: ps[0:M, :], [(c("rw1"), cont)], read=["cont"])
                yield "lg"
                for x in covered(u, "lg", ["rh"]):
                    pe.wait_ge(*bank_read(u, x))
                pe.wait_ge(*bank_free(u, "lg"))
                ps, full_ = place(u, "lg", full)
                for i in range(TT):
                    ins = nc.tensor.matmul(ps[:, i * E:(i + 1) * E], rh[:, i * P:(i + 1) * P], c("rw2"), start=True,
                                           stop=True)
                ins.then_inc(full_, 1)
                for kind, n in EXPERTS:
                    yield (kind, n)
                    if kind == "hid":
                        if n == 0:
                            pe.wait_ge(*nth(u, "cont_lo_ready", 1))
                        w = we1[:, n // 2, (n % 2) * P:(n % 2 + 1) * P]
                        product(u, ("hid", n), lambda ps: ps[:], [(w, cont_hi), (w, cont_lo)])
                    elif kind == "gT":
                        pe.wait_ge(*nth(u, "gates_ready", 1))
                        pe.wait_ge(*bank_free(u, ("gT", 0)))
                        ps, full_ = place(u, ("gT", 0), full)
                        nc.tensor.matmul(ps[:, 0:P], ident_b[:], causal[:], start=True, stop=True)
                        for i in range(TT):
                            ins = nc.tensor.transpose(ps[0:3 * E, i * P // 2:(i + 1) * P // 2].bitcast(bf16),
                                                      gate_parts[:, i, :, :].rearrange("p s e -> p (s e)"), ident_b[:])
                        ins.then_inc(full_, 1)
                    elif kind == "gb":
                        product(u, ("gb", n), lambda ps: ps[:], [(pair_sel[:, n, :], gT[:])], read=[("gT", 0)])
                    else:
                        for x in covered(u, ("eo", n), [("hid", m) for m in range(4 * n, 4 * n + 4)]):
                            pe.wait_ge(*bank_read(u, x))
                        pe.wait_ge(*bank_free(u, ("eo", n)))
                        ps, full_ = place(u, ("eo", n), full)
                        for k in range(2):
                            for e in range(2):
                                ins = nc.tensor.matmul(ps[M * e:M * (e + 1), :], we2[:, 2 * n + e, k, :],
                                                       hid[:, (4 * n + 2 * e + k) % RH, :], start=k == 0, stop=k == 1)
                        ins.then_inc(full_, 1)
                for m in range(KF):
                    yield ("c2s", m)
                    if m == 0:
                        pe.wait_ge(*nth(u, "moe_ready", 1))
                    product(u, ("c2s", m), lambda ps: ps[:], [(c("c2s_w", m * P, P), moe)])
                for n in range(TT // 2):
                    yield ("dec", n)
                    for x in covered(u, ("dec", n), [("c2s", m) for m in range(KF)]):
                        pe.wait_ge(*bank_read(u, x))
                    pe.wait_ge(*bank_free(u, ("dec", n)))
                    ps, full_ = place(u, ("dec", n), full)
                    for i in range(2):
                        at = (2 * n + i) * P
                        for k in range(KF):
                            ins = nc.tensor.matmul(ps[:, i * D:(i + 1) * D], t_moe[:, k, at:at + P], dec_w[:, k, :],
                                                   start=k == 0, stop=k == KF - 1)
                    ins.then_inc(full_, 1)

            for _ in local_attention(FIRST_A):
                pass
            pe.wait_ge(setup_dve, DVE_SETUP - 2)
            for k in range(KF):
                ins = nc.tensor.matmul(bank[5][:, 0:D], ones[:], dec_w[:, k, :], start=k == 0, stop=k == KF - 1)
            ins.then_inc(setup_pe, 1)
            for k in range(KF):
                ins = nc.tensor.matmul(bank[6][:, 0:1], s2c_w[:, k, :], ones[:, 0:1], start=k == 0,
                                       stop=k == KF - 1)
            ins.then_inc(setup_pe, 1)
            pe.wait_ge(setup_dve, DVE_SETUP)
            rounds(pe, local_attention, causal_attention, experts)


def lay_out(a):
    def rows(w, k):
        return w.reshape(k, P, -1).transpose(1, 0, 2).reshape(P, -1)

    def padded(w):
        out = np.zeros((P,) + w.shape[1:], np.float32)
        out[:w.shape[0]] = w
        return out.reshape(P, -1)

    def spread(v):
        return np.broadcast_to(v[None, :], (P, v.shape[0]))

    A, B, F = ({k[len(p):]: v for k, v in a.items() if k.startswith(p)} for p in ("L0_attn_a_", "L0_attn_b_", "L0_ffn_"))
    row = np.arange(P)
    slot_mask = np.zeros((P, 4, HS), np.float32)
    for r in range(4):
        slot_mask[row, r, HPT * r + row // HD] = 1.0
    is_slot = np.zeros((P, NG, P), np.float32)
    ahead = np.zeros((P, T), np.float32)
    bias = np.zeros((P, 2, NG), np.float32)
    for g, n in enumerate(GROUP_J):
        for j in range(n):
            at = slice(j * HPT, (j + 1) * HPT)
            is_slot[16 * g + j, g, at] = 1.0
            ahead[16 * g + j, :SLOTS[16 * g + j]] = NEG
            for hf in range(2):
                bias[at, hf, g] = A["pos_bias"][REF_OF[16 * g + j], hf * HPT:(hf + 1) * HPT]
    pair_ = np.zeros((P, E // 2, P), np.float32)
    for e in range(E):
        pair_[[e, E + e, 2 * E + e], e // 2, (e % 2) * M:(e % 2 + 1) * M] = 1.0
    parts = {
        "ident": np.eye(P, dtype=np.float32), "slot_mask": slot_mask, "is_slot": is_slot, "ahead": ahead,
        "pos_bias": bias,
        "se": np.tile(A["scale_embed"][REF_OF].T, (HPT, 1)), "w_qkv": rows(A["w_qkv"], KD),
        "w_out_a": rows(A["w_out"], KD), "gain": np.repeat(A["if_gain"], HD).reshape(KD, P).T,
        "wq": rows(B["Wq"], KD), "wk": rows(B["Wk"], KD), "wv": rows(B["Wv"], KD), "wo": rows(B["Wo"], KD),
        "bq": B["bq"].reshape(KD, P).T, "bk": B["bk"].reshape(KD, P).T, "bv": spread(B["bv"]), "bo": spread(B["bo"]),
        "enc_w": rows(F["enc_W"], KD), "enc_b": F["enc_b"].reshape(KF, P).T, "s2c_w": rows(np.concatenate([F["s2c_W"], F["s2c_W"]], axis=1), KF),
        "s2c_b": np.tile(F["s2c_b"], 2)[:, None], "rw1": padded(F["rW1"]), "rb1": padded(F["rb1"][:, None]),
        "rw2": padded(np.concatenate([F["rW2"], F["rb2"][None]])),
        "we1": np.tile(F["We1"].transpose(1, 0, 2), (2, 1, 1)), "be1": F["be1"].reshape(2 * E, P).T,
        "we2": F["We2"].reshape(E, 2, P, M).transpose(2, 0, 1, 3), "be2": F["be2"].reshape(E // 2, 2 * M).T,
        "c2s_w": np.concatenate([F["c2s_W"], F["c2s_W"]]), "c2s_b": F["c2s_b"].reshape(KF, P).T,
        "dec_w": rows(F["dec_W"], KF), "dec_b": spread(F["dec_b"]), "ln_g": spread(F["ln_g"]),
        "ln_b": spread(F["ln_b"]), "pair_sel": pair_,
        "before": np.broadcast_to(np.tril(np.ones((E, E), np.float32), -1).reshape(1, -1), (P, E * E)),
        "causal": np.triu(np.full((P, P), NEG, np.float32), 1),
        "causal_T": np.tril(np.full((P, P), NEG, np.float32), -1),
    }
    return tuple(np.concatenate([np.ascontiguousarray(parts[n]).reshape(P, w) for n, w in names], axis=1)
                 for names in (PACK_A + PACK_B, PACK_S))


def kernel(**inputs):
    import concourse.bacc as _bacc
    from concourse.bass_utils import run_bass_kernel_spmd as _run

    a = {k: np.asarray(v) for k, v in inputs.items()}
    kept, setup_ = lay_out(a)
    arrays = {"x": np.ascontiguousarray(a["L0_attn_a_x"]), "kept_pack": kept, "setup_pack": setup_}
    nc = _bacc.Bacc("TRN2", target_bir_lowering=False, num_devices=1)
    args = [nc.dram_tensor(n, v.shape, mybir.dt.float32, kind="ExternalInput").ap() for n, v in arrays.items()]
    args.append(nc.dram_tensor("out", (NB, T, D), mybir.dt.float32, kind="ExternalOutput").ap())
    build(nc, *args)
    r = _run(nc, [arrays], core_ids=[0])
    return r.results[0]["out"]
```
